# Optimizing a Trainium2 kernel written in Bass

```python
import numpy as np
import jax
import jax.numpy as jnp

def _softmax(x, axis=-1):
    return jax.nn.softmax(x, axis=axis)

def _gelu(x):
    return jax.nn.gelu(x, approximate=True)

def _silu(x):
    return jax.nn.silu(x)

def _sigmoid(x):
    return jax.nn.sigmoid(x)

def _layernorm(x, axis=-1, eps=1e-05):
    m = jnp.mean(x, axis=axis, keepdims=True)
    v = jnp.var(x, axis=axis, keepdims=True)
    return (x - m) / jnp.sqrt(v + eps)

def _scatter_add(tgt, idx, src, axis=0):
    return tgt.at[idx].add(src)

def _segment_sum(src, seg, n):
    return jax.ops.segment_sum(src, seg, n)
kernel_name = 'mk_seq_preln_d2_jaxref_r8_7814f9'

def setup_inputs(seed: int=0):
    np.random.seed(seed)
    _w = jnp.asarray

    def _L0_attn_setup():
        import jax, jax.numpy as jnp
        import numpy as np
        NUM_HEADS = 16
        key = jax.random.key(seed)
        k1, k2, k3 = jax.random.split(key, 3)
        B, T, D = (4, 256, 128)
        x = jax.random.normal(k1, (B, T, D), dtype=jnp.float32)
        w = jax.random.normal(k2, (3 * D, D), dtype=jnp.float32) * (1.0 / np.sqrt(D))
        w_out = jax.random.normal(k3, (D, D), dtype=jnp.float32) * (1.0 / np.sqrt(D))
        return {'x': x, 'w': w, 'w_out': w_out}
    _L0_attn_in = _L0_attn_setup()

    def _L0_ffn_setup():
        import jax, jax.numpy as jnp
        import numpy as np
        DIM = 128
        NUM_EXPERTS = 8
        HIDDEN = 512
        CAP_FACTOR = 2.0
        B, S = (4, 256)
        key = jax.random.key(seed)
        ks = jax.random.split(key, 6)
        scale_r = 1.0 / np.sqrt(DIM)
        scale_1 = 1.0 / np.sqrt(DIM)
        scale_2 = 1.0 / np.sqrt(HIDDEN)
        return {'x': jax.random.normal(ks[0], (B, S, DIM), dtype=jnp.float32), 'router_w': jax.random.uniform(ks[1], (NUM_EXPERTS, DIM), jnp.float32, -scale_r, scale_r), 'w1': jax.random.uniform(ks[2], (NUM_EXPERTS, DIM, HIDDEN), jnp.float32, -scale_1, scale_1), 'b1': jax.random.uniform(ks[3], (NUM_EXPERTS, HIDDEN), jnp.float32, -scale_1, scale_1), 'w2': jax.random.uniform(ks[4], (NUM_EXPERTS, HIDDEN, DIM), jnp.float32, -scale_2, scale_2), 'b2': jax.random.uniform(ks[5], (NUM_EXPERTS, DIM), jnp.float32, -scale_2, scale_2)}
    _L0_ffn_in = _L0_ffn_setup()

    def _L1_attn_setup():
        import jax, jax.numpy as jnp
        import numpy as np
        import math
        D = 128
        H = 16
        HEAD_D = D // H
        T = 256
        B = 4
        key = jax.random.key(seed)
        k1, k2, k3 = jax.random.split(key, 3)
        x = jax.random.normal(k1, (B, T, D), dtype=jnp.float32)
        w_attn = jax.random.normal(k2, (D, D + 2 * HEAD_D), dtype=jnp.float32) * (1.0 / math.sqrt(D))
        w_proj = jax.random.normal(k3, (D, D), dtype=jnp.float32) * (1.0 / math.sqrt(D))
        return {'x': x, 'w_attn': w_attn, 'w_proj': w_proj}
    _L1_attn_in = _L1_attn_setup()

    def _L1_ffn_setup():
        import jax, jax.numpy as jnp
        import numpy as np
        B, N, D = (4, 256, 128)
        SPARSITY = 0.01
        key = jax.random.key(seed)
        k1, k2, k3 = jax.random.split(key, 3)
        x = jax.random.normal(k1, (B, N, D), dtype=jnp.float32)
        spatial = jax.random.normal(k2, (D, D), dtype=jnp.float32) * 0.02
        freq = jnp.fft.fft(spatial, axis=-1)
        k = int(D * SPARSITY)
        mag = jnp.abs(freq)
        kth = jax.lax.top_k(mag, k)[0][:, -1:]
        w_sparse = jnp.where(mag >= kth, freq, 0.0 + 0j)
        bias = jax.random.normal(k3, (D,), dtype=jnp.float32) * 0.01
        return {'x': x, 'w_freq_real': jnp.real(w_sparse).astype(jnp.float32), 'w_freq_imag': jnp.imag(w_sparse).astype(jnp.float32), 'bias': bias}
    _L1_ffn_in = _L1_ffn_setup()
    _d = {'L0_attn_x': _L0_attn_in['x'], 'L0_attn_w': _L0_attn_in['w'], 'L0_attn_w_out': _L0_attn_in['w_out'], 'L0_ffn_router_w': _L0_ffn_in['router_w'], 'L0_ffn_w1': _L0_ffn_in['w1'], 'L0_ffn_b1': _L0_ffn_in['b1'], 'L0_ffn_w2': _L0_ffn_in['w2'], 'L0_ffn_b2': _L0_ffn_in['b2'], 'L1_attn_w_attn': _L1_attn_in['w_attn'], 'L1_attn_w_proj': _L1_attn_in['w_proj'], 'L1_ffn_w_freq_real': _L1_ffn_in['w_freq_real'], 'L1_ffn_w_freq_imag': _L1_ffn_in['w_freq_imag'], 'L1_ffn_bias': _L1_ffn_in['bias']}
    _x0 = _d['L0_attn_x']
    _d['L0_attn_x'] = jax.random.normal(jax.random.fold_in(jax.random.key(seed), 1), (8, 512, 128), dtype=_x0.dtype)
    del _x0
    return _d

def reference(L0_attn_x, L0_attn_w, L0_attn_w_out, L0_ffn_router_w, L0_ffn_w1, L0_ffn_b1, L0_ffn_w2, L0_ffn_b2, L1_attn_w_attn, L1_attn_w_proj, L1_ffn_w_freq_real, L1_ffn_w_freq_imag, L1_ffn_bias):

    def _L0_attn_ref(x, w, w_out):
        import jax, jax.numpy as jnp
        import numpy as np
        NUM_HEADS = 16
        B, T, D = x.shape
        H = NUM_HEADS
        L = D // H
        q, k, v = jnp.split(jnp.matmul(x, w.T), 3, axis=2)
        q = q.reshape(B, T, H, L).transpose(1, 0, 2, 3)
        k = k.reshape(B, T, H, L).transpose(1, 0, 2, 3)
        v = v.reshape(B, T, H, L).transpose(1, 0, 2, 3)
        scale = jax.lax.rsqrt(jnp.float32(L))
        k_exp = jnp.exp(k * scale) + 1e-06
        k_norm = jnp.cumsum(k_exp, axis=0)
        qs = jax.nn.softmax(q * scale, axis=-1) / k_norm

        def step(carry, args):
            qs_t, k_t, v_t = args
            carry = carry + k_t[..., :, None] * v_t[..., None, :]
            y_t = jnp.einsum('bhl,bhlm->bhm', qs_t, carry)
            return (carry, y_t)
        init = jnp.zeros((B, H, L, L), dtype=x.dtype)
        _, y = jax.lax.scan(step, init, (qs, k_exp, v))
        y = y.reshape(T, B, D).transpose(1, 0, 2)
        return jnp.matmul(y, w_out)

    def _L0_ffn_ref(x, router_w, w1, b1, w2, b2):
        import jax, jax.numpy as jnp
        import numpy as np
        DIM = 128
        NUM_EXPERTS = 8
        HIDDEN = 512
        CAP_FACTOR = 2.0
        B, S = (4, 256)
        Bz, Sz, Dz = x.shape
        E = router_w.shape[0]
        capacity = max(1, int(Sz * CAP_FACTOR / E) + 1)
        scores = jax.nn.softmax(jnp.einsum('bsd,ed->bse', x, router_w), axis=-1)
        scores_t = jnp.swapaxes(scores, 1, 2)
        gate_vals, sel_idx = jax.lax.top_k(scores_t, capacity)
        b_idx = jnp.arange(Bz)[:, None, None]
        tokens = x[b_idx, sel_idx]
        h = jnp.einsum('becd,edh->bech', tokens, w1) + b1[None, :, None, :]
        h = jax.nn.gelu(h, approximate=False)
        y = jnp.einsum('bech,ehd->becd', h, w2) + b2[None, :, None, :]
        gated = y * gate_vals[..., None]
        out = jnp.zeros_like(x).at[b_idx, sel_idx].add(gated)
        return out

    def _L1_attn_ref(x, w_attn, w_proj):
        import jax, jax.numpy as jnp
        import numpy as np
        import math
        D = 128
        H = 16
        HEAD_D = D // H
        T = 256
        B = 4
        Bv, Tv, _ = x.shape
        qkv = x @ w_attn
        q = qkv[..., :D].reshape(Bv, Tv, H, HEAD_D).transpose(0, 2, 1, 3)
        k = qkv[..., D:D + HEAD_D]
        v = qkv[..., D + HEAD_D:]
        scale = 1.0 / math.sqrt(HEAD_D)
        att = jnp.einsum('bhqd,bkd->bhqk', q, k) * scale
        causal = jnp.tril(jnp.ones((Tv, Tv), dtype=bool))
        att = jnp.where(causal[None, None, :, :], att, -jnp.inf)
        att = jax.nn.softmax(att, axis=-1)
        y = jnp.einsum('bhqk,bkd->bhqd', att, v)
        y = y.transpose(0, 2, 1, 3).reshape(Bv, Tv, D)
        return y @ w_proj

    def _L1_ffn_ref(x, w_freq_real, w_freq_imag, bias):
        import jax, jax.numpy as jnp
        import numpy as np
        B, N, D = (4, 256, 128)
        SPARSITY = 0.01
        w = jax.lax.complex(w_freq_real, w_freq_imag)
        x_freq = jnp.fft.fft(x, axis=-1)
        y_freq = jnp.einsum('bnd,do->bno', x_freq, w)
        y = jnp.real(jnp.fft.ifft(y_freq, axis=-1))
        return y + bias
    x = L0_attn_x
    x = x + _L0_attn_ref(_layernorm(x, axis=-1), L0_attn_w, L0_attn_w_out)
    x = x + _L0_ffn_ref(_layernorm(x, axis=-1), L0_ffn_router_w, L0_ffn_w1, L0_ffn_b1, L0_ffn_w2, L0_ffn_b2)
    x = x + _L1_attn_ref(_layernorm(x, axis=-1), L1_attn_w_attn, L1_attn_w_proj)
    x = x + _L1_ffn_ref(_layernorm(x, axis=-1), L1_ffn_w_freq_real, L1_ffn_w_freq_imag, L1_ffn_bias)
    return x

_drawn_inputs = setup_inputs


def setup_inputs(seed=0):
    import zlib

    import numpy as np

    out = dict(_drawn_inputs(seed))
    spreads = {}
    factors = {'L0_ffn_b1': 8.0, 'L0_ffn_b2': 6.228, 'L1_ffn_bias': 6.371}
    for name, (base, spread) in spreads.items():
        noise = np.random.default_rng([zlib.crc32(name.encode()), seed]).standard_normal(out[name].shape)
        drawn = base * np.exp(spread * noise) if base else spread * noise
        out[name] = jnp.asarray(drawn.astype(out[name].dtype))
    for name, factor in factors.items():
        out[name] = (out[name] * factor).astype(out[name].dtype)
    return out
```

```python
from contextlib import ExitStack

import concourse.bass as bass
from concourse import mybir

F32 = mybir.dt.float32
BF16 = mybir.dt.bfloat16
ALU = mybir.AluOpType
ACT = mybir.ActivationFunctionType
AX = mybir.AxisListType

P = 128
HEADS = 16
EPS = 1e-5
NEG = -1.0e30
PARTS = 3


class Signal:

    START = 1

    def __init__(self, sem, per, step=1):
        self.sem, self.per, self.step = sem, per, step

    def at(self, turn, nth):
        return turn * (self.per * self.step) + (nth * self.step + self.START)

    def total(self, raised):
        return raised + self.START


def build(nc, x_in, w_qkv, w_out, router_w, w1, b1, w2, b2, w_attn, w_proj, wf_re, wf_im, f_bias,
          consts, out, layout):
    B, T, D = x_in.shape
    E, _, H = w1.shape
    NT = T // P
    L = D // HEADS
    CAP = max(1, int(T * 2.0 / E) + 1)
    HC = H // P
    SCALE = float(L) ** -0.5
    BE = B * E
    GC = 344
    assert CAP == P + 1 and D == P and E * CAP == 3 * GC and BE == 64
    QR = PARTS * PARTS * L
    NQ = HEADS // 4

    with ExitStack() as ctx:
        def sb(name, shape, dt=F32):
            return ctx.enter_context(nc.sbuf_tensor(name, shape, dt))

        made = []

        def signal(name, per=1, step=1):
            made.append(Signal(ctx.enter_context(nc.semaphore(name)), per, step))
            return made[-1]

        def psum(name, banks):
            return ctx.enter_context(nc.psum_tensor(name, [P, 512 * banks], F32))

        bank = {i: psum(f"bank{i}", 1) for i in (0, 1, 2, 7)}
        wide, wide2 = psum("wide", 2), psum("wide2", 2)
        bank[5], bank[6] = wide2[:, 0:512], wide2[:, 512:1024]

        x_sb = sb("x_sb", [P, B, NT, D])
        cst = sb("cst", [P, layout["width"]])

        def const(name):
            a, n = layout[name]
            return cst[:, a:a + n]

        ident, tri, ones = const("ident"), const("tri"), const("ones")
        dft_c, dft_s, dft_ns = const("dft_c"), const("dft_s"), const("dft_ns")
        blockdiag, seqmask = const("blockdiag"), const("seqmask")
        wq_raw = sb("wq_raw", [P, 3, D])
        wqT = sb("wqT", [P, 3 * D])
        wo_sb = sb("wo_sb", [P, D])
        r_raw = sb("r_raw", [E, D])
        rT = sb("rT", [P, E])
        w1_sb = sb("w1_sb", [P, E, H])
        w2_sb = sb("w2_sb", [P, E, HC, D])
        b1_raw = sb("b1_raw", [E * HC, P])
        b1T = sb("b1T", [P, E * HC])
        b2rep = sb("b2rep", [P, D])
        wa_sb = sb("wa_sb", [P, D + 2 * L])
        wp_sb = sb("wp_sb", [P, D])
        wf_sb = sb("wf_sb", [P, 2, D])
        fb_sb = sb("fb_sb", [P, D])
        a12 = sb("a12", [P, 2, D])
        m_sb = sb("m_sb", [P, D])
        ident_bf = sb("ident_bf", [P, P], BF16)

        sc_part = sb("sc_part", [P, NT, B, E, PARTS], BF16)
        posT = sb("posT", [P, NT, B, E])
        rest_l = sb("rest_l", [P, T])

        st6 = sb("st6", [P, NT, 6])
        mvt = sb("mvt", [P, NT, 2])
        mv = sb("mv", [P, B, NT, 2])
        sd = sb("sd", [P, B, NT])
        rstd = sb("rstd", [P, B, NT])
        xln = sb("xln", [P, NT, D])
        xT = sb("xT", [P, T])

        passed = signal("waits_passed")

        def waits_end(engine):
            engine.sem_inc(passed.sem, 1)

        stage = [ExitStack()]

        def new_stage():
            stage[0].close()
            stage[0] = ctx.enter_context(ExitStack())

        def scratch(name, shape, dt=F32):
            return stage[0].enter_context(nc.sbuf_tensor(name, shape, dt))

        s_x = signal("x_loaded", 1, 16)
        s_w = signal("weights_loaded", 1, 16)
        s_c = signal("consts_loaded", 1, 16)

        NW = 11
        s_prep_t = signal("prep_transposed")
        s_prep_v = signal("prep_evacuated")
        s_idb = signal("ident_bf_ready")

        def start_signals(sp):
            for s in made:
                sp.sem_inc(s.sem, Signal.START)

        def prep_sync(sp):
            sp.dma_start(cst[:, :], consts).then_inc(s_c.sem, 16)
            for b in range(B):
                sp.dma_start(x_sb[:, b], x_in[b].rearrange("(k p) d -> p k d", p=P)).then_inc(s_x.sem, 16)

        def prep_act(q):
            for dst, src in (
                (wq_raw[:, :, :], w_qkv.rearrange("(g p) d -> p g d", p=P)),
                (wo_sb[:, :], w_out),
                (r_raw[:, :], router_w),
                (b1_raw[:, :], b1.rearrange("e (c p) -> (e c) p", p=P)),
                (wf_sb[:, 0, :], wf_re),
                (wf_sb[:, 1, :], wf_im),
                (wa_sb[:, :], w_attn),
                (wp_sb[:, :], w_proj),
                (fb_sb[:, :], f_bias.rearrange("(a d) -> a d", a=1).broadcast_to([P, D])),
                (w1_sb[:, :, :], w1.rearrange("e d h -> d e h")),
                (w2_sb[:, :, :, :].rearrange("p e c d -> p (e c) d"),
                 w2.rearrange("e (c p) d -> p (e c) d", p=P)),
            ):
                q.dma_start(dst, src).then_inc(s_w.sem, 16)
            for b in range(B):
                q.dma_start(b2rep[BE + b * E:BE + (b + 1) * E, :], b2).then_inc(s_w.sem, 16)

        def prep_pe(pe):
            pe.wait_ge(s_c.sem, s_c.total(16))
            pe.wait_ge(s_w.sem, s_w.total(16 * (NW + B)))
            for g in range(3):
                nc.tensor.transpose(bank[0][:, g * D:(g + 1) * D], wq_raw[:, g, :], ident)
            nc.tensor.transpose(bank[1][:, 0:E], r_raw[:, :], ident[0:E, 0:E])
            nc.tensor.transpose(bank[1][:, 64:64 + E * HC], b1_raw[:, :], ident[0:E * HC, 0:E * HC])
            re, im = wf_sb[:, 0, :], wf_sb[:, 1, :]
            nc.tensor.matmul(bank[2][:, 0:D], re, dft_c, start=True, stop=False)
            nc.tensor.matmul(bank[2][:, 0:D], im, dft_s, start=False, stop=True)
            nc.tensor.matmul(bank[2][:, D:2 * D], im, dft_c, start=True, stop=False)
            nc.tensor.matmul(bank[2][:, D:2 * D], re, dft_ns, start=False, stop=True).then_inc(s_prep_t.sem, 1)
            pe.wait_ge(s_prep_v.sem, s_prep_v.total(4))
            nc.tensor.matmul(bank[5][:, 0:D], a12[:, 0, :], dft_c, start=True, stop=False)
            nc.tensor.matmul(bank[5][:, 0:D], a12[:, 1, :], dft_ns, start=False, stop=True).then_inc(s_prep_t.sem, 1)

        def prep_dve(dve):
            dve.wait_ge(s_c.sem, s_c.total(16))
            nc.vector.tensor_copy(ident_bf[:, :], ident).then_inc(s_idb.sem, 1)
            dve.wait_ge(s_prep_t.sem, s_prep_t.total(1))
            nc.vector.tensor_copy(wqT[:, :], bank[0][:, 0:3 * D]).then_inc(s_prep_v.sem, 1)
            nc.vector.tensor_copy(rT[:, :], bank[1][:, 0:E]).then_inc(s_prep_v.sem, 1)
            nc.vector.tensor_copy(b1T[:, :], bank[1][:, 64:64 + E * HC]).then_inc(s_prep_v.sem, 1)
            nc.vector.tensor_copy(a12[:, :, :].rearrange("p a d -> p (a d)"),
                                  bank[2][:, 0:2 * D]).then_inc(s_prep_v.sem, 1)
            dve.wait_ge(s_prep_t.sem, s_prep_t.total(2))
            nc.vector.tensor_scalar(m_sb[:, :], bank[5][:, 0:D], 1.0 / D, None, ALU.mult).then_inc(s_prep_v.sem, 1)

        def layer_norm_stats(tag):
            s_six = signal(f"{tag}_bn_stats")
            s_agg = signal(f"{tag}_bn_aggr")
            s_mv = signal(f"{tag}_mean_var")
            s_ve = signal(f"{tag}_var_eps")
            s_sd = signal(f"{tag}_std")
            s_rstd = signal(f"{tag}_rstd")

            def dve_stats(dve):
                with nc.vector.Fori(0, B) as i:
                    dve.wait_ge(s_agg.sem, s_agg.at(i, 0))
                    for k in range(NT):
                        ins = nc.vector.bn_stats(st6[:, k, :], x_sb[:, i, k, :])
                    ins.then_inc(s_six.sem, 1)
                    dve.wait_ge(s_six.sem, s_six.at(i, 1))
                    dve.wait_ge(s_mv.sem, s_mv.at(i, 0))
                    waits_end(dve)
                    for k in range(NT):
                        ins = nc.vector.bn_aggr(mvt[:, k, :], st6[:, k, :])
                    ins.then_inc(s_agg.sem, 1)
                    dve.wait_ge(s_agg.sem, s_agg.at(i, 1))
                    nc.vector.tensor_copy(mv[:, i, :, :], mvt[:, :, :]).then_inc(s_mv.sem, 1)
                dve.wait_ge(s_mv.sem, s_mv.total(B))
                nc.vector.tensor_scalar(sd[:, :, :], mv[:, :, :, 1], EPS, None, ALU.add).then_inc(s_ve.sem, 1)
                dve.wait_ge(s_sd.sem, s_sd.total(1))
                nc.vector.reciprocal(rstd[:, :, :], sd[:, :, :]).then_inc(s_rstd.sem, 1)
                dve.wait_ge(s_rstd.sem, s_rstd.total(1))

            def act_std(act):
                act.wait_ge(s_ve.sem, s_ve.total(1))
                nc.scalar.activation(sd[:, :, :], sd[:, :, :], ACT.Sqrt).then_inc(s_sd.sem, 1)

            return dve_stats, act_std

        def normalise(s_xln, i):
            for k in range(NT):
                nc.vector.tensor_scalar(xln[:, k, :], x_sb[:, i, k, :], mv[:, i, k, 0:1],
                                                   rstd[:, i, k:k + 1], ALU.subtract, ALU.mult).then_inc(s_xln.sem, 1)

        ln1_dve, ln1_act = layer_norm_stats("ln1")
        ln2_dve, ln2_act = layer_norm_stats("ln2")
        ln3_dve, ln3_act = layer_norm_stats("ln3")
        ln4_dve, ln4_act = layer_norm_stats("ln4")

        A = lambda name, per=1: signal("lin_" + name, per)
        a_xln, a_xTp, a_xT = A("xln", NT), A("xT_psum"), A("xT")
        a_qkv, a_qv, a_kx, a_kxe = A("qkv_psum", NT), A("qv", NT), A("exp_k", NT), A("exp_k_eps")
        a_qmax, a_qc, a_qe, a_qsum = A("q_max"), A("q_shifted"), A("q_exp"), A("q_sum")
        a_kn, a_den, a_rden, a_qs = A("k_norm_psum"), A("denominator"), A("denominator_inverse"), A("q_soft")
        a_kv, a_cum, a_prod, a_red = A("outer", NT), A("outer_sums_psum", NT), A("q_times_sums", NT), A("y_intra", NT)
        a_stp, a_st = A("state_psum"), A("state")
        a_qsTp, a_qsT, a_yTp, a_yT = A("q_soft_T_psum"), A("q_soft_T"), A("yT_psum"), A("yT")
        a_o, a_x = A("projected_psum"), A("x_updated")

        new_stage()
        qv = scratch("qv", [P, 2, NT, D])
        kx = scratch("kx", [P, NT, D])
        qmax = scratch("qmax", [P, NT * HEADS])
        qe = scratch("qe", [P, NT, D])
        qsum = scratch("qsum", [P, NT * HEADS])
        qs = scratch("qs", [P, NT, D])
        kv = scratch("kv", [P, 2, HEADS * L * L])
        prod = scratch("prod", [P, 2, HEADS * L * L])
        state = scratch("state", [P, NT - 1, D])
        tT = scratch("tT", [P, T])
        yT = scratch("yT", [P, T])
        y_in = scratch("y_in", [P, NT, D])
        by_head = lambda ap: ap.rearrange("p k (h l) -> p (k h) l", l=L)
        psT, psN, psS, psY = bank[0], bank[5], bank[6], bank[7]
        psQ = (bank[1], bank[2])

        def lin_dve(dve):
            with nc.vector.Fori(0, B) as i:
                dve.wait_ge(a_xTp.sem, a_xTp.at(i, 0))
                normalise(a_xln, i)
                dve.wait_ge(a_qv.sem, a_qv.at(i, NT))
                dve.wait_ge(a_qc.sem, a_qc.at(i, 0))
                nc.vector.tensor_reduce(qmax[:, :], by_head(qv[:, 0, :, :]), AX.X, ALU.max).then_inc(a_qmax.sem, 1)
                dve.wait_ge(a_qmax.sem, a_qmax.at(i, 1))
                dve.wait_ge(a_qe.sem, a_qe.at(i, 0))
                nc.vector.tensor_tensor(by_head(qs[:, :, :]), by_head(qv[:, 0, :, :]),
                                                  qmax[:, :].unsqueeze(2).broadcast_to([P, NT * HEADS, L]),
                                                  ALU.subtract).then_inc(a_qc.sem, 1)
                dve.wait_ge(a_qe.sem, a_qe.at(i, 1))
                nc.vector.tensor_reduce(qsum[:, :], by_head(qe[:, :, :]), AX.X, ALU.add).then_inc(a_qsum.sem, 1)
                dve.wait_ge(a_kn.sem, a_kn.at(i, 1))
                dve.wait_ge(a_qsum.sem, a_qsum.at(i, 1))
                nc.vector.tensor_tensor(by_head(y_in[:, :, :]), psN[:, :].rearrange("p (kh l) -> p kh l", l=L),
                                                   qsum[:, :].unsqueeze(2).broadcast_to([P, NT * HEADS, L]), ALU.mult).then_inc(a_den.sem, 1)
                dve.wait_ge(a_den.sem, a_den.at(i, 1))
                nc.vector.reciprocal(y_in[:, :, :], y_in[:, :, :]).then_inc(a_rden.sem, 1)
                dve.wait_ge(a_rden.sem, a_rden.at(i, 1))
                nc.vector.tensor_tensor(qs[:, :, :], qe[:, :, :], y_in[:, :, :], ALU.mult).then_inc(a_qs.sem, 1)
                dve.wait_ge(a_qs.sem, a_qs.at(i, 1))
                dve.wait_ge(a_stp.sem, a_stp.at(i, 1))
                nc.vector.tensor_tensor(state[:, :, :], psS[:, 0:(NT - 1) * D].rearrange("p (k d) -> p k d", d=D),
                                                  blockdiag.unsqueeze(1).broadcast_to([P, NT - 1, D]), ALU.mult).then_inc(a_st.sem, 1)
                for k in range(NT):
                    dve.wait_ge(a_cum.sem, a_cum.at(i, k + 1))
                    if k >= 2:
                        dve.wait_ge(a_red.sem, a_red.at(i, k - 1))
                    else:
                        dve.wait_ge(a_red.sem, a_red.at(i, 0))
                    nc.vector.tensor_tensor(
                        prod[:, k % 2, :].rearrange("p (hl m) -> p hl m", m=L),
                        wide[:, :].rearrange("p (hl m) -> p hl m", m=L),
                        qs[:, k, :].unsqueeze(2).broadcast_to([P, D, L]), ALU.mult).then_inc(a_prod.sem, 1)
                    dve.wait_ge(a_prod.sem, a_prod.at(i, k + 1))
                    if k == 0:
                        dve.wait_ge(a_yTp.sem, a_yTp.at(i, 0))
                    nc.vector.tensor_reduce(
                        y_in[:, k, :].rearrange("p (h m) -> p h m", m=L),
                        prod[:, k % 2, :].rearrange("p (h l m) -> p h m l", l=L, m=L), AX.X, ALU.add).then_inc(a_red.sem, 1)
                dve.wait_ge(a_o.sem, a_o.at(i, 1))
                nc.vector.tensor_tensor(x_sb[:, i, :, :], x_sb[:, i, :, :],
                                                 psN[:, :].rearrange("p (k d) -> p k d", d=D), ALU.add).then_inc(a_x.sem, 1)
                dve.wait_ge(a_x.sem, a_x.at(i, 1))

        def lin_act(act):
            with nc.scalar.Fori(0, B) as i:
                act.wait_ge(a_xTp.sem, a_xTp.at(i, 1))
                act.wait_ge(a_qkv.sem, a_qkv.at(i, 0))
                nc.scalar.activation(xT[:, :], psT[:, :], ACT.Copy).then_inc(a_xT.sem, 1)
                act.wait_ge(a_kv.sem, a_kv.at(i, 0))
                act.wait_ge(a_stp.sem, a_stp.at(i, 0))
                act.wait_ge(a_kn.sem, a_kn.at(i, 0))
                act.wait_ge(a_qc.sem, a_qc.at(i, 0))
                for k in range(NT):
                    act.wait_ge(a_qkv.sem, a_qkv.at(i, k + 1))
                    psq = psQ[k % 2][:, 0:3 * D].rearrange("p (g d) -> p g d", g=3)
                    nc.scalar.activation(kx[:, k, :], psq[:, 1, :], ACT.Exp, scale=SCALE).then_inc(a_kx.sem, 1)
                    nc.scalar.activation(qv[:, :, k, :], psq[:, 0:3:2, :], ACT.Copy).then_inc(a_qv.sem, 1)
                act.wait_ge(a_qc.sem, a_qc.at(i, 1))
                act.wait_ge(a_qs.sem, a_qs.at(i, 0))
                nc.scalar.activation(qe[:, :, :], qs[:, :, :], ACT.Exp, scale=SCALE).then_inc(a_qe.sem, 1)
                act.wait_ge(a_qsTp.sem, a_qsTp.at(i, 1))
                act.wait_ge(a_yTp.sem, a_yTp.at(i, 0))
                nc.scalar.activation(tT[:, 0:(NT - 1) * P], psT[:, 0:(NT - 1) * P], ACT.Copy).then_inc(a_qsT.sem, 1)
                act.wait_ge(a_yTp.sem, a_yTp.at(i, 1))
                act.wait_ge(a_o.sem, a_o.at(i, 0))
                nc.scalar.activation(yT[:, :], psY[:, :], ACT.Copy).then_inc(a_yT.sem, 1)

        def lin_pool(pool):
            with nc.gpsimd.Fori(0, B) as i:
                pool.wait_ge(a_kx.sem, a_kx.at(i, NT))
                waits_end(pool)
                nc.gpsimd.tensor_scalar(kx[:, :, :], kx[:, :, :], 1e-6, None, ALU.add).then_inc(a_kxe.sem, 1)
                pool.wait_ge(a_kxe.sem, a_kxe.at(i, 1))
                pool.wait_ge(a_qv.sem, a_qv.at(i, NT))
                for k in range(NT):
                    pool.wait_ge(a_cum.sem, a_cum.at(i, k - 1 if k >= 2 else 0))
                    shape = [P, HEADS, L, L]
                    nc.gpsimd.tensor_tensor(
                        kv[:, k % 2, :].rearrange("p (h l m) -> p h l m", l=L, m=L),
                        kx[:, k, :].rearrange("p (h l) -> p h l", l=L).unsqueeze(3).broadcast_to(shape),
                        qv[:, 1, k, :].rearrange("p (h m) -> p h m", m=L).unsqueeze(2).broadcast_to(shape),
                        ALU.mult).then_inc(a_kv.sem, 1)

        def lin_pe(pe):
            with nc.tensor.Fori(0, B) as i:
                pe.wait_ge(a_xln.sem, a_xln.at(i, NT))
                pe.wait_ge(a_qsT.sem, a_qsT.at(i, 0))
                for k in range(NT):
                    ins = nc.tensor.transpose(psT[:, k * P:(k + 1) * P], xln[:, k, :], ident)
                ins.then_inc(a_xTp.sem, 1)
                pe.wait_ge(a_xT.sem, a_xT.at(i, 1))
                for k in range(NT):
                    if k >= 2:
                        pe.wait_ge(a_qv.sem, a_qv.at(i, k - 1))
                    else:
                        pe.wait_ge(a_qv.sem, a_qv.at(i, 0))
                    nc.tensor.matmul(psQ[k % 2][:, 0:3 * D], xT[:, k * P:(k + 1) * P], wqT[:, :],
                                                start=True, stop=True).then_inc(a_qkv.sem, 1)
                pe.wait_ge(a_kxe.sem, a_kxe.at(i, 1))
                pe.wait_ge(a_x.sem, a_x.at(i, 0))
                for k in range(NT):
                    for j in range(k):
                        nc.tensor.matmul(psN[:, k * D:(k + 1) * D], ones, kx[:, j, :], start=j == 0, stop=False)
                    ins = nc.tensor.matmul(psN[:, k * D:(k + 1) * D], tri, kx[:, k, :], start=k == 0, stop=True)
                ins.then_inc(a_kn.sem, 1)
                pe.wait_ge(a_st.sem, a_st.at(i, 0))
                pe.wait_ge(a_qv.sem, a_qv.at(i, NT))
                for k in range(1, NT):
                    for j in range(k):
                        ins = nc.tensor.matmul(psS[:, (k - 1) * D:k * D], kx[:, j, :], qv[:, 1, j, :],
                                               start=j == 0, stop=j == k - 1)
                ins.then_inc(a_stp.sem, 1)
                for k in range(NT):
                    pe.wait_ge(a_kv.sem, a_kv.at(i, k + 1))
                    pe.wait_ge(a_prod.sem, a_prod.at(i, k))
                    nc.tensor.matmul(wide[:, 0:512], tri, kv[:, k % 2, 0:512], start=True, stop=True)
                    nc.tensor.matmul(wide[:, 512:1024], tri, kv[:, k % 2, 512:1024],
                                                start=True, stop=True).then_inc(a_cum.sem, 1)
                pe.wait_ge(a_qs.sem, a_qs.at(i, 1))
                for k in range(1, NT):
                    ins = nc.tensor.transpose(psT[:, (k - 1) * P:k * P], qs[:, k, :], ident)
                ins.then_inc(a_qsTp.sem, 1)
                pe.wait_ge(a_qsT.sem, a_qsT.at(i, 1))
                pe.wait_ge(a_st.sem, a_st.at(i, 1))
                pe.wait_ge(a_red.sem, a_red.at(i, NT))
                pe.wait_ge(a_yT.sem, a_yT.at(i, 0))
                for k in range(NT):
                    at = psY[:, k * P:(k + 1) * P]
                    if k:
                        nc.tensor.matmul(at, state[:, k - 1, :], tT[:, (k - 1) * P:k * P], start=True, stop=False)
                    ins = nc.tensor.matmul(at, y_in[:, k, :], ident, start=k == 0, stop=True)
                ins.then_inc(a_yTp.sem, 1)
                pe.wait_ge(a_yT.sem, a_yT.at(i, 1))
                for k in range(NT):
                    ins = nc.tensor.matmul(psN[:, k * D:(k + 1) * D], yT[:, k * P:(k + 1) * P], wo_sb[:, :],
                                           start=True, stop=True)
                ins.then_inc(a_o.sem, 1)

        R = lambda name, per=1, step=1: signal("route_" + name, per, step)
        r_xln, r_xTp, r_xT, r_lgp, r_lg = R("xln", NT), R("xT_psum"), R("xT"), R("logits_psum"), R("logits")
        r_max, r_sub, r_exp, r_sum, r_inv, r_sc = (R("max"), R("shifted"), R("exp"), R("sum"), R("inverse"),
                                                   R("scores"))
        r_scTp, r_scT, r_top, r_rep, r_eq = R("scores_T_psum"), R("scores_T", 2), R("top8"), R("replaced"), R("tie")
        r_run, r_first, r_mask, r_cnt, r_pos = R("tie_count"), R("tie_first"), R("mask"), R("count"), R("pos")
        r_posb, r_posTp, r_posT, r_last = R("pos_bf"), R("pos_T_psum"), R("pos_T"), R("last_slot", 2)
        r_gt, r_moved = R("gates_T"), R("gates_T_moved", 1, 16)
        r_posd = R("pos_in_dram", 1, 16)
        r_part = R("score_parts", 5)

        NR = NT * BE
        new_stage()
        lg = scratch("lg", [P, NT, B, E])
        rmax = scratch("rmax", [P, NT * B])
        sc = scratch("sc", [P, NT, B, E])
        sc_rest = scratch("sc_rest", [P, NT, B, E])
        scT = scratch("scT", [BE, T])
        work = scratch("work", [BE, T])
        top8 = scratch("top8", [BE, 8])
        tie = scratch("tie", [BE, T])
        cnt = scratch("cnt", [BE, T])
        pos = scratch("pos", [BE, T])
        pos_bf = scratch("pos_bf", [BE, T], BF16)
        gates_T = scratch("gates_T", [BE, T])
        pos_dram = nc.dram_tensor("pos_dram", (BE, T), BF16, kind="Internal").ap()

        def route_dve(dve):
            with nc.vector.Fori(0, B) as i:
                dve.wait_ge(r_xTp.sem, r_xTp.at(i, 0))
                normalise(r_xln, i)
            dve.wait_ge(r_lg.sem, r_lg.total(B))
            rows = lambda t: t[:, :, :, :].rearrange("p k b e -> p (k b) e")
            spread = rmax[:, :].unsqueeze(2).broadcast_to([P, NT * B, E])
            nc.vector.tensor_reduce(rmax[:, :], rows(lg), AX.X, ALU.max).then_inc(r_max.sem, 1)
            dve.wait_ge(r_max.sem, r_max.total(1))
            nc.vector.tensor_tensor(rows(lg), rows(lg), spread, ALU.subtract).then_inc(r_sub.sem, 1)
            dve.wait_ge(r_exp.sem, r_exp.total(1))
            nc.vector.tensor_reduce(rmax[:, :], rows(lg), AX.X, ALU.add).then_inc(r_sum.sem, 1)
            dve.wait_ge(r_sum.sem, r_sum.total(1))
            nc.vector.reciprocal(rmax[:, :], rmax[:, :]).then_inc(r_inv.sem, 1)
            dve.wait_ge(r_inv.sem, r_inv.total(1))
            nc.vector.tensor_tensor(rows(sc), rows(lg), spread, ALU.mult).then_inc(r_sc.sem, 1)
            dve.wait_ge(r_scTp.sem, r_scTp.total(1))
            nc.vector.tensor_copy(scT[:, :], bank[0][0:BE, :]).then_inc(r_scT.sem, 1)
            nc.vector.tensor_copy(work[:, :], bank[0][0:BE, :]).then_inc(r_scT.sem, 1)
            with nc.vector.Fori(0, (CAP - 1) // 8) as i:
                dve.wait_ge(r_scT.sem, r_scT.total(2))
                dve.wait_ge(r_rep.sem, r_rep.at(i, 0))
                waits_end(dve)
                nc.vector.max(top8[:, :], work[:, :]).then_inc(r_top.sem, 1)
                dve.wait_ge(r_top.sem, r_top.at(i, 1))
                waits_end(dve)
                nc.vector.match_replace(out=work[:, :], in_to_replace=top8[:, :], in_values=work[:, :],
                                                   imm_value=-1.0).then_inc(r_rep.sem, 1)
            dve.wait_ge(r_rep.sem, r_rep.total((CAP - 1) // 8))
            nc.vector.max(top8[:, :], work[:, :]).then_inc(r_top.sem, 1)
            dve.wait_ge(r_top.sem, r_top.total((CAP - 1) // 8 + 1))
            nc.vector.tensor_scalar(tie[:, :], work[:, :], top8[:, 0:1], None, ALU.is_equal).then_inc(r_eq.sem, 1)
            dve.wait_ge(r_eq.sem, r_eq.total(1))
            nc.vector.tensor_tensor_scan(out=cnt[:, :], data0=tie[:, :], data1=tie[:, :], initial=0.0,
                                                    op0=ALU.add, op1=ALU.bypass).then_inc(r_run.sem, 1)
            dve.wait_ge(r_run.sem, r_run.total(1))
            nc.vector.scalar_tensor_tensor(out=tie[:, :], in0=cnt[:, :], scalar=1.0, in1=tie[:, :],
                                                        op0=ALU.is_equal, op1=ALU.mult).then_inc(r_first.sem, 1)
            dve.wait_ge(r_first.sem, r_first.total(1))
            nc.vector.scalar_tensor_tensor(out=work[:, :], in0=work[:, :], scalar=-1.0, in1=tie[:, :],
                                                       op0=ALU.is_equal, op1=ALU.add).then_inc(r_mask.sem, 1)
            dve.wait_ge(r_mask.sem, r_mask.total(1))
            nc.vector.tensor_tensor_scan(out=cnt[:, :], data0=work[:, :], data1=work[:, :], initial=0.0,
                                                    op0=ALU.add, op1=ALU.bypass).then_inc(r_cnt.sem, 1)
            dve.wait_ge(r_cnt.sem, r_cnt.total(1))
            nc.vector.tensor_tensor(tie[:, :], cnt[:, :], work[:, :], ALU.mult).then_inc(r_run.sem, 1)
            dve.wait_ge(r_run.sem, r_run.total(2))
            nc.vector.tensor_scalar(pos[:, :], tie[:, :], -1.0, None, ALU.add).then_inc(r_pos.sem, 1)
            dve.wait_ge(r_pos.sem, r_pos.total(1))
            nc.vector.tensor_copy(pos_bf[:, :], pos[:, :]).then_inc(r_posb.sem, 1)
            nc.vector.tensor_tensor(gates_T[:, :], work[:, :], scT[:, :], ALU.mult).then_inc(r_gt.sem, 1)
            nc.vector.scalar_tensor_tensor(out=rest_l[0:BE, :], in0=pos[:, :], scalar=float(P),
                                                       in1=scT[:, :], op0=ALU.is_equal, op1=ALU.mult).then_inc(r_last.sem, 1)
            dve.wait_ge(r_posTp.sem, r_posTp.total(1))
            nc.vector.tensor_copy(posT[:, :, :, :].rearrange("p k b e -> p (k b e)"), bank[1][:, 0:NR]).then_inc(r_posT.sem, 1)
            split3(dve, r_part, sc, sc_rest, [sc_part[:, :, :, :, n] for n in range(PARTS)])

        def split3(dve, sig, whole, rest, parts):
            full = (slice(None),) * len(whole.shape)
            nc.vector.tensor_copy(parts[0], whole[full]).then_inc(sig.sem, 1)
            dve.wait_ge(sig.sem, sig.total(1))
            nc.vector.tensor_tensor(rest[full], whole[full], parts[0], ALU.subtract).then_inc(sig.sem, 1)
            dve.wait_ge(sig.sem, sig.total(2))
            nc.vector.tensor_copy(parts[1], rest[full]).then_inc(sig.sem, 1)
            dve.wait_ge(sig.sem, sig.total(3))
            nc.vector.tensor_tensor(rest[full], rest[full], parts[1], ALU.subtract).then_inc(sig.sem, 1)
            dve.wait_ge(sig.sem, sig.total(4))
            nc.vector.tensor_copy(parts[2], rest[full]).then_inc(sig.sem, 1)

        def route_act(act):
            with nc.scalar.Fori(0, B) as i:
                act.wait_ge(r_xTp.sem, r_xTp.at(i, 1))
                act.wait_ge(r_lgp.sem, r_lgp.at(i, 0))
                nc.scalar.activation(xT[:, :], bank[0][:, :], ACT.Copy).then_inc(r_xT.sem, 1)
                act.wait_ge(r_lgp.sem, r_lgp.at(i, 1))
                nc.scalar.activation(lg[:, :, i, :], bank[1][:, 0:NT * E].rearrange("p (k e) -> p k e", e=E),
                                               ACT.Copy).then_inc(r_lg.sem, 1)
            act.wait_ge(r_sub.sem, r_sub.total(1))
            nc.scalar.activation(lg[:, :, :, :], lg[:, :, :, :], ACT.Exp).then_inc(r_exp.sem, 1)

        def route_pe(pe):
            with nc.tensor.Fori(0, B) as i:
                pe.wait_ge(r_xln.sem, r_xln.at(i, NT))
                pe.wait_ge(r_xT.sem, r_xT.at(i, 0))
                for k in range(NT):
                    ins = nc.tensor.transpose(bank[0][:, k * P:(k + 1) * P], xln[:, k, :], ident)
                ins.then_inc(r_xTp.sem, 1)
                pe.wait_ge(r_xT.sem, r_xT.at(i, 1))
                pe.wait_ge(r_lg.sem, r_lg.at(i, 0))
                for k in range(NT):
                    ins = nc.tensor.matmul(bank[1][:, k * E:(k + 1) * E], xT[:, k * P:(k + 1) * P], rT[:, :],
                                           start=True, stop=True)
                ins.then_inc(r_lgp.sem, 1)
            pe.wait_ge(r_sc.sem, r_sc.total(1))
            for k in range(NT):
                ins = nc.tensor.transpose(bank[0][0:BE, k * P:(k + 1) * P],
                                          sc[:, k, :, :].rearrange("p b e -> p (b e)"), ident)
            ins.then_inc(r_scTp.sem, 1)
            pe.wait_ge(r_pos.sem, r_pos.total(1))
            for k in range(NT):
                ins = nc.tensor.transpose(bank[1][:, k * BE:(k + 1) * BE], pos[:, k * P:(k + 1) * P],
                                          ident[0:BE, 0:BE])
            ins.then_inc(r_posTp.sem, 1)

        def route_sync(sp):
            sp.wait_ge(r_posb.sem, r_posb.total(1))
            sp.dma_start(pos_dram, pos_bf[:, :]).then_inc(r_posd.sem, 16)
            sp.wait_ge(r_gt.sem, r_gt.total(1))
            sp.dma_start(rest_l[BE:2 * BE, :], gates_T[:, :]).then_inc(r_moved.sem, 16)

        NP = 2
        M = lambda name, per=1, step=1: signal("moe_" + name, per, step)
        m_bc, m_xln, m_part = M("pos_spread", NP, 16), M("xln", NP * NT), M("x_parts", NP * 5)
        m_scp, m_pick, m_place = M("score_parts", NP), M("pick", NP * NT), M("place", NP)
        m_xgp, m_xg = M("gathered_psum", NP * 3), M("gathered", NP * 3)
        m_gp, m_gate = M("gate_psum"), M("gate")
        m_hp, m_h = M("hidden_psum", E * HC), M("hidden", E * HC)
        m_yp, m_y, m_yl = M("y_psum", E), M("y_gated", E), M("y_last", E)
        m_rep, m_repT, m_rest = M("y_last_spread"), M("y_last_T_psum"), M("rest", 2 * NP)
        m_sp, m_x = M("scattered_psum", NP), M("x_updated", NP)

        slots, slot_row = const("slots"), const("slot_row")
        new_stage()
        slots_bf = scratch("slots_bf", [P, CAP], BF16)
        m_slots = M("slots_bf")
        pos_bc = scratch("pos_bc", [P, NP, E, T], BF16)
        x_rest = scratch("x_rest", [P, NT, D])
        x_part = scratch("x_part", [P, PARTS, NT, D], BF16)
        sc_now = scratch("sc_now", [P, NP, NT, E, PARTS], BF16)
        pick = scratch("pick", [P, NT, E, CAP], BF16)
        place = scratch("place", [P, NP, E, T])
        xg = scratch("xg", [P, NP, E, CAP])
        gate = scratch("gate", [P, NP, E])
        hT = scratch("hT", [P, 2, HC, NP, CAP])
        yg = scratch("yg", [P, NP, E, D])
        yl = scratch("yl", [P, NP, E])
        yl_rep = scratch("yl_rep", [P, NP, B, E])
        rest_r = scratch("rest_r", [P, NP, D])
        psH = (wide[:, 0:512], wide[:, 512:1024], bank[5], bank[6])
        psYe = (bank[7], bank[2])
        psG = bank[2]

        def moe_sync(sp):
            sp.wait_ge(r_posd.sem, r_posd.total(16))
            sp.wait_ge(r_moved.sem, r_moved.total(16))
            sp.wait_ge(r_part.sem, r_part.total(5))
            with nc.sync.Fori(0, B // NP) as i:
                sp.wait_ge(m_place.sem, m_place.at(i, 0))
                for r in range(NP):
                    src = pos_dram.rearrange("(b e) t -> b (e t)", e=E)[NP * i + r]
                    src = src.rearrange("(a n) -> a n", a=1) if len(src.shape) == 1 else src
                    sp.dma_start(pos_bc[:, r, :, :].rearrange("p e t -> p (e t)"),
                                 src.broadcast_to([P, E * T])).then_inc(m_bc.sem, 16)

        def moe_pool(pool):
            with nc.gpsimd.Fori(0, B // NP) as i:
                for r in range(NP):
                    pool.wait_ge(m_bc.sem, m_bc.at(i, NP))
                    pool.wait_ge(m_sp.sem, m_sp.at(i, 0))
                    waits_end(pool)
                    nc.gpsimd.tensor_scalar(place[:, r, :, :].rearrange("p e t -> p (e t)"),
                                                         pos_bc[:, r, :, :].rearrange("p e t -> p (e t)"),
                                                         slot_row, None, ALU.is_equal).then_inc(m_place.sem, 1)

        def moe_dve(dve):
            nc.vector.tensor_copy(slots_bf[:, :], slots).then_inc(m_slots.sem, 1)
            dve.wait_ge(m_slots.sem, m_slots.total(1))
            with nc.vector.Fori(0, B // NP) as i:
                for r in range(NP):
                    s = lambda n: 5 * r + n
                    for k in range(NT):
                        ins = nc.vector.tensor_scalar(xln[:, k, :], x_sb[:, NP * i + r, k, :], mv[:, NP * i + r, k, 0:1],
                                                      rstd[:, NP * i + r, k:k + 1], ALU.subtract, ALU.mult)
                        ins.then_inc(m_xln.sem, 1)
                    dve.wait_ge(m_xln.sem, m_xln.at(i, (r + 1) * NT))
                    dve.wait_ge(m_xgp.sem, m_xgp.at(i, 3 * r))
                    if r == 0:
                        dve.wait_ge(m_gp.sem, m_gp.at(i, 0))
                    nc.vector.tensor_copy(x_part[:, 0], xln[:, :, :]).then_inc(m_part.sem, 1)
                    dve.wait_ge(m_part.sem, m_part.at(i, s(1)))
                    nc.vector.tensor_tensor(x_rest[:, :, :], xln[:, :, :], x_part[:, 0], ALU.subtract).then_inc(m_part.sem, 1)
                    dve.wait_ge(m_part.sem, m_part.at(i, s(2)))
                    nc.vector.tensor_copy(x_part[:, 1], x_rest[:, :, :]).then_inc(m_part.sem, 1)
                    dve.wait_ge(m_part.sem, m_part.at(i, s(3)))
                    nc.vector.tensor_tensor(x_rest[:, :, :], x_rest[:, :, :], x_part[:, 1], ALU.subtract).then_inc(m_part.sem, 1)
                    dve.wait_ge(m_part.sem, m_part.at(i, s(4)))
                    nc.vector.tensor_copy(x_part[:, 2], x_rest[:, :, :]).then_inc(m_part.sem, 1)
                    nc.vector.tensor_copy(sc_now[:, r], sc_part[:, :, NP * i + r, :, :]).then_inc(m_scp.sem, 1)
                    if r == 1:
                        dve.wait_ge(m_gr.sem, m_gr.at(i, 1))
                    for k in range(NT):
                        nc.vector.tensor_tensor(
                            pick[:, k, :, :], slots_bf[:, :].unsqueeze(1).broadcast_to([P, E, CAP]),
                            posT[:, k, NP * i + r, :].unsqueeze(2).broadcast_to([P, E, CAP]), ALU.is_equal).then_inc(m_pick.sem, 1)
                dve.wait_ge(m_gp.sem, m_gp.at(i, 1))
                dve.wait_ge(m_y.sem, m_y.at(i, 0))
                nc.vector.tensor_reduce(gate[:, :, :],
                                                    psG[:, 0:NP * E * PARTS].rearrange("p (r e n) -> p r e n", e=E, n=PARTS),
                                                    AX.X, ALU.add).then_inc(m_gate.sem, 1)
                dve.wait_ge(m_gate.sem, m_gate.at(i, 1))
                for e in range(E):
                    dve.wait_ge(m_yp.sem, m_yp.at(i, e + 1))
                    dve.wait_ge(m_sp.sem, m_sp.at(i, 0))
                    nc.vector.tensor_tensor(yg[:, :, e, :],
                                                     psYe[e % 2][:, 0:NP * D].rearrange("p (r d) -> p r d", d=D),
                                                     gate[:, :, e].unsqueeze(2).broadcast_to([P, NP, D]), ALU.mult).then_inc(m_y.sem, 1)
                    dve.wait_ge(m_rep.sem, m_rep.at(i, 0))
                    nc.vector.tensor_copy(yl[:, :, e], psYe[e % 2][:, NP * D:NP * D + NP]).then_inc(m_yl.sem, 1)
                dve.wait_ge(m_yl.sem, m_yl.at(i, E))
                dve.wait_ge(m_repT.sem, m_repT.at(i, 0))
                nc.vector.tensor_copy(yl_rep[:, :, :, :], yl[:, :, :].unsqueeze(2).broadcast_to([P, NP, B, E])).then_inc(m_rep.sem, 1)
                dve.wait_ge(m_repT.sem, m_repT.at(i, 1))
                for r in range(NP):
                    nc.vector.tensor_scalar(rest_r[0:BE, r, :], bank[5][0:BE, r * D:(r + 1) * D],
                                                        seqmask[0:BE, NP * i + r].unsqueeze(1), None, ALU.mult).then_inc(m_rest.sem, 1)
                    nc.vector.tensor_scalar(rest_r[BE:2 * BE, r, :], b2rep[BE:2 * BE, :],
                                                        seqmask[BE:2 * BE, NP * i + r].unsqueeze(1), None, ALU.mult).then_inc(m_rest.sem, 1)
                for r in range(NP):
                    dve.wait_ge(m_sp.sem, m_sp.at(i, r + 1))
                    nc.vector.tensor_tensor(x_sb[:, NP * i + r], x_sb[:, NP * i + r],
                                                     bank[r][:, :].rearrange("p (k d) -> p k d", d=D), ALU.add).then_inc(m_x.sem, 1)
            dve.wait_ge(m_x.sem, m_x.at(B // NP, 0))

        m_gr = M("gates_gathered_first")

        def moe_act(act):
            with nc.scalar.Fori(0, B // NP) as i:
                for r in range(NP):
                    for c in range(3):
                        act.wait_ge(m_xgp.sem, m_xgp.at(i, 3 * r + c + 1))
                        act.wait_ge(m_hp.sem, m_hp.at(i, 0))
                        nc.scalar.activation(
                            xg[:, r, :, :].rearrange("p e c -> p (e c)")[:, c * GC:(c + 1) * GC],
                            bank[(3 * r + c) % 2][:, 0:GC], ACT.Copy).then_inc(m_xg.sem, 1)
                for e in range(E):
                    for c in range(HC):
                        act.wait_ge(m_hp.sem, m_hp.at(i, e * HC + c + 1))
                        act.wait_ge(m_yp.sem, m_yp.at(i, e - 1 if e >= 2 else 0))
                        nc.scalar.activation(hT[:, e % 2, c, :, :],
                                                      psH[c][:, 0:NP * CAP].rearrange("p (r c) -> p r c", c=CAP),
                                                      ACT.Gelu, bias=b1T[:, e * HC + c:e * HC + c + 1]).then_inc(m_h.sem, 1)

        def moe_pe(pe):
            def hidden(i, e):
                for c in range(HC):
                    if e:
                        pe.wait_ge(m_h.sem, m_h.at(i, (e - 1) * HC + c + 1))
                    else:
                        pe.wait_ge(m_h.sem, m_h.at(i, 0))
                    nc.tensor.matmul(psH[c][:, 0:NP * CAP].rearrange("p (r c) -> p r c", c=CAP),
                                               w1_sb[:, e, c * P:(c + 1) * P], xg[:, :, e, :], start=True, stop=True).then_inc(m_hp.sem, 1)

            def output(i, e):
                pe.wait_ge(m_h.sem, m_h.at(i, (e + 1) * HC))
                if e >= 2:
                    pe.wait_ge(m_yl.sem, m_yl.at(i, e - 1))
                else:
                    pe.wait_ge(m_yl.sem, m_yl.at(i, 0))
                for r in range(NP):
                    for c in range(HC):
                        nc.tensor.matmul(psYe[e % 2][:, r * D:(r + 1) * D], hT[:, e % 2, c, r, 0:P], w2_sb[:, e, c, :],
                                         start=c == 0, stop=c == HC - 1)
                for c in range(HC):
                    ins = nc.tensor.matmul(psYe[e % 2][:, NP * D:NP * D + NP], w2_sb[:, e, c, :],
                                           hT[:, e % 2, c, :, P], start=c == 0, stop=c == HC - 1)
                ins.then_inc(m_yp.sem, 1)

            pe.wait_ge(r_moved.sem, r_moved.total(16))
            with nc.tensor.Fori(0, B // NP) as i:
                pe.wait_ge(m_x.sem, m_x.at(i, 0))
                for r in range(NP):
                    pe.wait_ge(m_part.sem, m_part.at(i, 5 * (r + 1)))
                    pe.wait_ge(m_pick.sem, m_pick.at(i, (r + 1) * NT))
                    for c in range(3):
                        u = 3 * r + c
                        if u >= 2:
                            pe.wait_ge(m_xg.sem, m_xg.at(i, u - 1))
                        else:
                            pe.wait_ge(m_xg.sem, m_xg.at(i, 0))
                        for k in range(NT):
                            for n in range(PARTS):
                                ins = nc.tensor.matmul(
                                    bank[u % 2][:, 0:GC], x_part[:, n, k, :],
                                    pick[:, k, :, :].rearrange("p e c -> p (e c)")[:, c * GC:(c + 1) * GC],
                                    start=k == 0 and n == 0, stop=k == NT - 1 and n == PARTS - 1)
                        ins.then_inc(m_xgp.sem, 1)
                    pe.wait_ge(m_scp.sem, m_scp.at(i, r + 1))
                    if r == 0:
                        pe.wait_ge(m_yl.sem, m_yl.at(i, 0))
                    for e in range(E):
                        for k in range(NT):
                            at = (r * E + e) * PARTS
                            ins = nc.tensor.matmul(psG[:, at:at + PARTS], pick[:, k, e, 0:P], sc_now[:, r, k, e, :],
                                                   start=k == 0, stop=k == NT - 1)
                    ins.then_inc((m_gr if r == 0 else m_gp).sem, 1)
                pe.wait_ge(m_xg.sem, m_xg.at(i, 3 * NP))
                hidden(i, 0)
                for e in range(E):
                    if e + 1 < E:
                        hidden(i, e + 1)
                    if e == 1:
                        pe.wait_ge(m_gate.sem, m_gate.at(i, 1))
                    output(i, e)
                pe.wait_ge(m_rep.sem, m_rep.at(i, 1))
                pe.wait_ge(m_h.sem, m_h.at(i, E * HC))
                waits_end(pe)
                for r in range(NP):
                    ins = nc.tensor.transpose(bank[5][0:BE, r * D:(r + 1) * D],
                                              yl_rep[:, r, :, :].rearrange("p b e -> p (b e)"), ident)
                ins.then_inc(m_repT.sem, 1)
                pe.wait_ge(m_rest.sem, m_rest.at(i, 2 * NP))
                pe.wait_ge(m_y.sem, m_y.at(i, E))
                pe.wait_ge(m_place.sem, m_place.at(i, NP))
                for r in range(NP):
                    for k in range(NT):
                        at = bank[r][:, k * D:(k + 1) * D]
                        for e in range(E):
                            nc.tensor.matmul(at, place[:, r, e, k * P:(k + 1) * P], yg[:, r, e, :],
                                             start=e == 0, stop=False)
                        ins = nc.tensor.matmul(at, rest_l[:, k * P:(k + 1) * P], rest_r[:, r, :], start=False, stop=True)
                    ins.then_inc(m_sp.sem, 1)

        Q = lambda name, per=1, step=1: signal("mqa_" + name, per, step)
        q_init = Q("buffers_set")
        q_xln, q_xTp, q_xT, q_qkvp, q_qkv = Q("xln", NT), Q("xT_psum"), Q("xT"), Q("qkv_psum", NT), Q("qkv", NT)
        q_kpart, q_qpart, q_v, q_kx, q_qx = Q("k_parts", 5), Q("q_parts", 5), Q("v"), Q("k_slots", 3), Q("q_slots", 3)
        q_kTp, q_kTm, q_kTe = Q("kT_psum"), Q("kT_for_max"), Q("kT_for_exp")
        NU = HEADS // 2
        q_qTp, q_qTa, q_qTv = Q("qT_psum", NU), Q("qT_even", NU // 2), Q("qT_odd", NU // 2)
        max_units = [(k, h, n) for k in range(NT) for n in (max(1, 4 // (k + 1) if k != 2 else 1),)
                     for h in range(0, HEADS, n)]
        NM = len(max_units)
        q_smp, q_mx, q_neg, q_mpart = Q("max_scores_psum", NM), Q("max", NM), Q("neg_max"), Q("neg_max_parts", 5)
        q_mTp, q_mT, q_mrow = Q("neg_max_T_psum"), Q("neg_max_T"), Q("shift_rows", PARTS, 16)
        NX = NQ * NT * 2
        q_sp, q_p = Q("scores_psum", NX), Q("exp", NX)
        q_av, q_o = Q("values_summed", NQ * NT), Q("o", NQ)
        q_oTp, q_rd, q_y = Q("o_back_psum", NT), Q("sum_inverse", NT), Q("y", NT)
        q_yTp, q_yT, q_prp, q_x = Q("yT_psum"), Q("yT"), Q("projected_psum"), Q("x_updated")

        new_stage()
        qkv = scratch("qkv", [P, NT, D + 2 * L])
        kp = scratch("kp", [P, PARTS, NT, L], BF16)
        k_rest = scratch("k_rest", [P, NT, L])
        qp = scratch("qp", [P, PARTS, NT, D], BF16)
        q_rest = scratch("q_rest", [P, NT, D])
        vx = scratch("vx", [P, NT, 32])
        kx3 = scratch("kx3", [P, NT, PARTS, PARTS, L], BF16)
        qx3 = scratch("qx3", [P, NT * HEADS, PARTS, PARTS, L], BF16)
        kTm = scratch("kTm", [P, T], BF16)
        kTe = scratch("kTe", [P, T], BF16)
        qT = scratch("qT", [P, HEADS, T], BF16)
        mx = scratch("mx", [P, NT, HEADS])
        mp = scratch("mp", [P, NT, PARTS, HEADS], BF16)
        mT = scratch("mT", [PARTS * HEADS, T], BF16)
        pexp = scratch("pexp", [P, 4, 2, T])
        oT = scratch("oT", [P, NQ, T])
        rd = scratch("rd", [P, 2, HEADS])
        y2 = scratch("y2", [P, NT, D])
        y2T = scratch("y2T", [P, T])
        mask_qk = scratch("mask_qk", [P, P], BF16)
        mask_kq = scratch("mask_kq", [P, P], BF16)
        causal_qk, causal_kq, shift_rows = const("causal_qk"), const("causal_kq"), const("shift_rows")
        psM2, psE, psO = (bank[1], bank[2]), (wide, wide2), bank[7]
        psQT = (bank[0], bank[7])

        def mqa_dve(dve):
            nc.vector.tensor_copy(mask_qk[:, :], causal_qk)
            nc.vector.tensor_copy(mask_kq[:, :], causal_kq)
            nc.vector.memset(kTm[64:P, :], 0.0)
            nc.vector.memset(qT[64:P, :, :], 0.0)
            nc.vector.memset(vx[:, :, :], 0.0)
            nc.vector.tensor_copy(kTe[64:P, :], shift_rows[64:P, :].broadcast_to([64, T])).then_inc(q_init.sem, 1)
            dve.wait_ge(q_init.sem, q_init.total(1))
            nc.vector.memset(vx[:, :, L:L + 1], 1.0).then_inc(q_init.sem, 1)
            dve.wait_ge(q_init.sem, q_init.total(2))

            def split(sig, i, whole, rest, parts):
                nc.vector.tensor_copy(parts[0], whole).then_inc(sig.sem, 1)
                dve.wait_ge(sig.sem, sig.at(i, 1))
                nc.vector.tensor_tensor(rest, whole, parts[0], ALU.subtract).then_inc(sig.sem, 1)
                dve.wait_ge(sig.sem, sig.at(i, 2))
                nc.vector.tensor_copy(parts[1], rest).then_inc(sig.sem, 1)
                dve.wait_ge(sig.sem, sig.at(i, 3))
                nc.vector.tensor_tensor(rest, rest, parts[1], ALU.subtract).then_inc(sig.sem, 1)
                dve.wait_ge(sig.sem, sig.at(i, 4))
                nc.vector.tensor_copy(parts[2], rest).then_inc(sig.sem, 1)

            with nc.vector.Fori(0, B) as i:
                dve.wait_ge(q_xTp.sem, q_xTp.at(i, 0))
                normalise(q_xln, i)
                dve.wait_ge(q_qkv.sem, q_qkv.at(i, NT))
                dve.wait_ge(q_kx.sem, q_kx.at(i, 0))
                split(q_kpart, i, qkv[:, :, D:D + L], k_rest[:, :, :], [kp[:, n] for n in range(PARTS)])
                dve.wait_ge(q_qx.sem, q_qx.at(i, 0))
                split(q_qpart, i, qkv[:, :, 0:D], q_rest[:, :, :], [qp[:, n] for n in range(PARTS)])
                dve.wait_ge(q_av.sem, q_av.at(i, 0))
                nc.vector.tensor_copy(vx[:, :, 0:L], qkv[:, :, D + L:D + 2 * L]).then_inc(q_v.sem, 1)
                dve.wait_ge(q_kTp.sem, q_kTp.at(i, 1))
                nc.vector.tensor_copy(kTm[0:QR, :], bank[0][:, :].bitcast(BF16)[0:QR, 0:T]).then_inc(q_kTm.sem, 1)
                nc.vector.tensor_copy(kTe[0:QR, :], bank[0][:, :].bitcast(BF16)[0:QR, 0:T]).then_inc(q_kTe.sem, 1)
                for u in range(1, NU, 2):
                    dve.wait_ge(q_qTp.sem, q_qTp.at(i, u + 1))
                    nc.vector.tensor_copy(qT[0:QR, 2 * u:2 * u + 2, :].rearrange("p h t -> p (h t)"),
                                                    psQT[u % 2][:, :].bitcast(BF16)[0:QR, :]).then_inc(q_qTv.sem, 1)
                dve.wait_ge(q_neg.sem, q_neg.at(i, 0))
                for n, (k, h, nh) in enumerate(max_units):
                    dve.wait_ge(q_smp.sem, q_smp.at(i, n + 1))
                    w = P * (k + 1)
                    nc.vector.tensor_reduce(mx[:, k, h:h + nh],
                                                      psM2[n % 2][:, 0:nh * w].rearrange("p (h s) -> p h s", s=w),
                                                      AX.X, ALU.max).then_inc(q_mx.sem, 1)
                dve.wait_ge(q_mx.sem, q_mx.at(i, NM))
                dve.wait_ge(q_mTp.sem, q_mTp.at(i, 0))
                nc.vector.tensor_scalar(mx[:, :, :], mx[:, :, :], -1.0, None, ALU.mult).then_inc(q_neg.sem, 1)
                dve.wait_ge(q_neg.sem, q_neg.at(i, 1))
                split(q_mpart, i, mx[:, :, :], mx[:, :, :], [mp[:, :, n, :] for n in range(PARTS)])
                dve.wait_ge(q_mTp.sem, q_mTp.at(i, 1))
                dve.wait_ge(q_mrow.sem, q_mrow.at(i, 0))
                nc.vector.tensor_copy(mT[:, :], bank[0][:, :].bitcast(BF16)[0:PARTS * HEADS, 0:T]).then_inc(q_mT.sem, 1)
                for qd in range(NQ):
                    dve.wait_ge(q_av.sem, q_av.at(i, (qd + 1) * NT))
                    nc.vector.tensor_copy(oT[:, qd, :], psO[:, :]).then_inc(q_o.sem, 1)
                for k in range(NT):
                    dve.wait_ge(q_oTp.sem, q_oTp.at(i, k + 1))
                    ps = psM2[k % 2][:, :].rearrange("p (h c) -> p h c", c=32)
                    nc.vector.reciprocal(rd[:, k % 2, :], ps[:, :, L]).then_inc(q_rd.sem, 1)
                    dve.wait_ge(q_rd.sem, q_rd.at(i, k + 1))
                    nc.vector.tensor_tensor(y2[:, k, :].rearrange("p (h l) -> p h l", l=L), ps[:, :, 0:L],
                                                     rd[:, k % 2, :].unsqueeze(2).broadcast_to([P, HEADS, L]), ALU.mult).then_inc(q_y.sem, 1)
                dve.wait_ge(q_prp.sem, q_prp.at(i, 1))
                nc.vector.tensor_tensor(x_sb[:, i], x_sb[:, i],
                                                 bank[0][:, :].rearrange("p (k d) -> p k d", d=D), ALU.add).then_inc(q_x.sem, 1)
            dve.wait_ge(q_x.sem, q_x.at(B, 0))

        def mqa_pool(pool):
            with nc.gpsimd.Fori(0, B) as i:
                pool.wait_ge(q_kpart.sem, q_kpart.at(i, 5))
                pool.wait_ge(q_kTp.sem, q_kTp.at(i, 0))
                waits_end(pool)
                for n in range(PARTS):
                    nc.gpsimd.tensor_copy(kx3[:, :, :, n, :],
                                                    kp[:, n].unsqueeze(2).broadcast_to([P, NT, PARTS, L])).then_inc(q_kx.sem, 1)
                pool.wait_ge(q_qpart.sem, q_qpart.at(i, 5))
                pool.wait_ge(q_qTp.sem, q_qTp.at(i, 0))
                waits_end(pool)
                for n in range(PARTS):
                    nc.gpsimd.tensor_copy(
                        qx3[:, :, n, :, :], qp[:, n].rearrange("p k (h l) -> p (k h) l", l=L).unsqueeze(2)
                        .broadcast_to([P, NT * HEADS, PARTS, L])).then_inc(q_qx.sem, 1)

        def mqa_act(act):
            with nc.scalar.Fori(0, B) as i:
                act.wait_ge(q_xTp.sem, q_xTp.at(i, 1))
                act.wait_ge(q_qkvp.sem, q_qkvp.at(i, 0))
                nc.scalar.activation(xT[:, :], bank[0][:, :], ACT.Copy).then_inc(q_xT.sem, 1)
                act.wait_ge(q_kpart.sem, q_kpart.at(i, 0))
                act.wait_ge(q_v.sem, q_v.at(i, 0))
                for k in range(NT):
                    act.wait_ge(q_qkvp.sem, q_qkvp.at(i, k + 1))
                    nc.scalar.activation(qkv[:, k, :], psM2[k % 2][:, 0:D + 2 * L], ACT.Copy).then_inc(q_qkv.sem, 1)
                for u in range(0, NU, 2):
                    act.wait_ge(q_qTp.sem, q_qTp.at(i, u + 1))
                    nc.scalar.activation(qT[0:QR, 2 * u:2 * u + 2, :].rearrange("p h t -> p (h t)"),
                                                   psQT[u % 2][:, :].bitcast(BF16)[0:QR, :], ACT.Copy).then_inc(q_qTa.sem, 1)
                for n in range(NX):
                    w = T - P * (n // 2 % NT)
                    act.wait_ge(q_sp.sem, q_sp.at(i, n + 1))
                    act.wait_ge(q_av.sem, q_av.at(i, n // 2 - 1 if n >= 4 else 0))
                    nc.scalar.activation(pexp[:, n % 4, :, 0:w],
                                                  psE[n % 2][:, :].rearrange("p (h t) -> p h t", h=2)[:, :, 0:w],
                                                  ACT.Exp, scale=SCALE).then_inc(q_p.sem, 1)
                act.wait_ge(q_yTp.sem, q_yTp.at(i, 1))
                act.wait_ge(q_prp.sem, q_prp.at(i, 0))
                nc.scalar.activation(y2T[:, :], bank[7][:, :], ACT.Copy).then_inc(q_yT.sem, 1)

        def mqa_sync(sp):
            with nc.sync.Fori(0, B) as i:
                sp.wait_ge(q_mT.sem, q_mT.at(i, 1))
                for n in range(PARTS):
                    sp.dma_start(qT[QR + n:QR + n + 1, :, :], mT[n * HEADS:(n + 1) * HEADS, :]).then_inc(q_mrow.sem, 16)

        def mqa_pe(pe):
            def scores(i, step):
                qd, j = divmod(step, NT)
                w = T - P * j
                for half in range(2):
                    n = 2 * step + half
                    pe.wait_ge(q_p.sem, q_p.at(i, n - 1 if n >= 2 else 0))
                    for hh in range(2):
                        h = 4 * qd + 2 * half + hh
                        at = psE[half][:, hh * 512:hh * 512 + w]
                        nc.tensor.matmul(at, kTe[:, j * P:(j + 1) * P], qT[:, h, j * P:T], start=True, stop=False)
                        ins = nc.tensor.matmul(at[:, 0:P], ident_bf[:, :], mask_kq[:, :], start=False, stop=True)
                    ins.then_inc(q_sp.sem, 1)

            def values(i, step):
                qd, j = divmod(step, NT)
                w = T - P * j
                pe.wait_ge(q_p.sem, q_p.at(i, 2 * step + 2))
                if j == 0:
                    pe.wait_ge(q_o.sem, q_o.at(i, qd))
                for g in range(4):
                    ins = nc.tensor.matmul(psO[32 * g:32 * g + 32, j * P:T], vx[:, j, :],
                                           pexp[:, (2 * step + g // 2) % 4, g % 2, 0:w], start=j == 0, stop=j == NT - 1)
                ins.then_inc(q_av.sem, 1)

            pe.wait_ge(q_init.sem, q_init.total(2))
            with nc.tensor.Fori(0, B) as i:
                pe.wait_ge(q_xln.sem, q_xln.at(i, NT))
                pe.wait_ge(q_x.sem, q_x.at(i, 0))
                for k in range(NT):
                    ins = nc.tensor.transpose(bank[0][:, k * P:(k + 1) * P], xln[:, k, :], ident)
                ins.then_inc(q_xTp.sem, 1)
                pe.wait_ge(q_xT.sem, q_xT.at(i, 1))
                pe.wait_ge(q_y.sem, q_y.at(i, 0))
                for k in range(NT):
                    if k >= 2:
                        pe.wait_ge(q_qkv.sem, q_qkv.at(i, k - 1))
                    nc.tensor.matmul(psM2[k % 2][:, 0:D + 2 * L], xT[:, k * P:(k + 1) * P], wa_sb[:, :],
                                                 start=True, stop=True).then_inc(q_qkvp.sem, 1)
                pe.wait_ge(q_kx.sem, q_kx.at(i, 3))
                for k in range(NT):
                    ins = nc.tensor.transpose(bank[0][:, :].bitcast(BF16)[0:QR, k * P:(k + 1) * P],
                                              kx3[:, k].rearrange("p n j l -> p (n j l)"), ident_bf[:, :])
                ins.then_inc(q_kTp.sem, 1)
                pe.wait_ge(q_qx.sem, q_qx.at(i, 3))
                pe.wait_ge(q_kTe.sem, q_kTe.at(i, 1))
                pe.wait_ge(q_yT.sem, q_yT.at(i, 0))
                for u in range(NU):
                    if u >= 2:
                        pe.wait_ge((q_qTv if u % 2 else q_qTa).sem, (q_qTv if u % 2 else q_qTa).at(i, u // 2))
                    for hh in range(2):
                        for k in range(NT):
                            ins = nc.tensor.transpose(
                                psQT[u % 2][:, :].bitcast(BF16)[0:QR, (hh * NT + k) * P:(hh * NT + k + 1) * P],
                                qx3[:, k * HEADS + 2 * u + hh].rearrange("p n j l -> p (n j l)"), ident_bf[:, :])
                    ins.then_inc(q_qTp.sem, 1)
                pe.wait_ge(q_qTa.sem, q_qTa.at(i, NU // 2))
                pe.wait_ge(q_qTv.sem, q_qTv.at(i, NU // 2))
                pe.wait_ge(q_qkv.sem, q_qkv.at(i, NT))
                for n, (k, h, nh) in enumerate(max_units):
                    if n >= 2:
                        pe.wait_ge(q_mx.sem, q_mx.at(i, n - 1))
                    w = P * (k + 1)
                    for hh in range(nh):
                        at = psM2[n % 2][:, hh * w:(hh + 1) * w]
                        nc.tensor.matmul(at, qT[:, h + hh, k * P:(k + 1) * P], kTm[:, 0:w], start=True, stop=False)
                        ins = nc.tensor.matmul(at[:, w - P:w], ident_bf[:, :], mask_qk[:, :], start=False, stop=True)
                    ins.then_inc(q_smp.sem, 1)
                pe.wait_ge(q_mpart.sem, q_mpart.at(i, 5))
                waits_end(pe)
                for k in range(NT):
                    ins = nc.tensor.transpose(bank[0][:, :].bitcast(BF16)[0:PARTS * HEADS, k * P:(k + 1) * P],
                                              mp[:, k].rearrange("p n h -> p (n h)"), ident_bf[:, :])
                ins.then_inc(q_mTp.sem, 1)
                pe.wait_ge(q_mrow.sem, q_mrow.at(i, PARTS))
                pe.wait_ge(q_v.sem, q_v.at(i, 1))
                scores(i, 0)
                for step in range(NQ * NT):
                    if step + 1 < NQ * NT:
                        scores(i, step + 1)
                    values(i, step)
                pe.wait_ge(q_o.sem, q_o.at(i, NQ))
                for k in range(NT):
                    if k >= 2:
                        pe.wait_ge(q_y.sem, q_y.at(i, k - 1))
                    for qd in range(NQ):
                        ins = nc.tensor.transpose(psM2[k % 2][:, qd * P:(qd + 1) * P], oT[:, qd, k * P:(k + 1) * P], ident)
                    ins.then_inc(q_oTp.sem, 1)
                pe.wait_ge(q_y.sem, q_y.at(i, NT))
                for k in range(NT):
                    ins = nc.tensor.transpose(bank[7][:, k * P:(k + 1) * P], y2[:, k, :], ident)
                ins.then_inc(q_yTp.sem, 1)
                pe.wait_ge(q_yT.sem, q_yT.at(i, 1))
                for k in range(NT):
                    ins = nc.tensor.matmul(bank[0][:, k * D:(k + 1) * D], y2T[:, k * P:(k + 1) * P], wp_sb[:, :],
                                           start=True, stop=True)
                ins.then_inc(q_prp.sem, 1)

        F = lambda name, per=1, step=1: signal("filter_" + name, per, step)
        f_xln, f_xTp, f_xT, f_yp, f_b, f_x, f_out = (F("xln", NT), F("xT_psum"), F("xT"), F("y_psum"), F("biased"),
                                                     F("x_updated"), F("stored", 1, 16))
        new_stage()
        fy = scratch("fy", [P, NT, D])

        def filter_dve(dve):
            with nc.vector.Fori(0, B) as i:
                dve.wait_ge(f_xTp.sem, f_xTp.at(i, 0))
                normalise(f_xln, i)
                dve.wait_ge(f_x.sem, f_x.at(i, 0))
                dve.wait_ge(f_yp.sem, f_yp.at(i, 1))
                nc.vector.tensor_tensor(fy[:, :, :], bank[1][:, :].rearrange("p (k d) -> p k d", d=D),
                                                 fb_sb[:, :].unsqueeze(1).broadcast_to([P, NT, D]), ALU.add).then_inc(f_b.sem, 1)
                dve.wait_ge(f_b.sem, f_b.at(i, 1))
                nc.vector.tensor_tensor(x_sb[:, i], x_sb[:, i], fy[:, :, :], ALU.add).then_inc(f_x.sem, 1)

        def filter_act(act):
            with nc.scalar.Fori(0, B) as i:
                act.wait_ge(f_xTp.sem, f_xTp.at(i, 1))
                act.wait_ge(f_yp.sem, f_yp.at(i, 0))
                nc.scalar.activation(xT[:, :], bank[0][:, :], ACT.Copy).then_inc(f_xT.sem, 1)

        def filter_pe(pe):
            with nc.tensor.Fori(0, B) as i:
                pe.wait_ge(f_xln.sem, f_xln.at(i, NT))
                pe.wait_ge(f_xT.sem, f_xT.at(i, 0))
                for k in range(NT):
                    ins = nc.tensor.transpose(bank[0][:, k * P:(k + 1) * P], xln[:, k, :], ident)
                ins.then_inc(f_xTp.sem, 1)
                pe.wait_ge(f_xT.sem, f_xT.at(i, 1))
                pe.wait_ge(f_b.sem, f_b.at(i, 0))
                for k in range(NT):
                    ins = nc.tensor.matmul(bank[1][:, k * D:(k + 1) * D], xT[:, k * P:(k + 1) * P], m_sb[:, :],
                                           start=True, stop=True)
                ins.then_inc(f_yp.sem, 1)

        def filter_sync(sp):
            with nc.sync.Fori(0, B) as i:
                sp.wait_ge(f_x.sem, f_x.at(i, 1))
                sp.dma_start(out[i].rearrange("(k p) d -> p k d", p=P), x_sb[:, i]).then_inc(f_out.sem, 16)
            sp.wait_ge(f_out.sem, f_out.total(16 * B))

        block = ctx.enter_context(nc.Block())

        @block.sync
        def _(sp):
            prep_sync(sp)
            start_signals(sp)
            route_sync(sp)
            moe_sync(sp)
            mqa_sync(sp)
            filter_sync(sp)

        @block.scalar
        def _(act):
            prep_act(act)
            ln1_act(act)
            lin_act(act)
            ln2_act(act)
            route_act(act)
            moe_act(act)
            ln3_act(act)
            mqa_act(act)
            ln4_act(act)
            filter_act(act)

        @block.tensor
        def _(pe):
            prep_pe(pe)
            lin_pe(pe)
            route_pe(pe)
            moe_pe(pe)
            mqa_pe(pe)
            filter_pe(pe)

        @block.vector
        def _(dve):
            prep_dve(dve)
            dve.wait_ge(s_x.sem, s_x.total(16 * B))
            ln1_dve(dve)
            lin_dve(dve)
            ln2_dve(dve)
            route_dve(dve)
            moe_dve(dve)
            ln3_dve(dve)
            mqa_dve(dve)
            ln4_dve(dve)
            filter_dve(dve)

        @block.gpsimd
        def _(pool):
            lin_pool(pool)
            moe_pool(pool)
            mqa_pool(pool)


def constants():
    import numpy as np
    n = np.arange(P)
    angle = 2.0 * np.pi * ((n[:, None] * n[None, :]) % P) / P
    head = n // 8
    parts = {
        "ident": np.eye(P),
        "tri": n[:, None] <= n[None, :],
        "ones": np.ones((P, P)),
        "dft_c": np.cos(angle),
        "dft_s": np.sin(angle),
        "dft_ns": -np.sin(angle),
        "blockdiag": head[:, None] == head[None, :],
        "causal_qk": np.where(n[:, None] < n[None, :], NEG, 0.0),
        "causal_kq": np.where(n[:, None] > n[None, :], NEG, 0.0),
        "slots": np.broadcast_to(np.arange(P + 1)[None, :], (P, P + 1)),
        "slot_row": n[:, None],
        "seqmask": ((n[:, None] % 64) // 8) == np.arange(8)[None, :],
        "shift_rows": ((n >= 72) & (n < 75))[:, None],
    }
    layout, at = {}, 0
    for name, a in parts.items():
        layout[name] = (at, a.shape[1])
        at += a.shape[1]
    layout["width"] = at
    return layout, np.concatenate([np.asarray(a, np.float32) for a in parts.values()], axis=1)


_INS = ["L0_attn_x", "L0_attn_w", "L0_attn_w_out", "L0_ffn_router_w", "L0_ffn_w1", "L0_ffn_b1", "L0_ffn_w2",
        "L0_ffn_b2", "L1_attn_w_attn", "L1_attn_w_proj", "L1_ffn_w_freq_real", "L1_ffn_w_freq_imag",
        "L1_ffn_bias"]


def kernel(**inputs):
    import numpy as np
    import concourse.bacc as bacc
    from concourse.bass_utils import run_bass_kernel_spmd

    nc = bacc.Bacc("TRN2", target_bir_lowering=False, num_devices=1)
    layout, table = constants()
    arrays, args = {}, []
    for name in _INS:
        arrays[f"in_{name}"] = np.ascontiguousarray(inputs[name])
    arrays["constants"] = table
    for name, a in arrays.items():
        args.append(nc.dram_tensor(name, a.shape, mybir.dt.from_np(a.dtype), kind="ExternalInput").ap())
    x = arrays["in_L0_attn_x"]
    out = nc.dram_tensor("out_x", x.shape, F32, kind="ExternalOutput").ap()
    build(nc, *args, out, layout)
    return run_bass_kernel_spmd(nc, [arrays], core_ids=[0]).results[0]["out_x"]
```

```python
from contextlib import ExitStack

import concourse.bass as bass
from concourse import mybir

F32 = mybir.dt.float32
BF16 = mybir.dt.bfloat16
ALU = mybir.AluOpType
ACT = mybir.ActivationFunctionType
AX = mybir.AxisListType

P = 128
HEADS = 16
EPS = 1e-5
NEG = -1.0e30
PARTS = 3


class Signal:

    START = 1

    def __init__(self, sem, per, step=1):
        self.sem, self.per, self.step = sem, per, step

    def at(self, turn, nth):
        return turn * (self.per * self.step) + (nth * self.step + self.START)

    def total(self, raised):
        return raised + self.START


def build(nc, x_in, w_qkv, w_out, router_w, w1, b1, w2, b2, w_attn, w_proj, wf_re, wf_im, f_bias,
          consts, out, layout):
    B, T, D = x_in.shape
    E, _, H = w1.shape
    NT = T // P
    L = D // HEADS
    CAP = max(1, int(T * 2.0 / E) + 1)
    HC = H // P
    SCALE = float(L) ** -0.5
    BE = B * E
    GC = 344
    assert CAP == P + 1 and D == P and E * CAP == 3 * GC and BE == 64
    QR = PARTS * PARTS * L
    NQ = HEADS // 4

    with ExitStack() as ctx:
        def sb(name, shape, dt=F32):
            return ctx.enter_context(nc.sbuf_tensor(name, shape, dt))

        made = []

        def signal(name, per=1, step=1):
            made.append(Signal(ctx.enter_context(nc.semaphore(name)), per, step))
            return made[-1]

        def psum(name, banks):
            return ctx.enter_context(nc.psum_tensor(name, [P, 512 * banks], F32))

        bank = {i: psum(f"bank{i}", 1) for i in (0, 1, 2, 7)}
        wide, wide2 = psum("wide", 2), psum("wide2", 2)
        bank[5], bank[6] = wide2[:, 0:512], wide2[:, 512:1024]

        x_sb = sb("x_sb", [P, B, NT, D])
        cst = sb("cst", [P, layout["width"]])

        def const(name):
            a, n = layout[name]
            return cst[:, a:a + n]

        ident, tri, ones = const("ident"), const("tri"), const("ones")
        dft_c, dft_s, dft_ns = const("dft_c"), const("dft_s"), const("dft_ns")
        blockdiag, seqmask = const("blockdiag"), const("seqmask")
        wq_raw = sb("wq_raw", [P, 3, D])
        wqT = sb("wqT", [P, 3 * D])
        wo_sb = sb("wo_sb", [P, D])
        r_raw = sb("r_raw", [E, D])
        rT = sb("rT", [P, E])
        w1_sb = sb("w1_sb", [P, E, H])
        w2_sb = sb("w2_sb", [P, E, HC, D])
        b1_raw = sb("b1_raw", [E * HC, P])
        b1T = sb("b1T", [P, E * HC])
        b2rep = sb("b2rep", [P, D])
        wa_sb = sb("wa_sb", [P, D + 2 * L])
        wp_sb = sb("wp_sb", [P, D])
        wf_sb = sb("wf_sb", [P, 2, D])
        fb_sb = sb("fb_sb", [P, D])
        a12 = sb("a12", [P, 2, D])
        m_sb = sb("m_sb", [P, D])
        ident_bf = sb("ident_bf", [P, P], BF16)

        sc_part = sb("sc_part", [P, NT, B, E, PARTS], BF16)
        posT = sb("posT", [P, NT, B, E])
        rest_l = sb("rest_l", [P, T])

        st6 = sb("st6", [P, NT, 6])
        mvt = sb("mvt", [P, NT, 2])
        mv = sb("mv", [P, B, NT, 2])
        sd = sb("sd", [P, B, NT])
        rstd = sb("rstd", [P, B, NT])
        xln = sb("xln", [P, NT, D])
        xT = sb("xT", [P, T])

        passed = signal("waits_passed")

        def waits_end(engine):
            engine.sem_inc(passed.sem, 1)

        stage = [ExitStack()]

        def new_stage():
            stage[0].close()
            stage[0] = ctx.enter_context(ExitStack())

        def scratch(name, shape, dt=F32):
            return stage[0].enter_context(nc.sbuf_tensor(name, shape, dt))

        s_x = signal("x_loaded", 1, 16)
        s_w = signal("weights_loaded", 1, 16)
        s_c = signal("consts_loaded", 1, 16)

        NW = 11
        s_prep_t = signal("prep_transposed")
        s_prep_v = signal("prep_evacuated")
        s_idb = signal("ident_bf_ready")

        def start_signals(sp):
            for s in made:
                sp.sem_inc(s.sem, Signal.START)

        def prep_sync(sp):
            sp.dma_start(cst[:, :], consts).then_inc(s_c.sem, 16)
            for b in range(B):
                sp.dma_start(x_sb[:, b], x_in[b].rearrange("(k p) d -> p k d", p=P)).then_inc(s_x.sem, 16)

        def prep_act(q):
            for dst, src in (
                (wq_raw[:, :, :], w_qkv.rearrange("(g p) d -> p g d", p=P)),
                (wo_sb[:, :], w_out),
                (r_raw[:, :], router_w),
                (b1_raw[:, :], b1.rearrange("e (c p) -> (e c) p", p=P)),
                (wf_sb[:, 0, :], wf_re),
                (wf_sb[:, 1, :], wf_im),
                (wa_sb[:, :], w_attn),
                (wp_sb[:, :], w_proj),
                (fb_sb[:, :], f_bias.rearrange("(a d) -> a d", a=1).broadcast_to([P, D])),
                (w1_sb[:, :, :], w1.rearrange("e d h -> d e h")),
                (w2_sb[:, :, :, :].rearrange("p e c d -> p (e c) d"),
                 w2.rearrange("e (c p) d -> p (e c) d", p=P)),
            ):
                q.dma_start(dst, src).then_inc(s_w.sem, 16)
            for b in range(B):
                q.dma_start(b2rep[BE + b * E:BE + (b + 1) * E, :], b2).then_inc(s_w.sem, 16)

        def prep_pe(pe):
            pe.wait_ge(s_c.sem, s_c.total(16))
            pe.wait_ge(s_w.sem, s_w.total(16 * (NW + B)))
            for g in range(3):
                nc.tensor.transpose(bank[0][:, g * D:(g + 1) * D], wq_raw[:, g, :], ident)
            nc.tensor.transpose(bank[1][:, 0:E], r_raw[:, :], ident[0:E, 0:E])
            nc.tensor.transpose(bank[1][:, 64:64 + E * HC], b1_raw[:, :], ident[0:E * HC, 0:E * HC])
            re, im = wf_sb[:, 0, :], wf_sb[:, 1, :]
            nc.tensor.matmul(bank[2][:, 0:D], re, dft_c, start=True, stop=False)
            nc.tensor.matmul(bank[2][:, 0:D], im, dft_s, start=False, stop=True)
            nc.tensor.matmul(bank[2][:, D:2 * D], im, dft_c, start=True, stop=False)
            nc.tensor.matmul(bank[2][:, D:2 * D], re, dft_ns, start=False, stop=True).then_inc(s_prep_t.sem, 1)
            pe.wait_ge(s_prep_v.sem, s_prep_v.total(4))
            nc.tensor.matmul(bank[5][:, 0:D], a12[:, 0, :], dft_c, start=True, stop=False)
            nc.tensor.matmul(bank[5][:, 0:D], a12[:, 1, :], dft_ns, start=False, stop=True).then_inc(s_prep_t.sem, 1)

        def prep_dve(dve):
            dve.wait_ge(s_c.sem, s_c.total(16))
            nc.vector.tensor_copy(ident_bf[:, :], ident).then_inc(s_idb.sem, 1)
            dve.wait_ge(s_prep_t.sem, s_prep_t.total(1))
            nc.vector.tensor_copy(wqT[:, :], bank[0][:, 0:3 * D]).then_inc(s_prep_v.sem, 1)
            nc.vector.tensor_copy(rT[:, :], bank[1][:, 0:E]).then_inc(s_prep_v.sem, 1)
            nc.vector.tensor_copy(b1T[:, :], bank[1][:, 64:64 + E * HC]).then_inc(s_prep_v.sem, 1)
            nc.vector.tensor_copy(a12[:, :, :].rearrange("p a d -> p (a d)"),
                                  bank[2][:, 0:2 * D]).then_inc(s_prep_v.sem, 1)
            dve.wait_ge(s_prep_t.sem, s_prep_t.total(2))
            nc.vector.tensor_scalar(m_sb[:, :], bank[5][:, 0:D], 1.0 / D, None, ALU.mult).then_inc(s_prep_v.sem, 1)

        class LayerNorm:

            def __init__(self, tag):
                self.six = signal(f"{tag}_bn_stats")
                self.agg = signal(f"{tag}_bn_aggr")
                self.mv = signal(f"{tag}_mean_var")
                self.ve = signal(f"{tag}_var_eps")
                self.sd = signal(f"{tag}_std")
                self.rstd = signal(f"{tag}_rstd")

            def dve_sequence(self, dve, i):
                dve.wait_ge(self.agg.sem, self.agg.at(i, 0))
                waits_end(dve)
                for k in range(NT):
                    ins = nc.vector.bn_stats(st6[:, k, :], x_sb[:, i, k, :])
                ins.then_inc(self.six.sem, 1)
                dve.wait_ge(self.six.sem, self.six.at(i, 1))
                dve.wait_ge(self.mv.sem, self.mv.at(i, 0))
                waits_end(dve)
                for k in range(NT):
                    ins = nc.vector.bn_aggr(mvt[:, k, :], st6[:, k, :])
                ins.then_inc(self.agg.sem, 1)
                dve.wait_ge(self.agg.sem, self.agg.at(i, 1))
                nc.vector.tensor_copy(mv[:, i, :, :], mvt[:, :, :]).then_inc(self.mv.sem, 1)

            def dve_rstd(self, dve):
                dve.wait_ge(self.mv.sem, self.mv.total(B))
                nc.vector.tensor_scalar(sd[:, :, :], mv[:, :, :, 1], EPS, None, ALU.add).then_inc(self.ve.sem, 1)
                dve.wait_ge(self.sd.sem, self.sd.total(1))
                nc.vector.reciprocal(rstd[:, :, :], sd[:, :, :]).then_inc(self.rstd.sem, 1)
                dve.wait_ge(self.rstd.sem, self.rstd.total(1))

            def act_std(self, act):
                act.wait_ge(self.ve.sem, self.ve.total(1))
                nc.scalar.activation(sd[:, :, :], sd[:, :, :], ACT.Sqrt).then_inc(self.sd.sem, 1)

        def normalise(s_xln, i):
            for k in range(NT):
                nc.vector.tensor_scalar(xln[:, k, :], x_sb[:, i, k, :], mv[:, i, k, 0:1],
                                                   rstd[:, i, k:k + 1], ALU.subtract, ALU.mult).then_inc(s_xln.sem, 1)

        ln1, ln2, ln3, ln4 = (LayerNorm(f"ln{n}") for n in range(1, 5))

        A = lambda name, per=1: signal("lin_" + name, per)
        a_xln, a_xTp, a_xT = A("xln", NT), A("xT_psum"), A("xT")
        a_qkv, a_qv, a_kx, a_kxe = A("qkv_psum", NT), A("qv", NT), A("exp_k", NT), A("exp_k_eps")
        a_qmax, a_qc, a_qe, a_qsum = A("q_max"), A("q_shifted"), A("q_exp"), A("q_sum")
        a_kn, a_den, a_rden, a_qs = A("k_norm_psum"), A("denominator"), A("denominator_inverse"), A("q_soft")
        a_kv, a_cum, a_prod, a_red = A("outer", NT), A("outer_sums_psum", NT), A("q_times_sums", NT), A("y_intra", NT)
        a_stp, a_st = A("state_psum"), A("state")
        a_qsTp, a_qsT, a_yTp, a_yT = A("q_soft_T_psum"), A("q_soft_T"), A("yT_psum"), A("yT")
        a_o, a_x = A("projected_psum"), A("x_updated")

        new_stage()
        qv = scratch("qv", [P, 2, 2, NT, D])
        kx = scratch("kx", [P, 2, NT, D])
        qmax = scratch("qmax", [P, NT * HEADS])
        q_sh = scratch("q_sh", [P, NT, D])
        qe = scratch("qe", [P, NT, D])
        qsum = scratch("qsum", [P, NT * HEADS])
        den = scratch("den", [P, NT, D])
        qs = scratch("qs", [P, NT, D])
        kv = scratch("kv", [P, 2, HEADS * L * L])
        prod = scratch("prod", [P, 2, HEADS * L * L])
        state = scratch("state", [P, NT - 1, D])
        tT = scratch("tT", [P, T])
        yT = scratch("yT", [P, T])
        y_in = scratch("y_in", [P, NT, D])
        by_head = lambda ap: ap.rearrange("p k (h l) -> p (k h) l", l=L)
        psT, psN, psS, psY = bank[0], bank[5], bank[6], bank[7]
        psQ = (bank[1], bank[2])


        def dve_lin_qmax(dve, b, par):
            dve.wait_ge(a_qv.sem, a_qv.at(b, NT))
            dve.wait_ge(a_qc.sem, a_qc.at(b, 0))
            nc.vector.tensor_reduce(qmax[:, :], by_head(qv[:, par, 0, :, :]), AX.X, ALU.max).then_inc(a_qmax.sem, 1)

        def dve_lin_qsum(dve, b):
            dve.wait_ge(a_qe.sem, a_qe.at(b, 1))
            dve.wait_ge(a_den.sem, a_den.at(b, 0))
            nc.vector.tensor_reduce(qsum[:, :], by_head(qe[:, :, :]), AX.X, ALU.add).then_inc(a_qsum.sem, 1)

        def dve_lin_den(dve, b):
            dve.wait_ge(a_kn.sem, a_kn.at(b, 1))
            dve.wait_ge(a_qsum.sem, a_qsum.at(b, 1))
            dve.wait_ge(a_qs.sem, a_qs.at(b, 0))
            nc.vector.tensor_tensor(by_head(den[:, :, :]), psN[:, :].rearrange("p (kh l) -> p kh l", l=L),
                                    qsum[:, :].unsqueeze(2).broadcast_to([P, NT * HEADS, L]),
                                    ALU.mult).then_inc(a_den.sem, 1)
            dve.wait_ge(a_den.sem, a_den.at(b, 1))
            nc.vector.reciprocal(den[:, :, :], den[:, :, :]).then_inc(a_rden.sem, 1)

        def dve_lin_xln(dve, b):
            dve.wait_ge(a_xTp.sem, a_xTp.at(b, 0))
            normalise(a_xln, b)

        def dve_lin_prod(dve, b, k):
            dve.wait_ge(a_cum.sem, a_cum.at(b, k + 1))
            dve.wait_ge(a_qs.sem, a_qs.at(b, 1))
            dve.wait_ge(a_red.sem, a_red.at(b, k - 1 if k >= 2 else 0))
            nc.vector.tensor_tensor(
                prod[:, k % 2, :].rearrange("p (hl m) -> p hl m", m=L),
                wide[:, :].rearrange("p (hl m) -> p hl m", m=L),
                qs[:, k, :].unsqueeze(2).broadcast_to([P, D, L]), ALU.mult).then_inc(a_prod.sem, 1)

        def dve_lin_reduce(dve, b, k):
            dve.wait_ge(a_prod.sem, a_prod.at(b, k + 1))
            if k == 0:
                dve.wait_ge(a_yTp.sem, a_yTp.at(b, 0))
            nc.vector.tensor_reduce(
                y_in[:, k, :].rearrange("p (h m) -> p h m", m=L),
                prod[:, k % 2, :].rearrange("p (h l m) -> p h m l", l=L, m=L), AX.X, ALU.add).then_inc(a_red.sem, 1)

        def dve_lin_state(dve, b):
            dve.wait_ge(a_stp.sem, a_stp.at(b, 1))
            dve.wait_ge(a_yTp.sem, a_yTp.at(b, 0))
            nc.vector.tensor_tensor(state[:, :, :], psS[:, 0:(NT - 1) * D].rearrange("p (k d) -> p k d", d=D),
                                    blockdiag.unsqueeze(1).broadcast_to([P, NT - 1, D]), ALU.mult).then_inc(a_st.sem, 1)

        def dve_lin_residual(dve, b):
            dve.wait_ge(a_o.sem, a_o.at(b, 1))
            nc.vector.tensor_tensor(x_sb[:, b, :, :], x_sb[:, b, :, :],
                                    psN[:, :].rearrange("p (k d) -> p k d", d=D), ALU.add).then_inc(a_x.sem, 1)

        def dve_lin_stats(dve, b):
            dve.wait_ge(a_x.sem, a_x.at(b, 1))
            ln2.dve_sequence(dve, b)

        def dve_lin_turn(dve, b, par, tail=True, front=True, ahead=True):
            dve_lin_prod(dve, b, 0)
            dve_lin_reduce(dve, b, 0)
            if tail:
                dve_lin_residual(dve, b - 1)
            dve_lin_prod(dve, b, 1)
            dve_lin_reduce(dve, b, 1)
            if tail:
                dve_lin_stats(dve, b - 1)
            dve_lin_prod(dve, b, 2)
            dve_lin_state(dve, b)
            if front:
                dve_lin_qmax(dve, b + 1, 1 - par)
            dve_lin_reduce(dve, b, 2)
            if ahead:
                dve_lin_xln(dve, b + 2)
            dve_lin_prod(dve, b, 3)
            dve_lin_reduce(dve, b, 3)
            if front:
                dve_lin_qsum(dve, b + 1)
                dve_lin_den(dve, b + 1)

        def lin_dve(dve):
            dve_lin_xln(dve, 0)
            dve_lin_qmax(dve, 0, 0)
            dve_lin_xln(dve, 1)
            dve_lin_qsum(dve, 0)
            dve_lin_den(dve, 0)
            dve_lin_turn(dve, 0, 0, tail=False)
            dve_lin_turn(dve, 1, 1)
            with nc.vector.Fori(1, B // 2 - 1) as i:
                dve_lin_turn(dve, 2 * i, 0)
                dve_lin_turn(dve, 2 * i + 1, 1)
            dve_lin_turn(dve, B - 2, 0, ahead=False)
            dve_lin_turn(dve, B - 1, 1, front=False, ahead=False)
            dve_lin_residual(dve, B - 1)
            dve_lin_stats(dve, B - 1)
            dve.wait_ge(a_x.sem, a_x.total(B))

        def act_lin_xT(act, b):
            act.wait_ge(a_xTp.sem, a_xTp.at(b, 1))
            act.wait_ge(a_qkv.sem, a_qkv.at(b, 0))
            nc.scalar.activation(xT[:, :], psT[:, :], ACT.Copy).then_inc(a_xT.sem, 1)

        def act_lin_kx_qv(act, b, par, k, first=False):
            act.wait_ge(a_qkv.sem, a_qkv.at(b, k + 1))
            if k == 0 and not first:
                act.wait_ge(a_kv.sem, a_kv.at(b - 1, 0))
                act.wait_ge(a_stp.sem, a_stp.at(b - 1, 0))
                act.wait_ge(a_kn.sem, a_kn.at(b - 1, 0))
                act.wait_ge(a_qc.sem, a_qc.at(b - 1, 0))
            psq = psQ[k % 2][:, 0:3 * D].rearrange("p (g d) -> p g d", g=3)
            nc.scalar.activation(kx[:, par, k, :], psq[:, 1, :], ACT.Exp, scale=SCALE).then_inc(a_kx.sem, 1)
            nc.scalar.activation(qv[:, par, :, k, :], psq[:, 0:3:2, :], ACT.Copy).then_inc(a_qv.sem, 1)

        def act_lin_qe(act, b):
            act.wait_ge(a_qc.sem, a_qc.at(b, 1))
            act.wait_ge(a_qs.sem, a_qs.at(b, 0))
            nc.scalar.activation(qe[:, :, :], q_sh[:, :, :], ACT.Exp, scale=SCALE).then_inc(a_qe.sem, 1)

        def act_lin_qsT(act, b):
            act.wait_ge(a_qsTp.sem, a_qsTp.at(b, 1))
            act.wait_ge(a_yTp.sem, a_yTp.at(b, 0))
            nc.scalar.activation(tT[:, 0:(NT - 1) * P], psT[:, 0:(NT - 1) * P], ACT.Copy).then_inc(a_qsT.sem, 1)

        def act_lin_yT(act, b):
            act.wait_ge(a_yTp.sem, a_yTp.at(b, 1))
            act.wait_ge(a_o.sem, a_o.at(b, 0))
            nc.scalar.activation(yT[:, :], psY[:, :], ACT.Copy).then_inc(a_yT.sem, 1)

        def act_lin_turn(act, b, par, tail=True, front=True):
            if front:
                act_lin_xT(act, b + 1)
            if tail:
                act_lin_yT(act, b - 1)
            if front:
                for k in range(NT):
                    act_lin_kx_qv(act, b + 1, 1 - par, k)
            act_lin_qsT(act, b)
            if front:
                act_lin_qe(act, b + 1)

        def lin_act(act):
            act_lin_xT(act, 0)
            for k in range(NT):
                act_lin_kx_qv(act, 0, 0, k, first=True)
            act_lin_qe(act, 0)
            act_lin_turn(act, 0, 0, tail=False)
            act_lin_turn(act, 1, 1)
            with nc.scalar.Fori(1, B // 2 - 1) as i:
                act_lin_turn(act, 2 * i, 0)
                act_lin_turn(act, 2 * i + 1, 1)
            act_lin_turn(act, B - 2, 0)
            act_lin_turn(act, B - 1, 1, front=False)
            act_lin_yT(act, B - 1)

        def pool_lin_keys(pool, b, par):
            pool.wait_ge(a_kx.sem, a_kx.at(b, NT))
            waits_end(pool)
            nc.gpsimd.tensor_scalar(kx[:, par], kx[:, par], 1e-6, None, ALU.add).then_inc(a_kxe.sem, 1)

        def pool_lin_shift(pool, b, par):
            pool.wait_ge(a_qmax.sem, a_qmax.at(b, 1))
            pool.wait_ge(a_qv.sem, a_qv.at(b, NT))
            pool.wait_ge(a_qe.sem, a_qe.at(b, 0))
            nc.gpsimd.tensor_tensor(by_head(q_sh[:, :, :]), by_head(qv[:, par, 0, :, :]),
                                    qmax[:, :].unsqueeze(2).broadcast_to([P, NT * HEADS, L]),
                                    ALU.subtract).then_inc(a_qc.sem, 1)

        def pool_lin_qs(pool, b):
            pool.wait_ge(a_rden.sem, a_rden.at(b, 1))
            pool.wait_ge(a_prod.sem, a_prod.at(b, 0))
            pool.wait_ge(a_qsTp.sem, a_qsTp.at(b, 0))
            nc.gpsimd.tensor_tensor(qs[:, :, :], qe[:, :, :], den[:, :, :], ALU.mult).then_inc(a_qs.sem, 1)

        def pool_lin_outer(pool, b, par, k, first=False):
            pool.wait_ge(a_kxe.sem, a_kxe.at(b, 1))
            pool.wait_ge(a_qv.sem, a_qv.at(b, NT))
            if k >= 2:
                pool.wait_ge(a_cum.sem, a_cum.at(b, k - 1))
            elif not first:
                pool.wait_ge(a_cum.sem, a_cum.at(b - 1, NT + k - 1))
            shape = [P, HEADS, L, L]
            nc.gpsimd.tensor_tensor(
                kv[:, k % 2, :].rearrange("p (h l m) -> p h l m", l=L, m=L),
                kx[:, par, k, :].rearrange("p (h l) -> p h l", l=L).unsqueeze(3).broadcast_to(shape),
                qv[:, par, 1, k, :].rearrange("p (h m) -> p h m", m=L).unsqueeze(2).broadcast_to(shape),
                ALU.mult).then_inc(a_kv.sem, 1)

        def pool_lin_turn(pool, b, par, front=True):
            pool_lin_qs(pool, b)
            pool_lin_outer(pool, b, par, 2)
            pool_lin_outer(pool, b, par, 3)
            if front:
                pool_lin_keys(pool, b + 1, 1 - par)
                pool_lin_shift(pool, b + 1, 1 - par)
                pool_lin_outer(pool, b + 1, 1 - par, 0)
                pool_lin_outer(pool, b + 1, 1 - par, 1)

        def lin_pool(pool):
            pool_lin_keys(pool, 0, 0)
            pool_lin_shift(pool, 0, 0)
            pool_lin_outer(pool, 0, 0, 0, first=True)
            pool_lin_outer(pool, 0, 0, 1, first=True)
            with nc.gpsimd.Fori(0, B // 2 - 1) as i:
                pool_lin_turn(pool, 2 * i, 0)
                pool_lin_turn(pool, 2 * i + 1, 1)
            pool_lin_turn(pool, B - 2, 0)
            pool_lin_turn(pool, B - 1, 1, front=False)

        def pe_lin_xT(pe, b, first=False):
            pe.wait_ge(a_xln.sem, a_xln.at(b, NT))
            if not first:
                pe.wait_ge(a_qsT.sem, a_qsT.at(b - 1, 0))
            for k in range(NT):
                ins = nc.tensor.transpose(psT[:, k * P:(k + 1) * P], xln[:, k, :], ident)
            ins.then_inc(a_xTp.sem, 1)

        def pe_lin_qkv(pe, b, k):
            pe.wait_ge(a_xT.sem, a_xT.at(b, 1))
            if k >= 2:
                pe.wait_ge(a_qv.sem, a_qv.at(b, k - 1))
            else:
                pe.wait_ge(a_qv.sem, a_qv.at(b, 0))
            nc.tensor.matmul(psQ[k % 2][:, 0:3 * D], xT[:, k * P:(k + 1) * P], wqT[:, :],
                             start=True, stop=True).then_inc(a_qkv.sem, 1)

        def pe_lin_key_sums(pe, b, par, first=False):
            pe.wait_ge(a_kxe.sem, a_kxe.at(b, 1))
            if not first:
                pe.wait_ge(a_x.sem, a_x.at(b - 1, 0))
            for k in range(NT):
                for j in range(k):
                    nc.tensor.matmul(psN[:, k * D:(k + 1) * D], ones, kx[:, par, j, :], start=j == 0, stop=False)
                ins = nc.tensor.matmul(psN[:, k * D:(k + 1) * D], tri, kx[:, par, k, :], start=k == 0, stop=True)
            ins.then_inc(a_kn.sem, 1)

        def pe_lin_states(pe, b, par):
            pe.wait_ge(a_st.sem, a_st.at(b, 0))
            pe.wait_ge(a_kxe.sem, a_kxe.at(b, 1))
            pe.wait_ge(a_qv.sem, a_qv.at(b, NT))
            for k in range(1, NT):
                for j in range(k):
                    ins = nc.tensor.matmul(psS[:, (k - 1) * D:k * D], kx[:, par, j, :], qv[:, par, 1, j, :],
                                           start=j == 0, stop=j == k - 1)
            ins.then_inc(a_stp.sem, 1)

        def pe_lin_outer_sums(pe, b, k):
            pe.wait_ge(a_kv.sem, a_kv.at(b, k + 1))
            pe.wait_ge(a_prod.sem, a_prod.at(b, k))
            nc.tensor.matmul(wide[:, 0:512], tri, kv[:, k % 2, 0:512], start=True, stop=True)
            nc.tensor.matmul(wide[:, 512:1024], tri, kv[:, k % 2, 512:1024],
                             start=True, stop=True).then_inc(a_cum.sem, 1)

        def pe_lin_qsT(pe, b, front):
            pe.wait_ge(a_qs.sem, a_qs.at(b, 1))
            if front:
                pe.wait_ge(a_xT.sem, a_xT.at(b + 1, 1))
            else:
                pe.wait_ge(a_qsT.sem, a_qsT.at(b, 0))
            for k in range(1, NT):
                ins = nc.tensor.transpose(psT[:, (k - 1) * P:k * P], qs[:, k, :], ident)
            ins.then_inc(a_qsTp.sem, 1)

        def pe_lin_yT(pe, b):
            pe.wait_ge(a_qsT.sem, a_qsT.at(b, 1))
            pe.wait_ge(a_st.sem, a_st.at(b, 1))
            pe.wait_ge(a_red.sem, a_red.at(b, NT))
            pe.wait_ge(a_yT.sem, a_yT.at(b, 0))
            for k in range(NT):
                at = psY[:, k * P:(k + 1) * P]
                if k:
                    nc.tensor.matmul(at, state[:, k - 1, :], tT[:, (k - 1) * P:k * P], start=True, stop=False)
                ins = nc.tensor.matmul(at, y_in[:, k, :], ident, start=k == 0, stop=True)
            ins.then_inc(a_yTp.sem, 1)

        def pe_lin_project(pe, b, last=False):
            pe.wait_ge(a_yT.sem, a_yT.at(b, 1))
            if not last:
                pe.wait_ge(a_den.sem, a_den.at(b + 1, 1))
            for k in range(NT):
                ins = nc.tensor.matmul(psN[:, k * D:(k + 1) * D], yT[:, k * P:(k + 1) * P], wo_sb[:, :],
                                       start=True, stop=True)
            ins.then_inc(a_o.sem, 1)

        def pe_lin_turn(pe, b, par, tail=True, front=True):
            pe_lin_outer_sums(pe, b, 0)
            if front:
                pe_lin_xT(pe, b + 1)
            if tail:
                pe_lin_yT(pe, b - 1)
                pe_lin_project(pe, b - 1)
            if front:
                pe_lin_qkv(pe, b + 1, 0)
                pe_lin_qkv(pe, b + 1, 1)
            pe_lin_outer_sums(pe, b, 1)
            pe_lin_states(pe, b, par)
            if front:
                pe_lin_qkv(pe, b + 1, 2)
                pe_lin_qkv(pe, b + 1, 3)
            pe_lin_outer_sums(pe, b, 2)
            pe_lin_qsT(pe, b, front)
            if front:
                pe_lin_key_sums(pe, b + 1, 1 - par)
            pe_lin_outer_sums(pe, b, 3)

        def lin_pe(pe):
            pe_lin_xT(pe, 0, first=True)
            for k in range(NT):
                pe_lin_qkv(pe, 0, k)
            pe_lin_key_sums(pe, 0, 0, first=True)
            pe_lin_turn(pe, 0, 0, tail=False)
            pe_lin_turn(pe, 1, 1)
            with nc.tensor.Fori(1, B // 2 - 1) as i:
                pe_lin_turn(pe, 2 * i, 0)
                pe_lin_turn(pe, 2 * i + 1, 1)
            pe_lin_turn(pe, B - 2, 0)
            pe_lin_turn(pe, B - 1, 1, front=False)
            pe_lin_yT(pe, B - 1)
            pe_lin_project(pe, B - 1, last=True)

        R = lambda name, per=1, step=1: signal("route_" + name, per, step)
        r_xln, r_xTp, r_xT, r_lgp, r_lg = R("xln", NT), R("xT_psum"), R("xT"), R("logits_psum"), R("logits")
        r_max, r_sub, r_exp, r_sum, r_inv, r_sc = (R("max"), R("shifted"), R("exp"), R("sum"), R("inverse"),
                                                   R("scores"))
        r_scTp, r_scT, r_top, r_rep, r_eq = R("scores_T_psum"), R("scores_T", 2), R("top8"), R("replaced"), R("tie")
        r_run, r_first, r_mask, r_cnt, r_pos = R("tie_count"), R("tie_first"), R("mask"), R("count"), R("pos")
        r_posb, r_posTp, r_posT, r_last = R("pos_bf"), R("pos_T_psum"), R("pos_T"), R("last_slot", 2)
        r_gt, r_moved = R("gates_T"), R("gates_T_moved", 1, 16)
        r_posd = R("pos_in_dram", 1, 16)
        r_part = R("score_parts", 5)

        NR = NT * BE
        new_stage()
        lg = scratch("lg", [P, NT, B, E])
        rmax = scratch("rmax", [P, NT * B])
        sc = scratch("sc", [P, NT, B, E])
        sc_rest = scratch("sc_rest", [P, NT, B, E])
        scT = scratch("scT", [BE, T])
        work = scratch("work", [BE, T])
        top8 = scratch("top8", [BE, 8])
        tie = scratch("tie", [BE, T])
        cnt = scratch("cnt", [BE, T])
        pos = scratch("pos", [BE, T])
        pos_bf = scratch("pos_bf", [BE, T], BF16)
        gates_T = scratch("gates_T", [BE, T])
        pos_dram = nc.dram_tensor("pos_dram", (BE, T), BF16, kind="Internal").ap()

        def route_dve(dve):
            with nc.vector.Fori(0, B) as i:
                dve.wait_ge(r_xTp.sem, r_xTp.at(i, 0))
                normalise(r_xln, i)
            dve.wait_ge(r_lg.sem, r_lg.total(B))
            rows = lambda t: t[:, :, :, :].rearrange("p k b e -> p (k b) e")
            spread = rmax[:, :].unsqueeze(2).broadcast_to([P, NT * B, E])
            nc.vector.tensor_reduce(rmax[:, :], rows(lg), AX.X, ALU.max).then_inc(r_max.sem, 1)
            dve.wait_ge(r_max.sem, r_max.total(1))
            nc.vector.tensor_tensor(rows(lg), rows(lg), spread, ALU.subtract).then_inc(r_sub.sem, 1)
            dve.wait_ge(r_exp.sem, r_exp.total(1))
            nc.vector.tensor_reduce(rmax[:, :], rows(lg), AX.X, ALU.add).then_inc(r_sum.sem, 1)
            dve.wait_ge(r_sum.sem, r_sum.total(1))
            nc.vector.reciprocal(rmax[:, :], rmax[:, :]).then_inc(r_inv.sem, 1)
            dve.wait_ge(r_inv.sem, r_inv.total(1))
            nc.vector.tensor_tensor(rows(sc), rows(lg), spread, ALU.mult).then_inc(r_sc.sem, 1)
            dve.wait_ge(r_scTp.sem, r_scTp.total(1))
            nc.vector.tensor_copy(scT[:, :], bank[0][0:BE, :]).then_inc(r_scT.sem, 1)
            nc.vector.tensor_copy(work[:, :], bank[0][0:BE, :]).then_inc(r_scT.sem, 1)
            with nc.vector.Fori(0, (CAP - 1) // 8) as i:
                dve.wait_ge(r_scT.sem, r_scT.total(2))
                dve.wait_ge(r_rep.sem, r_rep.at(i, 0))
                waits_end(dve)
                nc.vector.max(top8[:, :], work[:, :]).then_inc(r_top.sem, 1)
                dve.wait_ge(r_top.sem, r_top.at(i, 1))
                waits_end(dve)
                nc.vector.match_replace(out=work[:, :], in_to_replace=top8[:, :], in_values=work[:, :],
                                                   imm_value=-1.0).then_inc(r_rep.sem, 1)
            dve.wait_ge(r_rep.sem, r_rep.total((CAP - 1) // 8))
            nc.vector.max(top8[:, :], work[:, :]).then_inc(r_top.sem, 1)
            dve.wait_ge(r_top.sem, r_top.total((CAP - 1) // 8 + 1))
            nc.vector.tensor_scalar(tie[:, :], work[:, :], top8[:, 0:1], None, ALU.is_equal).then_inc(r_eq.sem, 1)
            dve.wait_ge(r_eq.sem, r_eq.total(1))
            nc.vector.tensor_tensor_scan(out=cnt[:, :], data0=tie[:, :], data1=tie[:, :], initial=0.0,
                                                    op0=ALU.add, op1=ALU.bypass).then_inc(r_run.sem, 1)
            dve.wait_ge(r_run.sem, r_run.total(1))
            nc.vector.scalar_tensor_tensor(out=tie[:, :], in0=cnt[:, :], scalar=1.0, in1=tie[:, :],
                                                        op0=ALU.is_equal, op1=ALU.mult).then_inc(r_first.sem, 1)
            dve.wait_ge(r_first.sem, r_first.total(1))
            nc.vector.scalar_tensor_tensor(out=work[:, :], in0=work[:, :], scalar=-1.0, in1=tie[:, :],
                                                       op0=ALU.is_equal, op1=ALU.add).then_inc(r_mask.sem, 1)
            dve.wait_ge(r_mask.sem, r_mask.total(1))
            nc.vector.tensor_tensor_scan(out=cnt[:, :], data0=work[:, :], data1=work[:, :], initial=0.0,
                                                    op0=ALU.add, op1=ALU.bypass).then_inc(r_cnt.sem, 1)
            dve.wait_ge(r_cnt.sem, r_cnt.total(1))
            nc.vector.tensor_tensor(tie[:, :], cnt[:, :], work[:, :], ALU.mult).then_inc(r_run.sem, 1)
            dve.wait_ge(r_run.sem, r_run.total(2))
            nc.vector.tensor_scalar(pos[:, :], tie[:, :], -1.0, None, ALU.add).then_inc(r_pos.sem, 1)
            dve.wait_ge(r_pos.sem, r_pos.total(1))
            nc.vector.tensor_copy(pos_bf[:, :], pos[:, :]).then_inc(r_posb.sem, 1)
            nc.vector.tensor_tensor(gates_T[:, :], work[:, :], scT[:, :], ALU.mult).then_inc(r_gt.sem, 1)
            nc.vector.scalar_tensor_tensor(out=rest_l[0:BE, :], in0=pos[:, :], scalar=float(P),
                                                       in1=scT[:, :], op0=ALU.is_equal, op1=ALU.mult).then_inc(r_last.sem, 1)
            dve.wait_ge(r_posTp.sem, r_posTp.total(1))
            nc.vector.tensor_copy(posT[:, :, :, :].rearrange("p k b e -> p (k b e)"), bank[1][:, 0:NR]).then_inc(r_posT.sem, 1)
            split3(dve, r_part, sc, sc_rest, [sc_part[:, :, :, :, n] for n in range(PARTS)])

        def split3(dve, sig, whole, rest, parts):
            full = (slice(None),) * len(whole.shape)
            nc.vector.tensor_copy(parts[0], whole[full]).then_inc(sig.sem, 1)
            dve.wait_ge(sig.sem, sig.total(1))
            nc.vector.tensor_tensor(rest[full], whole[full], parts[0], ALU.subtract).then_inc(sig.sem, 1)
            dve.wait_ge(sig.sem, sig.total(2))
            nc.vector.tensor_copy(parts[1], rest[full]).then_inc(sig.sem, 1)
            dve.wait_ge(sig.sem, sig.total(3))
            nc.vector.tensor_tensor(rest[full], rest[full], parts[1], ALU.subtract).then_inc(sig.sem, 1)
            dve.wait_ge(sig.sem, sig.total(4))
            nc.vector.tensor_copy(parts[2], rest[full]).then_inc(sig.sem, 1)

        def route_act(act):
            with nc.scalar.Fori(0, B) as i:
                act.wait_ge(r_xTp.sem, r_xTp.at(i, 1))
                act.wait_ge(r_lgp.sem, r_lgp.at(i, 0))
                nc.scalar.activation(xT[:, :], bank[0][:, :], ACT.Copy).then_inc(r_xT.sem, 1)
                act.wait_ge(r_lgp.sem, r_lgp.at(i, 1))
                nc.scalar.activation(lg[:, :, i, :], bank[1][:, 0:NT * E].rearrange("p (k e) -> p k e", e=E),
                                               ACT.Copy).then_inc(r_lg.sem, 1)
            act.wait_ge(r_sub.sem, r_sub.total(1))
            nc.scalar.activation(lg[:, :, :, :], lg[:, :, :, :], ACT.Exp).then_inc(r_exp.sem, 1)

        def route_pe(pe):
            with nc.tensor.Fori(0, B) as i:
                pe.wait_ge(r_xln.sem, r_xln.at(i, NT))
                pe.wait_ge(r_xT.sem, r_xT.at(i, 0))
                for k in range(NT):
                    ins = nc.tensor.transpose(bank[0][:, k * P:(k + 1) * P], xln[:, k, :], ident)
                ins.then_inc(r_xTp.sem, 1)
                pe.wait_ge(r_xT.sem, r_xT.at(i, 1))
                pe.wait_ge(r_lg.sem, r_lg.at(i, 0))
                for k in range(NT):
                    ins = nc.tensor.matmul(bank[1][:, k * E:(k + 1) * E], xT[:, k * P:(k + 1) * P], rT[:, :],
                                           start=True, stop=True)
                ins.then_inc(r_lgp.sem, 1)
            pe.wait_ge(r_sc.sem, r_sc.total(1))
            for k in range(NT):
                ins = nc.tensor.transpose(bank[0][0:BE, k * P:(k + 1) * P],
                                          sc[:, k, :, :].rearrange("p b e -> p (b e)"), ident)
            ins.then_inc(r_scTp.sem, 1)
            pe.wait_ge(r_pos.sem, r_pos.total(1))
            for k in range(NT):
                ins = nc.tensor.transpose(bank[1][:, k * BE:(k + 1) * BE], pos[:, k * P:(k + 1) * P],
                                          ident[0:BE, 0:BE])
            ins.then_inc(r_posTp.sem, 1)

        def route_sync(sp):
            sp.wait_ge(r_posb.sem, r_posb.total(1))
            sp.dma_start(pos_dram, pos_bf[:, :]).then_inc(r_posd.sem, 16)
            sp.wait_ge(r_gt.sem, r_gt.total(1))
            sp.dma_start(rest_l[BE:2 * BE, :], gates_T[:, :]).then_inc(r_moved.sem, 16)

        NP = 2
        M = lambda name, per=1, step=1: signal("moe_" + name, per, step)
        m_bc, m_xln, m_part = M("pos_spread", NP, 16), M("xln", NP * NT), M("x_parts", NP * 5)
        m_scp, m_pick, m_place = M("score_parts", NP), M("pick", NP * NT), M("place", NP)
        m_xgp, m_xg = M("gathered_psum", NP * 3), M("gathered", NP * 3)
        m_gp, m_gate = M("gate_psum", NP), M("gate")
        m_hp, m_h = M("hidden_psum", E * HC), M("hidden", E * HC)
        m_yp, m_y, m_yl = M("y_psum", E), M("y_gated", E), M("y_last", E)
        m_rep, m_repT, m_rest = M("y_last_spread"), M("y_last_T_psum"), M("rest", 2 * NP)
        m_sp, m_x = M("scattered_psum", NP), M("x_updated", NP)

        slots, slot_row = const("slots"), const("slot_row")
        new_stage()
        slots_bf = scratch("slots_bf", [P, CAP], BF16)
        m_slots = M("slots_bf")
        pos_bc = scratch("pos_bc", [P, NP, E, T], BF16)
        x_rest = scratch("x_rest", [P, NT, D])
        x_part = scratch("x_part", [P, NP, PARTS, NT, D], BF16)
        sc_now = scratch("sc_now", [P, NP, NT, E, PARTS], BF16)
        pick = scratch("pick", [P, NP, NT, E, CAP], BF16)
        place = scratch("place", [P, NP, E, T])
        xg = scratch("xg", [P, NP, E, CAP])
        gate = scratch("gate", [P, NP, E])
        hT = scratch("hT", [P, 2, HC, NP, CAP])
        yg = scratch("yg", [P, NP, E, D])
        yl = scratch("yl", [P, NP, E])
        yl_rep = scratch("yl_rep", [P, NP, B, E])
        rest_r = scratch("rest_r", [P, NP, D])
        psH = (wide[:, 0:512], wide[:, 512:1024], bank[5], bank[6])
        psYe = (bank[7], bank[2])
        psG = bank[2][:, 448:448 + NP * E * PARTS]
        psRep = (bank[7][0:BE, 384:384 + D], bank[2][0:BE, 264:264 + D])
        GP = 3
        experts_to = [-(-GC * (c + 1) // CAP) for c in range(GP)]
        gathers_for = [NP * -(-CAP * (e + 1) // GC) for e in range(E)]

        PARTS_AT = {0: (1,)}
        PICK_AT = {1: ((1, 0), (1, 1)), 2: ((1, 2), (1, 3))}
        GATE_AT = {2: 0, 4: 1}
        STATS_AT = {4: 0, 5: 1}
        GATHER_AT = {3: (0,), 4: (1,), 5: (2,), 6: (3,), 7: (4, 5)}

        def moe_sync(sp):
            sp.wait_ge(r_posd.sem, r_posd.total(16))
            sp.wait_ge(r_moved.sem, r_moved.total(16))
            sp.wait_ge(r_part.sem, r_part.total(5))
            with nc.sync.Fori(0, B // NP) as i:
                sp.wait_ge(m_place.sem, m_place.at(i, 0))
                for r in range(NP):
                    src = pos_dram.rearrange("(b e) t -> b (e t)", e=E)[NP * i + r]
                    src = src.rearrange("(a n) -> a n", a=1) if len(src.shape) == 1 else src
                    sp.dma_start(pos_bc[:, r, :, :].rearrange("p e t -> p (e t)"),
                                 src.broadcast_to([P, E * T])).then_inc(m_bc.sem, 16)

        def moe_pool(pool):
            with nc.gpsimd.Fori(0, B // NP) as i:
                for r in range(NP):
                    pool.wait_ge(m_bc.sem, m_bc.at(i, NP))
                    pool.wait_ge(m_sp.sem, m_sp.at(i, 0))
                    waits_end(pool)
                    nc.gpsimd.tensor_scalar(place[:, r, :, :].rearrange("p e t -> p (e t)"),
                                                         pos_bc[:, r, :, :].rearrange("p e t -> p (e t)"),
                                                         slot_row, None, ALU.is_equal).then_inc(m_place.sem, 1)

        def dve_moe_parts(dve, i, r):
            s = lambda n: 5 * r + n
            for k in range(NT):
                ins = nc.vector.tensor_scalar(xln[:, k, :], x_sb[:, NP * i + r, k, :], mv[:, NP * i + r, k, 0:1],
                                              rstd[:, NP * i + r, k:k + 1], ALU.subtract, ALU.mult)
                ins.then_inc(m_xln.sem, 1)
            dve.wait_ge(m_xln.sem, m_xln.at(i, (r + 1) * NT))
            dve.wait_ge(m_xgp.sem, m_xgp.at(i, 0))
            dve.wait_ge(m_gp.sem, m_gp.at(i, 0))
            nc.vector.tensor_copy(x_part[:, r, 0], xln[:, :, :]).then_inc(m_part.sem, 1)
            dve.wait_ge(m_part.sem, m_part.at(i, s(1)))
            nc.vector.tensor_tensor(x_rest[:, :, :], xln[:, :, :], x_part[:, r, 0], ALU.subtract).then_inc(m_part.sem, 1)
            dve.wait_ge(m_part.sem, m_part.at(i, s(2)))
            nc.vector.tensor_copy(x_part[:, r, 1], x_rest[:, :, :]).then_inc(m_part.sem, 1)
            dve.wait_ge(m_part.sem, m_part.at(i, s(3)))
            nc.vector.tensor_tensor(x_rest[:, :, :], x_rest[:, :, :], x_part[:, r, 1], ALU.subtract).then_inc(m_part.sem, 1)
            dve.wait_ge(m_part.sem, m_part.at(i, s(4)))
            nc.vector.tensor_copy(x_part[:, r, 2], x_rest[:, :, :]).then_inc(m_part.sem, 1)
            nc.vector.tensor_copy(sc_now[:, r], sc_part[:, :, NP * i + r, :, :]).then_inc(m_scp.sem, 1)

        def dve_moe_pick(dve, i, r, k):
            nc.vector.tensor_tensor(
                pick[:, r, k, :, :], slots_bf[:, :].unsqueeze(1).broadcast_to([P, E, CAP]),
                posT[:, k, NP * i + r, :].unsqueeze(2).broadcast_to([P, E, CAP]), ALU.is_equal).then_inc(m_pick.sem, 1)

        def dve_moe_gate(dve, i):
            dve.wait_ge(m_gp.sem, m_gp.at(i, NP))
            dve.wait_ge(m_y.sem, m_y.at(i, 0))
            nc.vector.tensor_reduce(gate[:, :, :], psG.rearrange("p (r e n) -> p r e n", e=E, n=PARTS),
                                    AX.X, ALU.add).then_inc(m_gate.sem, 1)

        def dve_moe_gated(dve, i, e):
            if e == 0:
                dve.wait_ge(m_gate.sem, m_gate.at(i, 1))
                dve.wait_ge(m_sp.sem, m_sp.at(i, 0))
                dve.wait_ge(m_rep.sem, m_rep.at(i, 0))
            dve.wait_ge(m_yp.sem, m_yp.at(i, e + 1))
            nc.vector.tensor_tensor(yg[:, :, e, :], psYe[e % 2][:, 0:NP * D].rearrange("p (r d) -> p r d", d=D),
                                    gate[:, :, e].unsqueeze(2).broadcast_to([P, NP, D]), ALU.mult).then_inc(m_y.sem, 1)
            nc.vector.tensor_copy(yl[:, :, e], psYe[e % 2][:, NP * D:NP * D + NP]).then_inc(m_yl.sem, 1)

        def dve_moe_last_spread(dve, i):
            dve.wait_ge(m_yl.sem, m_yl.at(i, E))
            dve.wait_ge(m_repT.sem, m_repT.at(i, 0))
            nc.vector.tensor_copy(yl_rep[:, :, :, :], yl[:, :, :].unsqueeze(2).broadcast_to([P, NP, B, E])).then_inc(m_rep.sem, 1)

        def dve_moe_rest(dve, i):
            dve.wait_ge(m_repT.sem, m_repT.at(i, 1))
            dve.wait_ge(m_sp.sem, m_sp.at(i, 0))
            for r in range(NP):
                nc.vector.tensor_scalar(rest_r[0:BE, r, :], psRep[r], seqmask[0:BE, NP * i + r].unsqueeze(1),
                                        None, ALU.mult).then_inc(m_rest.sem, 1)
                nc.vector.tensor_scalar(rest_r[BE:2 * BE, r, :], b2rep[BE:2 * BE, :],
                                        seqmask[BE:2 * BE, NP * i + r].unsqueeze(1), None, ALU.mult).then_inc(m_rest.sem, 1)

        def dve_moe_residual(dve, i, r):
            dve.wait_ge(m_sp.sem, m_sp.at(i, r + 1))
            nc.vector.tensor_tensor(x_sb[:, NP * i + r], x_sb[:, NP * i + r],
                                    bank[r][:, :].rearrange("p (k d) -> p k d", d=D), ALU.add).then_inc(m_x.sem, 1)

        def dve_moe_stats(dve, i, r):
            dve.wait_ge(m_x.sem, m_x.at(i, r + 1))
            ln3.dve_sequence(dve, NP * i + r)

        def dve_moe_turn(dve, i, scatter=True, gather=True):
            if scatter:
                dve_moe_rest(dve, i - 1)
            if gather:
                dve_moe_parts(dve, i + 1, 0)
                for k in range(NT):
                    dve_moe_pick(dve, i + 1, 0, k)
            if scatter:
                for r in range(NP):
                    dve_moe_residual(dve, i - 1, r)
            for e in range(E):
                dve_moe_gated(dve, i, e)
                if gather:
                    for r in PARTS_AT.get(e, ()):
                        dve_moe_parts(dve, i + 1, r)
                    for r, k in PICK_AT.get(e, ()):
                        dve_moe_pick(dve, i + 1, r, k)
                if scatter and e in STATS_AT:
                    dve_moe_stats(dve, i - 1, STATS_AT[e])
            dve_moe_last_spread(dve, i)
            if gather:
                dve_moe_gate(dve, i + 1)

        def moe_dve(dve):
            nc.vector.tensor_copy(slots_bf[:, :], slots).then_inc(m_slots.sem, 1)
            dve.wait_ge(m_slots.sem, m_slots.total(1))
            for r in range(NP):
                dve_moe_parts(dve, 0, r)
                for k in range(NT):
                    dve_moe_pick(dve, 0, r, k)
            dve_moe_gate(dve, 0)
            dve_moe_turn(dve, 0, scatter=False)
            with nc.vector.Fori(1, B // NP - 1) as i:
                dve_moe_turn(dve, i)
            dve_moe_turn(dve, B // NP - 1, gather=False)
            dve_moe_rest(dve, B // NP - 1)
            for r in range(NP):
                dve_moe_residual(dve, B // NP - 1, r)
                dve_moe_stats(dve, B // NP - 1, r)
            dve.wait_ge(m_x.sem, m_x.at(B // NP, 0))

        def act_moe_gathered(act, i, n, first=False):
            c, r = divmod(n, NP)
            act.wait_ge(m_xgp.sem, m_xgp.at(i, n + 1))
            if not first:
                act.wait_ge(m_hp.sem, m_hp.at(i - 1, experts_to[c] * HC))
            nc.scalar.activation(xg[:, r, :, :].rearrange("p e c -> p (e c)")[:, c * GC:(c + 1) * GC],
                                 bank[n % 2][:, 0:GC], ACT.Copy).then_inc(m_xg.sem, 1)

        def act_moe_gelu(act, i, e):
            for c in range(HC):
                act.wait_ge(m_hp.sem, m_hp.at(i, e * HC + c + 1))
                act.wait_ge(m_yp.sem, m_yp.at(i, e - 1 if e >= 2 else 0))
                nc.scalar.activation(hT[:, e % 2, c, :, :],
                                     psH[c][:, 0:NP * CAP].rearrange("p (r c) -> p r c", c=CAP),
                                     ACT.Gelu, bias=b1T[:, e * HC + c:e * HC + c + 1]).then_inc(m_h.sem, 1)

        def act_moe_turn(act, i, gather=True):
            act_moe_gelu(act, i, 0)
            for e in range(E):
                if e + 1 < E:
                    act_moe_gelu(act, i, e + 1)
                if gather:
                    for n in GATHER_AT.get(e, ()):
                        act_moe_gathered(act, i + 1, n)

        def moe_act(act):
            for n in range(NP * GP):
                act_moe_gathered(act, 0, n, first=True)
            with nc.scalar.Fori(0, B // NP - 1) as i:
                act_moe_turn(act, i)
            act_moe_turn(act, B // NP - 1, gather=False)

        def pe_moe_gather(pe, i, n):
            c, r = divmod(n, NP)
            pe.wait_ge(m_part.sem, m_part.at(i, 5 * (r + 1)))
            pe.wait_ge(m_pick.sem, m_pick.at(i, (r + 1) * NT))
            if n >= 2:
                pe.wait_ge(m_xg.sem, m_xg.at(i, n - 1))
            else:
                pe.wait_ge(m_xg.sem, m_xg.at(i, 0))
            for k in range(NT):
                for part in range(PARTS):
                    ins = nc.tensor.matmul(
                        bank[n % 2][:, 0:GC], x_part[:, r, part, k, :],
                        pick[:, r, k, :, :].rearrange("p e c -> p (e c)")[:, c * GC:(c + 1) * GC],
                        start=k == 0 and part == 0, stop=k == NT - 1 and part == PARTS - 1)
            ins.then_inc(m_xgp.sem, 1)

        def pe_moe_gates(pe, i, r, experts_before=0):
            pe.wait_ge(m_pick.sem, m_pick.at(i, (r + 1) * NT))
            pe.wait_ge(m_scp.sem, m_scp.at(i, r + 1))
            pe.wait_ge(m_gate.sem, m_gate.at(i, 0))
            if experts_before:
                pe.wait_ge(m_yl.sem, m_yl.at(i - 1, experts_before))
            for e in range(E):
                for k in range(NT):
                    at = (r * E + e) * PARTS
                    ins = nc.tensor.matmul(psG[:, at:at + PARTS], pick[:, r, k, e, 0:P], sc_now[:, r, k, e, :],
                                           start=k == 0, stop=k == NT - 1)
            ins.then_inc(m_gp.sem, 1)

        def pe_moe_hidden(pe, i, e):
            pe.wait_ge(m_xg.sem, m_xg.at(i, gathers_for[e]))
            for c in range(HC):
                if e:
                    pe.wait_ge(m_h.sem, m_h.at(i, (e - 1) * HC + c + 1))
                else:
                    pe.wait_ge(m_h.sem, m_h.at(i, 0))
                nc.tensor.matmul(psH[c][:, 0:NP * CAP].rearrange("p (r c) -> p r c", c=CAP),
                                 w1_sb[:, e, c * P:(c + 1) * P], xg[:, :, e, :], start=True, stop=True).then_inc(m_hp.sem, 1)

        def pe_moe_output(pe, i, e):
            pe.wait_ge(m_h.sem, m_h.at(i, (e + 1) * HC))
            if e >= 2:
                pe.wait_ge(m_yl.sem, m_yl.at(i, e - 1))
            else:
                pe.wait_ge(m_yl.sem, m_yl.at(i, 0))
            if e == 1:
                pe.wait_ge(m_gate.sem, m_gate.at(i, 1))
            for r in range(NP):
                for c in range(HC):
                    nc.tensor.matmul(psYe[e % 2][:, r * D:(r + 1) * D], hT[:, e % 2, c, r, 0:P], w2_sb[:, e, c, :],
                                     start=c == 0, stop=c == HC - 1)
            for c in range(HC):
                ins = nc.tensor.matmul(psYe[e % 2][:, NP * D:NP * D + NP], w2_sb[:, e, c, :],
                                       hT[:, e % 2, c, :, P], start=c == 0, stop=c == HC - 1)
            ins.then_inc(m_yp.sem, 1)

        def pe_moe_last_T(pe, i, last=False):
            pe.wait_ge(m_rep.sem, m_rep.at(i, 1))
            pe.wait_ge(m_rest.sem, m_rest.at(i, 0))
            if not last:
                pe.wait_ge(m_gate.sem, m_gate.at(i + 1, 1))
            waits_end(pe)
            for r in range(NP):
                ins = nc.tensor.transpose(psRep[r], yl_rep[:, r, :, :].rearrange("p b e -> p (b e)"), ident)
            ins.then_inc(m_repT.sem, 1)

        def pe_moe_scatter(pe, i, r, last=False):
            pe.wait_ge(m_y.sem, m_y.at(i, E))
            pe.wait_ge(m_place.sem, m_place.at(i, r + 1))
            pe.wait_ge(m_x.sem, m_x.at(i, 0))
            if not last:
                pe.wait_ge(m_xg.sem, m_xg.at(i + 1, NP * GP))
            for k in range(NT):
                at = bank[r][:, k * D:(k + 1) * D]
                for e in range(E):
                    nc.tensor.matmul(at, place[:, r, e, k * P:(k + 1) * P], yg[:, r, e, :],
                                     start=e == 0, stop=False)
                if k == 0:
                    pe.wait_ge(m_rest.sem, m_rest.at(i, 2 * NP))
                ins = nc.tensor.matmul(at, rest_l[:, k * P:(k + 1) * P], rest_r[:, r, :], start=False, stop=True)
            ins.then_inc(m_sp.sem, 1)

        def pe_moe_turn(pe, i, scatter=True, gather=True):
            pe_moe_hidden(pe, i, 0)
            if scatter:
                pe_moe_last_T(pe, i - 1)
                pe_moe_scatter(pe, i - 1, 0)
            pe_moe_hidden(pe, i, 1)
            if scatter:
                pe_moe_scatter(pe, i - 1, 1)
            for e in range(E):
                if 1 <= e < E - 1:
                    pe_moe_hidden(pe, i, e + 1)
                pe_moe_output(pe, i, e)
                if gather:
                    if e in GATE_AT:
                        pe_moe_gates(pe, i + 1, GATE_AT[e], experts_before=e)
                    for n in GATHER_AT.get(e, ()):
                        if n < NP and scatter:
                            pe.wait_ge(m_x.sem, m_x.at(i, 0))
                        pe_moe_gather(pe, i + 1, n)

        def moe_pe(pe):
            pe.wait_ge(r_moved.sem, r_moved.total(16))
            for n in range(NP * GP):
                pe_moe_gather(pe, 0, n)
            for r in range(NP):
                pe_moe_gates(pe, 0, r)
            pe_moe_turn(pe, 0, scatter=False)
            with nc.tensor.Fori(1, B // NP - 1) as i:
                pe_moe_turn(pe, i)
            pe_moe_turn(pe, B // NP - 1, gather=False)
            pe_moe_last_T(pe, B // NP - 1, last=True)
            for r in range(NP):
                pe_moe_scatter(pe, B // NP - 1, r, last=True)

        Q = lambda name, per=1, step=1: signal("mqa_" + name, per, step)
        q_init = Q("buffers_set")
        q_xln, q_xTp, q_xT, q_qkvp, q_qkv = Q("xln", NT), Q("xT_psum"), Q("xT"), Q("qkv_psum", 2), Q("qkv", 2)
        q_kpart, q_qpart, q_v, q_kx, q_qx = Q("k_parts", 5), Q("q_parts", 5), Q("v"), Q("k_slots", PARTS), Q("q_slots", NT * PARTS)
        q_kTp, q_kTm, q_kTe = Q("kT_psum"), Q("kT_for_max"), Q("kT_for_exp")
        NU = HEADS // 2
        q_qTp, q_qT = Q("qT_psum", 2 * NT), Q("qT", 2 * NT)
        max_units = [(k, h, n) for k in range(NT) for n in (max(1, 4 // (k + 1) if k != 2 else 1),)
                     for h in range(0, HEADS, n)]
        NM = len(max_units)
        q_smp, q_mx, q_neg, q_mpart = Q("max_scores_psum", NM), Q("max", NM), Q("neg_max"), Q("neg_max_parts", 5)
        q_mTp, q_mT, q_mrow = Q("neg_max_T_psum"), Q("neg_max_T"), Q("shift_rows", PARTS, 16)
        NX = NQ * NT * 2
        q_sp, q_p = Q("scores_psum", NX), Q("exp", NX)
        q_av, q_o = Q("values_summed", NQ * NT), Q("o", NQ)
        q_oTp, q_rd, q_y = Q("o_back_psum", NT), Q("sum_inverse", NT), Q("y", NT)
        q_yTp, q_yT, q_prp, q_x = Q("yT_psum"), Q("yT"), Q("projected_psum"), Q("x_updated")

        new_stage()
        qkv = scratch("qkv", [P, NT, D + 2 * L])
        kp = scratch("kp", [P, PARTS, NT, L], BF16)
        k_rest = scratch("k_rest", [P, NT, L])
        qp = scratch("qp", [P, PARTS, NT, D], BF16)
        q_rest = scratch("q_rest", [P, NT, D])
        vx = scratch("vx", [P, 2, NT, 32])
        kx3 = scratch("kx3", [P, NT, PARTS, PARTS, L], BF16)
        qx3 = scratch("qx3", [P, NT, HEADS, PARTS, PARTS, L], BF16)
        kTm = scratch("kTm", [P, T], BF16)
        kTe = scratch("kTe", [P, 2, T], BF16)
        qT = scratch("qT", [P, 2, HEADS, T], BF16)
        mx = scratch("mx", [P, NT, HEADS])
        mp = scratch("mp", [P, NT, PARTS, HEADS], BF16)
        mT = scratch("mT", [PARTS * HEADS, T], BF16)
        pexp = scratch("pexp", [P, 4, 2, T])
        oT = scratch("oT", [P, NQ, T])
        rd = scratch("rd", [P, 2, HEADS])
        y2 = scratch("y2", [P, NT, D])
        y2T = scratch("y2T", [P, T])
        mask_qk = scratch("mask_qk", [P, P], BF16)
        mask_kq = scratch("mask_kq", [P, P], BF16)
        causal_qk, causal_kq, shift_rows = const("causal_qk"), const("causal_kq"), const("shift_rows")
        psM2, psE, psO = (bank[1], bank[2]), (wide, wide2), bank[7]

        STEPS = NQ * NT
        MAX_STEPS = range(3, 14)
        XLN_STEP, XT_STEP, QKV_STEPS, SPLIT_STEP = 1, 3, (4, 5), 6
        IN_STEP = NM // len(MAX_STEPS)
        assert NM == IN_STEP * len(MAX_STEPS) and IN_STEP == 4
        NM_EARLY = sum(k < 2 for k, _, _ in max_units)
        BACK_T_STEP, PROJECT_STEP = 1, 2
        SHIFT_STEP, SHIFT_T_STEP = MAX_STEPS[-1] + 1, STEPS - 1

        def max_unit(s, n):
            return (IN_STEP * (s - MAX_STEPS[0]) + n,) if s in MAX_STEPS else ()

        def split(dve, sig, b, whole, rest, parts, ops=range(2 * PARTS - 1)):
            for n in ops:
                part = parts[n // 2]
                if n:
                    dve.wait_ge(sig.sem, sig.at(b, n))
                if n % 2 == 0:
                    nc.vector.tensor_copy(part, whole if n == 0 else rest).then_inc(sig.sem, 1)
                else:
                    nc.vector.tensor_tensor(rest, whole if n == 1 else rest, part, ALU.subtract).then_inc(sig.sem, 1)

        def dve_xln(dve, b):
            dve.wait_ge(q_xTp.sem, q_xTp.at(b, 0))
            normalise(q_xln, b)

        def dve_k_parts(dve, b, ops=range(5)):
            dve.wait_ge(q_qkv.sem, q_qkv.at(b, 2))
            dve.wait_ge(q_kx.sem, q_kx.at(b, 0))
            split(dve, q_kpart, b, qkv[:, :, D:D + L], k_rest[:, :, :], [kp[:, n] for n in range(PARTS)], ops)

        def dve_q_parts(dve, b, ops=range(5)):
            dve.wait_ge(q_qkv.sem, q_qkv.at(b, 2))
            dve.wait_ge(q_qx.sem, q_qx.at(b, 0))
            split(dve, q_qpart, b, qkv[:, :, 0:D], q_rest[:, :, :], [qp[:, n] for n in range(PARTS)], ops)

        def dve_v(dve, b, par, first):
            dve.wait_ge(q_qkv.sem, q_qkv.at(b, 2))
            if not first:
                dve.wait_ge(q_av.sem, q_av.at(b - 1, 0))
            nc.vector.tensor_copy(vx[:, par, :, 0:L], qkv[:, :, D + L:D + 2 * L]).then_inc(q_v.sem, 1)

        def dve_keys(dve, b, par):
            dve.wait_ge(q_kTp.sem, q_kTp.at(b, 1))
            src = bank[0][:, :].bitcast(BF16)[0:QR, 0:T]
            nc.vector.tensor_copy(kTm[0:QR, :], src).then_inc(q_kTm.sem, 1)
            nc.vector.tensor_copy(kTe[0:QR, par, :], src).then_inc(q_kTe.sem, 1)

        def dve_max(dve, b, units):
            for n in units:
                k, h, nh = max_units[n]
                w = P * (k + 1)
                if n == 0:
                    dve.wait_ge(q_mpart.sem, q_mpart.at(b, 0))
                dve.wait_ge(q_smp.sem, q_smp.at(b, n + 1))
                nc.vector.tensor_reduce(mx[:, k, h:h + nh],
                                        psM2[n % 2][:, 0:nh * w].rearrange("p (h s) -> p h s", s=w),
                                        AX.X, ALU.max).then_inc(q_mx.sem, 1)

        def dve_shift(dve, b):
            dve.wait_ge(q_mx.sem, q_mx.at(b, NM))
            nc.vector.tensor_scalar(mx[:, :, :], mx[:, :, :], -1.0, None, ALU.mult).then_inc(q_neg.sem, 1)
            dve.wait_ge(q_neg.sem, q_neg.at(b, 1))
            dve.wait_ge(q_mTp.sem, q_mTp.at(b, 0))
            split(dve, q_mpart, b, mx[:, :, :], mx[:, :, :], [mp[:, :, n, :] for n in range(PARTS)])

        def dve_shift_T(dve, b):
            dve.wait_ge(q_mTp.sem, q_mTp.at(b, 1))
            dve.wait_ge(q_mrow.sem, q_mrow.at(b, 0))
            nc.vector.tensor_copy(mT[:, :], bank[0][:, :].bitcast(BF16)[0:PARTS * HEADS, 0:T]).then_inc(q_mT.sem, 1)

        def dve_quad(dve, b, qd):
            dve.wait_ge(q_av.sem, q_av.at(b, (qd + 1) * NT))
            dve.wait_ge(q_oTp.sem, q_oTp.at(b, 0))
            nc.vector.tensor_copy(oT[:, qd, :], psO[:, :]).then_inc(q_o.sem, 1)

        def dve_divide(dve, b, tiles):
            for k in tiles:
                dve.wait_ge(q_oTp.sem, q_oTp.at(b, k + 1))
                ps = psM2[k % 2][:, :].rearrange("p (h c) -> p h c", c=32)
                nc.vector.reciprocal(rd[:, k % 2, :], ps[:, :, L]).then_inc(q_rd.sem, 1)
                dve.wait_ge(q_rd.sem, q_rd.at(b, k + 1))
                dve.wait_ge(q_yTp.sem, q_yTp.at(b, 0))
                nc.vector.tensor_tensor(y2[:, k, :].rearrange("p (h l) -> p h l", l=L), ps[:, :, 0:L],
                                        rd[:, k % 2, :].unsqueeze(2).broadcast_to([P, HEADS, L]),
                                        ALU.mult).then_inc(q_y.sem, 1)

        def dve_residual(dve, b):
            dve.wait_ge(q_prp.sem, q_prp.at(b, 1))
            nc.vector.tensor_tensor(x_sb[:, b], x_sb[:, b], psM2[1][:, :].rearrange("p (k d) -> p k d", d=D),
                                    ALU.add).then_inc(q_x.sem, 1)

        def dve_stats(dve, b):
            dve.wait_ge(q_x.sem, q_x.at(b, 1))
            ln4.dve_sequence(dve, b)

        def dve_turn(dve, b, par, tail=True, middle=True, front=True):
            if middle:
                dve_v(dve, b + 1, 1 - par, False)
                dve_keys(dve, b + 1, 1 - par)
            if tail:
                dve_divide(dve, b - 1, (0, 1))
                dve_divide(dve, b - 1, (2, 3))
            for s in range(STEPS):
                if s and s % NT == 0:
                    dve_quad(dve, b, s // NT - 1)
                if tail and s == PROJECT_STEP:
                    dve_residual(dve, b - 1)
                if front and s == XLN_STEP:
                    dve_xln(dve, b + 2)
                if tail and s == PROJECT_STEP:
                    dve_stats(dve, b - 1)
                for n in range(IN_STEP):
                    if middle:
                        dve_max(dve, b + 1, max_unit(s, n))
                    at = IN_STEP * (s - SPLIT_STEP) + n
                    if front and 0 <= at < 5:
                        dve_k_parts(dve, b + 2, (at,))
                    if front and 5 <= at < 10:
                        dve_q_parts(dve, b + 2, (at - 5,))
                if middle and s == MAX_STEPS[-1]:
                    dve_shift(dve, b + 1)
                if middle and s == SHIFT_T_STEP:
                    dve_shift_T(dve, b + 1)
            dve_quad(dve, b, NQ - 1)

        def mqa_dve(dve):
            nc.vector.tensor_copy(mask_qk[:, :], causal_qk)
            nc.vector.tensor_copy(mask_kq[:, :], causal_kq)
            nc.vector.memset(kTm[64:P, :], 0.0)
            nc.vector.memset(qT[64:P, :, :, :], 0.0)
            nc.vector.memset(vx[:, :, :, :], 0.0)
            nc.vector.tensor_copy(kTe[64:P, :, :], shift_rows[64:P, :].unsqueeze(2).broadcast_to([64, 2, T])).then_inc(q_init.sem, 1)
            dve.wait_ge(q_init.sem, q_init.total(1))
            nc.vector.memset(vx[:, :, :, L:L + 1], 1.0).then_inc(q_init.sem, 1)
            dve.wait_ge(q_init.sem, q_init.total(2))
            dve_xln(dve, 0)
            dve_k_parts(dve, 0)
            dve_q_parts(dve, 0)
            dve_v(dve, 0, 0, True)
            dve_xln(dve, 1)
            dve_keys(dve, 0, 0)
            dve_max(dve, 0, range(NM_EARLY))
            dve_k_parts(dve, 1)
            dve_q_parts(dve, 1)
            dve_max(dve, 0, range(NM_EARLY, NM))
            dve_shift(dve, 0)
            dve_shift_T(dve, 0)
            dve_turn(dve, 0, 0, tail=False)
            dve_turn(dve, 1, 1)
            with nc.vector.Fori(1, B // 2 - 1) as i:
                dve_turn(dve, 2 * i, 0)
                dve_turn(dve, 2 * i + 1, 1)
            dve_turn(dve, B - 2, 0, front=False)
            dve_turn(dve, B - 1, 1, middle=False, front=False)
            dve_divide(dve, B - 1, range(NT))
            dve_residual(dve, B - 1)
            dve_stats(dve, B - 1)
            dve.wait_ge(q_x.sem, q_x.total(B))

        def mqa_pool(pool):
            with nc.gpsimd.Fori(0, B) as b:
                pool.wait_ge(q_kpart.sem, q_kpart.at(b, 5))
                pool.wait_ge(q_kTp.sem, q_kTp.at(b, 0))
                waits_end(pool)
                for n in range(PARTS):
                    nc.gpsimd.tensor_copy(kx3[:, :, :, n, :],
                                          kp[:, n].unsqueeze(2).broadcast_to([P, NT, PARTS, L])).then_inc(q_kx.sem, 1)
                pool.wait_ge(q_qpart.sem, q_qpart.at(b, 5))
                pool.wait_ge(q_qTp.sem, q_qTp.at(b, 0))
                waits_end(pool)
                for k in range(NT):
                    for n in range(PARTS):
                        nc.gpsimd.tensor_copy(
                            qx3[:, k, :, n, :, :], qp[:, n, k].rearrange("p (h l) -> p h l", l=L).unsqueeze(2)
                            .broadcast_to([P, HEADS, PARTS, L])).then_inc(q_qx.sem, 1)

        def act_xT(act, b):
            act.wait_ge(q_xTp.sem, q_xTp.at(b, 1))
            act.wait_ge(q_qkvp.sem, q_qkvp.at(b, 0))
            nc.scalar.activation(xT[:, :], bank[0][:, :], ACT.Copy).then_inc(q_xT.sem, 1)

        def act_qkv(act, b, r):
            act.wait_ge(q_qkvp.sem, q_qkvp.at(b, r + 1))
            act.wait_ge(q_qpart.sem, q_qpart.at(b, 0))
            act.wait_ge(q_kpart.sem, q_kpart.at(b, 0))
            act.wait_ge(q_v.sem, q_v.at(b, 0))
            nc.scalar.activation(qkv[:, 2 * r:2 * r + 2, :],
                                 bank[0][:, 0:2 * (D + 2 * L)].rearrange("p (k n) -> p k n", k=2),
                                 ACT.Copy).then_inc(q_qkv.sem, 1)

        def act_qT(act, b, par, u):
            k, half = divmod(u, 2)
            act.wait_ge(q_qTp.sem, q_qTp.at(b, u + 1))
            nc.scalar.activation(qT[0:QR, par, half * NU:(half + 1) * NU, k * P:(k + 1) * P],
                                 bank[0][:, :].bitcast(BF16)[0:QR, :].rearrange("p (h t) -> p h t", h=NU),
                                 ACT.Copy).then_inc(q_qT.sem, 1)

        def act_exp(act, b, step, halves=(0, 1)):
            w = T - P * (step % NT)
            for n in (2 * step + half for half in halves):
                act.wait_ge(q_sp.sem, q_sp.at(b, n + 1))
                act.wait_ge(q_av.sem, q_av.at(b, step - 1 if step >= 2 else 0))
                nc.scalar.activation(pexp[:, n % 4, :, 0:w],
                                     psE[n % 2][:, :].rearrange("p (h t) -> p h t", h=2)[:, :, 0:w],
                                     ACT.Exp, scale=SCALE).then_inc(q_p.sem, 1)

        def act_yT(act, b):
            act.wait_ge(q_yTp.sem, q_yTp.at(b, 1))
            act.wait_ge(q_prp.sem, q_prp.at(b, 0))
            nc.scalar.activation(y2T[:, :], psM2[0][:, :], ACT.Copy).then_inc(q_yT.sem, 1)

        def act_turn(act, b, par, tail=True, middle=True, front=True):
            if middle:
                act.wait_ge(q_sp.sem, q_sp.at(b, 0))
                act_qT(act, b + 1, 1 - par, 0)
                act_qT(act, b + 1, 1 - par, 1)
            act_exp(act, b, 0)
            for s in range(STEPS):
                for half in range(2):
                    if s + 1 < STEPS:
                        act_exp(act, b, s + 1, (half,))
                    if middle and 2 * s + 2 + half < 2 * NT:
                        act_qT(act, b + 1, 1 - par, 2 * s + 2 + half)
                if tail and s == BACK_T_STEP:
                    act_yT(act, b - 1)
                if front and s == XT_STEP:
                    act_xT(act, b + 2)
                if front and s in QKV_STEPS:
                    act_qkv(act, b + 2, QKV_STEPS.index(s))

        def mqa_act(act):
            act_xT(act, 0)
            for r in range(2):
                act_qkv(act, 0, r)
            act_xT(act, 1)
            for r in range(2):
                act_qkv(act, 1, r)
            for u in range(2 * NT):
                act_qT(act, 0, 0, u)
            act_turn(act, 0, 0, tail=False)
            act_turn(act, 1, 1)
            with nc.scalar.Fori(1, B // 2 - 1) as i:
                act_turn(act, 2 * i, 0)
                act_turn(act, 2 * i + 1, 1)
            act_turn(act, B - 2, 0, front=False)
            act_turn(act, B - 1, 1, middle=False, front=False)
            act_yT(act, B - 1)

        def sp_rows(sp, b, par):
            sp.wait_ge(q_mT.sem, q_mT.at(b, 1))
            for n in range(PARTS):
                sp.dma_start(qT[QR + n:QR + n + 1, par, :, :],
                             mT[n * HEADS:(n + 1) * HEADS, :]).then_inc(q_mrow.sem, 16)

        def mqa_sync(sp):
            with nc.sync.Fori(0, B // 2) as i:
                sp_rows(sp, 2 * i, 0)
                sp_rows(sp, 2 * i + 1, 1)

        def pe_xT(pe, b, first=False):
            pe.wait_ge(q_xln.sem, q_xln.at(b, NT))
            if first:
                pe.wait_ge(q_qkv.sem, q_qkv.at(b, 0))
            else:
                pe.wait_ge(q_qT.sem, q_qT.at(b, 0))
            for k in range(NT):
                ins = nc.tensor.transpose(bank[0][:, k * P:(k + 1) * P], xln[:, k, :], ident)
            ins.then_inc(q_xTp.sem, 1)

        def pe_qkv(pe, b, r):
            pe.wait_ge(q_xT.sem, q_xT.at(b, 1))
            if r:
                pe.wait_ge(q_qkv.sem, q_qkv.at(b, r))
            n = D + 2 * L
            for j in range(2):
                k = 2 * r + j
                ins = nc.tensor.matmul(bank[0][:, j * n:(j + 1) * n], xT[:, k * P:(k + 1) * P], wa_sb[:, :],
                                       start=True, stop=True)
            ins.then_inc(q_qkvp.sem, 1)

        def pe_kT(pe, b, first=False):
            pe.wait_ge(q_kx.sem, q_kx.at(b, 3))
            pe.wait_ge(q_qkv.sem, q_qkv.at(b + 1 if first else b, 2))
            pe.wait_ge(q_mT.sem, q_mT.at(b, 0))
            for k in range(NT):
                ins = nc.tensor.transpose(bank[0][:, :].bitcast(BF16)[0:QR, k * P:(k + 1) * P],
                                          kx3[:, k].rearrange("p n j l -> p (n j l)"), ident_bf[:, :])
            ins.then_inc(q_kTp.sem, 1)

        def pe_qT(pe, b, u):
            k, half = divmod(u, 2)
            pe.wait_ge(q_qx.sem, q_qx.at(b, PARTS * (k + 1)))
            if u == 0:
                pe.wait_ge(q_kTe.sem, q_kTe.at(b, 1))
            else:
                pe.wait_ge(q_qT.sem, q_qT.at(b, u))
            for h in range(NU):
                ins = nc.tensor.transpose(bank[0][:, :].bitcast(BF16)[0:QR, h * P:(h + 1) * P],
                                          qx3[:, k, half * NU + h].rearrange("p n j l -> p (n j l)"), ident_bf[:, :])
            ins.then_inc(q_qTp.sem, 1)

        def pe_max(pe, b, par, units, first):
            for n in units:
                k, h, nh = max_units[n]
                pe.wait_ge(q_qT.sem, q_qT.at(b, 2 * k + 2))
                if n >= 2:
                    pe.wait_ge(q_mx.sem, q_mx.at(b, n - 1))
                elif not first:
                    pe.wait_ge(q_x.sem, q_x.at(b - 1, 0))
                w = P * (k + 1)
                for hh in range(nh):
                    at = psM2[n % 2][:, hh * w:(hh + 1) * w]
                    nc.tensor.matmul(at, qT[:, par, h + hh, k * P:(k + 1) * P], kTm[:, 0:w], start=True, stop=False)
                    ins = nc.tensor.matmul(at[:, w - P:w], ident_bf[:, :], mask_qk[:, :], start=False, stop=True)
                ins.then_inc(q_smp.sem, 1)

        def pe_shift(pe, b, front):
            pe.wait_ge(q_mpart.sem, q_mpart.at(b, 5))
            if front:
                pe.wait_ge(q_qkv.sem, q_qkv.at(b + 1, 2))
            waits_end(pe)
            for k in range(NT):
                ins = nc.tensor.transpose(bank[0][:, :].bitcast(BF16)[0:PARTS * HEADS, k * P:(k + 1) * P],
                                          mp[:, k].rearrange("p n h -> p (n h)"), ident_bf[:, :])
            ins.then_inc(q_mTp.sem, 1)

        def pe_scores(pe, b, par, step, halves=(0, 1)):
            qd, j = divmod(step, NT)
            w = T - P * j
            if step == 0:
                pe.wait_ge(q_mrow.sem, q_mrow.at(b, PARTS))
            for half in halves:
                n = 2 * step + half
                pe.wait_ge(q_p.sem, q_p.at(b, n - 1 if n >= 2 else 0))
                for hh in range(2):
                    h = 4 * qd + 2 * half + hh
                    at = psE[half][:, hh * 512:hh * 512 + w]
                    nc.tensor.matmul(at, kTe[:, par, j * P:(j + 1) * P], qT[:, par, h, j * P:T], start=True, stop=False)
                    ins = nc.tensor.matmul(at[:, 0:P], ident_bf[:, :], mask_kq[:, :], start=False, stop=True)
                ins.then_inc(q_sp.sem, 1)

        def pe_values(pe, b, par, step):
            qd, j = divmod(step, NT)
            w = T - P * j
            pe.wait_ge(q_p.sem, q_p.at(b, 2 * step + 2))
            if j == 0:
                pe.wait_ge(q_v.sem, q_v.at(b, 1))
                pe.wait_ge(q_o.sem, q_o.at(b, qd))
            for g in range(4):
                ins = nc.tensor.matmul(psO[32 * g:32 * g + 32, j * P:T], vx[:, par, j, :],
                                       pexp[:, (2 * step + g // 2) % 4, g % 2, 0:w], start=j == 0, stop=j == NT - 1)
            ins.then_inc(q_av.sem, 1)

        def pe_back(pe, b, tiles, last):
            for k in tiles:
                pe.wait_ge(q_o.sem, q_o.at(b, NQ))
                if k >= 2:
                    pe.wait_ge(q_y.sem, q_y.at(b, k - 1))
                else:
                    pe.wait_ge(q_mx.sem, q_mx.at(b + (1 if last else 2), 0))
                for qd in range(NQ):
                    ins = nc.tensor.transpose(psM2[k % 2][:, qd * P:(qd + 1) * P], oT[:, qd, k * P:(k + 1) * P], ident)
                ins.then_inc(q_oTp.sem, 1)

        def pe_yT(pe, b):
            pe.wait_ge(q_y.sem, q_y.at(b, NT))
            for k in range(NT):
                ins = nc.tensor.transpose(psM2[0][:, k * P:(k + 1) * P], y2[:, k, :], ident)
            ins.then_inc(q_yTp.sem, 1)

        def pe_project(pe, b):
            pe.wait_ge(q_yT.sem, q_yT.at(b, 1))
            for k in range(NT):
                ins = nc.tensor.matmul(psM2[1][:, k * D:(k + 1) * D], y2T[:, k * P:(k + 1) * P], wp_sb[:, :],
                                       start=True, stop=True)
            ins.then_inc(q_prp.sem, 1)

        def pe_turn(pe, b, par, tail=True, middle=True, front=True):
            if middle:
                pe_kT(pe, b + 1)
                pe_qT(pe, b + 1, 0)
            if tail:
                pe_back(pe, b - 1, (0, 1), False)
            if middle:
                pe_qT(pe, b + 1, 1)
            if tail:
                pe_back(pe, b - 1, (2, 3), False)
            pe_scores(pe, b, par, 0)
            for s in range(STEPS):
                for half in range(2):
                    if s + 1 < STEPS:
                        pe_scores(pe, b, par, s + 1, (half,))
                    if middle and 2 * s + 2 + half < 2 * NT:
                        pe_qT(pe, b + 1, 2 * s + 2 + half)
                    if middle:
                        pe_max(pe, b + 1, 1 - par, max_unit(s, half), False)
                if tail and s == BACK_T_STEP:
                    pe_yT(pe, b - 1)
                if tail and s == PROJECT_STEP:
                    pe_project(pe, b - 1)
                if front and s == XT_STEP:
                    pe_xT(pe, b + 2)
                if front and s in QKV_STEPS:
                    pe_qkv(pe, b + 2, QKV_STEPS.index(s))
                if middle:
                    pe_max(pe, b + 1, 1 - par, max_unit(s, 2), False)
                if middle and s == SHIFT_T_STEP:
                    pe_shift(pe, b + 1, front)
                pe_values(pe, b, par, s)
                if middle:
                    pe_max(pe, b + 1, 1 - par, max_unit(s, 3), False)

        def mqa_pe(pe):
            pe.wait_ge(q_init.sem, q_init.total(2))
            pe_xT(pe, 0, first=True)
            for r in range(2):
                pe_qkv(pe, 0, r)
            pe_xT(pe, 1, first=True)
            for r in range(2):
                pe_qkv(pe, 1, r)
            pe_kT(pe, 0, first=True)
            for u in range(2 * NT):
                pe_qT(pe, 0, u)
                if u % 2:
                    pe_max(pe, 0, 0, [n for n in range(NM) if max_units[n][0] == u // 2], True)
            pe_shift(pe, 0, True)
            pe_turn(pe, 0, 0, tail=False)
            pe_turn(pe, 1, 1)
            with nc.tensor.Fori(1, B // 2 - 1) as i:
                pe_turn(pe, 2 * i, 0)
                pe_turn(pe, 2 * i + 1, 1)
            pe_turn(pe, B - 2, 0, front=False)
            pe_turn(pe, B - 1, 1, middle=False, front=False)
            pe_back(pe, B - 1, range(NT), True)
            pe_yT(pe, B - 1)
            pe_project(pe, B - 1)

        F = lambda name, per=1, step=1: signal("filter_" + name, per, step)
        f_xln, f_xTp, f_xT, f_yp, f_b, f_x, f_out = (F("xln", NT), F("xT_psum"), F("xT"), F("y_psum"), F("biased"),
                                                     F("x_updated"), F("stored", 1, 16))
        new_stage()
        fx = scratch("fx", [P, 2, NT, D])
        fxT = scratch("fxT", [P, 2, T])
        psFT, psFY = (bank[0], bank[2]), (bank[1], bank[7])

        def dve_filter_xln(dve, b, par, first=False):
            if not first:
                dve.wait_ge(f_xTp.sem, f_xTp.at(b - 1, 0))
            for k in range(NT):
                nc.vector.tensor_scalar(fx[:, par, k, :], x_sb[:, b, k, :], mv[:, b, k, 0:1],
                                        rstd[:, b, k:k + 1], ALU.subtract, ALU.mult).then_inc(f_xln.sem, 1)

        def dve_filter_residual(dve, b, par):
            dve.wait_ge(f_yp.sem, f_yp.at(b, 1))
            dve.wait_ge(f_b.sem, f_b.at(b, 1))
            nc.vector.tensor_tensor(x_sb[:, b], x_sb[:, b], psFY[par][:, :].rearrange("p (k d) -> p k d", d=D),
                                    ALU.add).then_inc(f_x.sem, 1)

        def filter_dve(dve):
            dve_filter_xln(dve, 0, 0, first=True)
            dve_filter_xln(dve, 1, 1, first=True)
            with nc.vector.Fori(0, B // 2 - 1) as i:
                for par in range(2):
                    dve_filter_residual(dve, 2 * i + par, par)
                    dve_filter_xln(dve, 2 * i + par + 2, par)
            for par in range(2):
                dve_filter_residual(dve, B - 2 + par, par)

        def filter_pool(pool):
            with nc.gpsimd.Fori(0, B) as i:
                pool.wait_ge(f_xln.sem, f_xln.at(i, NT))
                nc.gpsimd.tensor_tensor(x_sb[:, i], x_sb[:, i], fb_sb[:, :].unsqueeze(1).broadcast_to([P, NT, D]),
                                        ALU.add).then_inc(f_b.sem, 1)

        def filter_act(act):
            with nc.scalar.Fori(0, B // 2) as i:
                for par in range(2):
                    act.wait_ge(f_xTp.sem, f_xTp.at(2 * i + par, 1))
                    act.wait_ge(f_yp.sem, f_yp.at(2 * i, 0))
                    nc.scalar.activation(fxT[:, par, :], psFT[par][:, :], ACT.Copy).then_inc(f_xT.sem, 1)

        def pe_filter_xT(pe, b, par, first=False):
            pe.wait_ge(f_xln.sem, f_xln.at(b, NT))
            if not first:
                pe.wait_ge(f_xT.sem, f_xT.at(b - 1, 0))
            for k in range(NT):
                ins = nc.tensor.transpose(psFT[par][:, k * P:(k + 1) * P], fx[:, par, k, :], ident)
            ins.then_inc(f_xTp.sem, 1)

        def pe_filter_product(pe, b, par, first=False):
            pe.wait_ge(f_xT.sem, f_xT.at(b, 1))
            if not first:
                pe.wait_ge(f_x.sem, f_x.at(b - 1, 0))
            for k in range(NT):
                ins = nc.tensor.matmul(psFY[par][:, k * D:(k + 1) * D], fxT[:, par, k * P:(k + 1) * P], m_sb[:, :],
                                       start=True, stop=True)
            ins.then_inc(f_yp.sem, 1)

        def filter_pe(pe):
            pe_filter_xT(pe, 0, 0, first=True)
            pe_filter_xT(pe, 1, 1, first=True)
            pe_filter_product(pe, 0, 0, first=True)
            pe_filter_product(pe, 1, 1, first=True)
            with nc.tensor.Fori(1, B // 2) as i:
                for par in range(2):
                    pe_filter_xT(pe, 2 * i + par, par)
                for par in range(2):
                    pe_filter_product(pe, 2 * i + par, par)

        def filter_sync(sp):
            with nc.sync.Fori(0, B) as i:
                sp.wait_ge(f_x.sem, f_x.at(i, 1))
                sp.dma_start(out[i].rearrange("(k p) d -> p k d", p=P), x_sb[:, i]).then_inc(f_out.sem, 16)
            sp.wait_ge(f_out.sem, f_out.total(16 * B))

        block = ctx.enter_context(nc.Block())

        @block.sync
        def _(sp):
            prep_sync(sp)
            start_signals(sp)
            route_sync(sp)
            moe_sync(sp)
            mqa_sync(sp)
            filter_sync(sp)

        @block.scalar
        def _(act):
            prep_act(act)
            ln1.act_std(act)
            lin_act(act)
            ln2.act_std(act)
            route_act(act)
            moe_act(act)
            ln3.act_std(act)
            mqa_act(act)
            ln4.act_std(act)
            filter_act(act)

        @block.tensor
        def _(pe):
            prep_pe(pe)
            lin_pe(pe)
            route_pe(pe)
            moe_pe(pe)
            mqa_pe(pe)
            filter_pe(pe)

        @block.vector
        def _(dve):
            dve.wait_ge(s_x.sem, s_x.total(16 * B))
            with nc.vector.Fori(0, B) as i:
                ln1.dve_sequence(dve, i)
            ln1.dve_rstd(dve)
            prep_dve(dve)
            lin_dve(dve)
            ln2.dve_rstd(dve)
            route_dve(dve)
            moe_dve(dve)
            ln3.dve_rstd(dve)
            mqa_dve(dve)
            ln4.dve_rstd(dve)
            filter_dve(dve)

        @block.gpsimd
        def _(pool):
            lin_pool(pool)
            moe_pool(pool)
            mqa_pool(pool)
            filter_pool(pool)


def constants():
    import numpy as np
    n = np.arange(P)
    angle = 2.0 * np.pi * ((n[:, None] * n[None, :]) % P) / P
    head = n // 8
    parts = {
        "ident": np.eye(P),
        "tri": n[:, None] <= n[None, :],
        "ones": np.ones((P, P)),
        "dft_c": np.cos(angle),
        "dft_s": np.sin(angle),
        "dft_ns": -np.sin(angle),
        "blockdiag": head[:, None] == head[None, :],
        "causal_qk": np.where(n[:, None] < n[None, :], NEG, 0.0),
        "causal_kq": np.where(n[:, None] > n[None, :], NEG, 0.0),
        "slots": np.broadcast_to(np.arange(P + 1)[None, :], (P, P + 1)),
        "slot_row": n[:, None],
        "seqmask": ((n[:, None] % 64) // 8) == np.arange(8)[None, :],
        "shift_rows": ((n >= 72) & (n < 75))[:, None],
    }
    layout, at = {}, 0
    for name, a in parts.items():
        layout[name] = (at, a.shape[1])
        at += a.shape[1]
    layout["width"] = at
    return layout, np.concatenate([np.asarray(a, np.float32) for a in parts.values()], axis=1)


_INS = ["L0_attn_x", "L0_attn_w", "L0_attn_w_out", "L0_ffn_router_w", "L0_ffn_w1", "L0_ffn_b1", "L0_ffn_w2",
        "L0_ffn_b2", "L1_attn_w_attn", "L1_attn_w_proj", "L1_ffn_w_freq_real", "L1_ffn_w_freq_imag",
        "L1_ffn_bias"]


def kernel(**inputs):
    import numpy as np
    import concourse.bacc as bacc
    from concourse.bass_utils import run_bass_kernel_spmd

    nc = bacc.Bacc("TRN2", target_bir_lowering=False, num_devices=1)
    layout, table = constants()
    arrays, args = {}, []
    for name in _INS:
        arrays[f"in_{name}"] = np.ascontiguousarray(inputs[name])
    arrays["constants"] = table
    for name, a in arrays.items():
        args.append(nc.dram_tensor(name, a.shape, mybir.dt.from_np(a.dtype), kind="ExternalInput").ap())
    x = arrays["in_L0_attn_x"]
    out = nc.dram_tensor("out_x", x.shape, F32, kind="ExternalOutput").ap()
    build(nc, *args, out, layout)
    return run_bass_kernel_spmd(nc, [arrays], core_ids=[0]).results[0]["out_x"]
```

```python
from contextlib import ExitStack

import concourse.bass as bass
from concourse import mybir

F32 = mybir.dt.float32
BF16 = mybir.dt.bfloat16
ALU = mybir.AluOpType
ACT = mybir.ActivationFunctionType
AX = mybir.AxisListType

P = 128
HEADS = 16
EPS = 1e-5
NEG = -1.0e30
PARTS = 3


class Signal:

    START = 1

    def __init__(self, sem, per, step=1):
        self.sem, self.per, self.step = sem, per, step

    def at(self, turn, nth):
        return turn * (self.per * self.step) + (nth * self.step + self.START)

    def total(self, raised):
        return raised + self.START


def build(nc, x_in, w_qkv, w_out, router_w, w1, b1, w2, b2, w_attn, w_proj, wf_re, wf_im, f_bias,
          consts, out, layout):
    B, T, D = x_in.shape
    E, _, H = w1.shape
    NT = T // P
    L = D // HEADS
    CAP = max(1, int(T * 2.0 / E) + 1)
    HC = H // P
    SCALE = float(L) ** -0.5
    BE = B * E
    GC = 344
    assert CAP == P + 1 and D == P and E * CAP == 3 * GC and BE == 64
    QR = PARTS * PARTS * L
    NQ = HEADS // 4

    with ExitStack() as ctx:
        def sb(name, shape, dt=F32):
            return ctx.enter_context(nc.sbuf_tensor(name, shape, dt))

        made = []

        def signal(name, per=1, step=1):
            made.append(Signal(ctx.enter_context(nc.semaphore(name)), per, step))
            return made[-1]

        def psum(name, banks):
            return ctx.enter_context(nc.psum_tensor(name, [P, 512 * banks], F32))

        bank = {i: psum(f"bank{i}", 1) for i in (0, 1, 2, 7)}
        wide, wide2 = psum("wide", 2), psum("wide2", 2)
        bank[5], bank[6] = wide2[:, 0:512], wide2[:, 512:1024]

        x_sb = sb("x_sb", [P, B, NT, D])
        cst = sb("cst", [P, layout["width"]])

        def const(name):
            a, n = layout[name]
            return cst[:, a:a + n]

        ident, tri, ones = const("ident"), const("tri"), const("ones")
        dft_c, dft_s, dft_ns = const("dft_c"), const("dft_s"), const("dft_ns")
        blockdiag, seqmask = const("blockdiag"), const("seqmask")
        wq_raw = sb("wq_raw", [P, 3, D])
        wqT = sb("wqT", [P, 3 * D])
        wo_sb = sb("wo_sb", [P, D])
        r_raw = sb("r_raw", [E, D])
        rT = sb("rT", [P, E])
        w1_sb = sb("w1_sb", [P, E, H])
        w2_sb = sb("w2_sb", [P, E, HC, D])
        b1_raw = sb("b1_raw", [E * HC, P])
        b1T = sb("b1T", [P, E * HC])
        b2rep = sb("b2rep", [P, D])
        wa_sb = sb("wa_sb", [P, D + 2 * L])
        wp_sb = sb("wp_sb", [P, D])
        wf_sb = sb("wf_sb", [P, 2, D])
        fb_sb = sb("fb_sb", [P, D])
        a12 = sb("a12", [P, 2, D])
        m_sb = sb("m_sb", [P, D])
        ident_bf = sb("ident_bf", [P, P], BF16)

        sc_part = sb("sc_part", [P, NT, B, E, PARTS], BF16)
        posT = sb("posT", [P, NT, B, E])
        rest_l = sb("rest_l", [P, T])

        st6 = sb("st6", [P, NT, 6])
        mvt = sb("mvt", [P, NT, 2])
        mv = sb("mv", [P, B, NT, 2])
        sd = sb("sd", [P, B, NT])
        rstd = sb("rstd", [P, B, NT])
        xln = sb("xln", [P, NT, D])
        xT = sb("xT", [P, T])

        x_rest = sb("x_rest", [P, NT, D])
        x_part = sb("x_part", [P, 2, PARTS, NT, D], BF16)

        passed = signal("waits_passed")

        def waits_end(engine):
            engine.sem_inc(passed.sem, 1)

        stage = [ExitStack()]

        def new_stage():
            stage[0].close()
            stage[0] = ctx.enter_context(ExitStack())

        def scratch(name, shape, dt=F32):
            return stage[0].enter_context(nc.sbuf_tensor(name, shape, dt))

        s_x = signal("x_loaded", 1, 16)
        s_w = signal("weights_loaded", 1, 16)
        s_we = signal("expert_weights_loaded", 1, 16)
        s_c = signal("consts_loaded", 1, 16)

        NW = 9
        NWE = 2 + B
        s_prep_t = signal("prep_transposed")
        s_prep_v = signal("prep_evacuated")
        s_idb = signal("ident_bf_ready")

        s_started = ctx.enter_context(nc.semaphore("signals_started"))

        def start_signals(pool):
            for s in made:
                pool.sem_inc(s.sem, Signal.START)
            pool.sem_inc(s_started, 1)

        def prep_sync(sp):
            sp.dma_start(cst[:, :], consts).then_inc(s_c.sem, 16)
            for b in range(B):
                sp.dma_start(x_sb[:, b], x_in[b].rearrange("(k p) d -> p k d", p=P)).then_inc(s_x.sem, 16)
            for dst, src in (
                (w1_sb[:, :, :], w1.rearrange("e d h -> d e h")),
                (w2_sb[:, :, :, :].rearrange("p e c d -> p (e c) d"),
                 w2.rearrange("e (c p) d -> p (e c) d", p=P)),
            ):
                sp.dma_start(dst, src).then_inc(s_we.sem, 16)
            for b in range(B):
                sp.dma_start(b2rep[BE + b * E:BE + (b + 1) * E, :], b2).then_inc(s_we.sem, 16)

        def prep_act(q):
            for dst, src in (
                (wq_raw[:, :, :], w_qkv.rearrange("(g p) d -> p g d", p=P)),
                (wo_sb[:, :], w_out),
                (r_raw[:, :], router_w),
                (b1_raw[:, :], b1.rearrange("e (c p) -> (e c) p", p=P)),
                (wf_sb[:, 0, :], wf_re),
                (wf_sb[:, 1, :], wf_im),
                (wa_sb[:, :], w_attn),
                (wp_sb[:, :], w_proj),
                (fb_sb[:, :], f_bias.rearrange("(a d) -> a d", a=1).broadcast_to([P, D])),
            ):
                q.dma_start(dst, src).then_inc(s_w.sem, 16)

        def prep_pe(pe):
            pe.wait_ge(s_started, 1)
            pe.wait_ge(s_c.sem, s_c.total(16))
            pe.wait_ge(s_w.sem, s_w.total(16 * NW))
            for g in range(3):
                nc.tensor.transpose(bank[0][:, g * D:(g + 1) * D], wq_raw[:, g, :], ident)
            nc.tensor.transpose(bank[1][:, 0:E], r_raw[:, :], ident[0:E, 0:E])
            nc.tensor.transpose(bank[1][:, 64:64 + E * HC], b1_raw[:, :], ident[0:E * HC, 0:E * HC])
            re, im = wf_sb[:, 0, :], wf_sb[:, 1, :]
            nc.tensor.matmul(bank[2][:, 0:D], re, dft_c, start=True, stop=False)
            nc.tensor.matmul(bank[2][:, 0:D], im, dft_s, start=False, stop=True)
            nc.tensor.matmul(bank[2][:, D:2 * D], im, dft_c, start=True, stop=False)
            nc.tensor.matmul(bank[2][:, D:2 * D], re, dft_ns, start=False, stop=True).then_inc(s_prep_t.sem, 1)
            pe.wait_ge(s_prep_v.sem, s_prep_v.total(4))
            nc.tensor.matmul(bank[5][:, 0:D], a12[:, 0, :], dft_c, start=True, stop=False)
            nc.tensor.matmul(bank[5][:, 0:D], a12[:, 1, :], dft_ns, start=False, stop=True).then_inc(s_prep_t.sem, 1)

        def prep_dve(dve):
            dve.wait_ge(s_c.sem, s_c.total(16))
            nc.vector.tensor_copy(ident_bf[:, :], ident).then_inc(s_idb.sem, 1)
            dve.wait_ge(s_prep_t.sem, s_prep_t.total(1))
            nc.vector.tensor_copy(wqT[:, :], bank[0][:, 0:3 * D]).then_inc(s_prep_v.sem, 1)
            nc.vector.tensor_copy(rT[:, :], bank[1][:, 0:E]).then_inc(s_prep_v.sem, 1)
            nc.vector.tensor_copy(b1T[:, :], bank[1][:, 64:64 + E * HC]).then_inc(s_prep_v.sem, 1)
            nc.vector.tensor_copy(a12[:, :, :].rearrange("p a d -> p (a d)"),
                                  bank[2][:, 0:2 * D]).then_inc(s_prep_v.sem, 1)
            dve.wait_ge(s_prep_t.sem, s_prep_t.total(2))
            nc.vector.tensor_scalar(m_sb[:, :], bank[5][:, 0:D], 1.0 / D, None, ALU.mult).then_inc(s_prep_v.sem, 1)

        class LayerNorm:

            def __init__(self, tag):
                self.six = signal(f"{tag}_bn_stats")
                self.agg = signal(f"{tag}_bn_aggr")
                self.mv = signal(f"{tag}_mean_var")
                self.ve = signal(f"{tag}_var_eps")
                self.sd = signal(f"{tag}_std")
                self.rstd = signal(f"{tag}_rstd")

            def dve_sequence(self, dve, i):
                dve.wait_ge(self.agg.sem, self.agg.at(i, 0))
                waits_end(dve)
                for k in range(NT):
                    ins = nc.vector.bn_stats(st6[:, k, :], x_sb[:, i, k, :])
                ins.then_inc(self.six.sem, 1)
                dve.wait_ge(self.six.sem, self.six.at(i, 1))
                dve.wait_ge(self.mv.sem, self.mv.at(i, 0))
                waits_end(dve)
                for k in range(NT):
                    ins = nc.vector.bn_aggr(mvt[:, k, :], st6[:, k, :])
                ins.then_inc(self.agg.sem, 1)
                dve.wait_ge(self.agg.sem, self.agg.at(i, 1))
                nc.vector.tensor_copy(mv[:, i, :, :], mvt[:, :, :]).then_inc(self.mv.sem, 1)

            def dve_rstd(self, dve):
                dve.wait_ge(self.mv.sem, self.mv.total(B))
                nc.vector.tensor_scalar(sd[:, :, :], mv[:, :, :, 1], EPS, None, ALU.add).then_inc(self.ve.sem, 1)
                dve.wait_ge(self.sd.sem, self.sd.total(1))
                nc.vector.reciprocal(rstd[:, :, :], sd[:, :, :]).then_inc(self.rstd.sem, 1)
                dve.wait_ge(self.rstd.sem, self.rstd.total(1))

            def act_std(self, act):
                act.wait_ge(self.ve.sem, self.ve.total(1))
                nc.scalar.activation(sd[:, :, :], sd[:, :, :], ACT.Sqrt).then_inc(self.sd.sem, 1)

        def normalise(s_xln, i):
            for k in range(NT):
                nc.vector.tensor_scalar(xln[:, k, :], x_sb[:, i, k, :], mv[:, i, k, 0:1],
                                                   rstd[:, i, k:k + 1], ALU.subtract, ALU.mult).then_inc(s_xln.sem, 1)

        ln1, ln2, ln3, ln4 = (LayerNorm(f"ln{n}") for n in range(1, 5))

        A = lambda name, per=1: signal("lin_" + name, per)
        a_xln, a_xTp, a_xT = A("xln", NT), A("xT_psum"), A("xT")
        a_qkv, a_qv, a_kx, a_kxe = A("qkv_psum", NT), A("qv", NT), A("exp_k", NT), A("exp_k_eps")
        a_qmax, a_qc, a_qe, a_qsum = A("q_max"), A("q_shifted"), A("q_exp"), A("q_sum")
        a_kn, a_den, a_rden, a_qs = A("k_norm_psum"), A("denominator"), A("denominator_inverse"), A("q_soft")
        a_kv, a_cum, a_prod, a_red = A("outer", NT), A("outer_sums_psum", NT), A("q_times_sums", NT), A("y_intra", NT)
        a_stp, a_st = A("state_psum"), A("state")
        a_qsTp, a_qsT, a_yTp, a_yT = A("q_soft_T_psum"), A("q_soft_T"), A("yT_psum"), A("yT")
        a_o, a_x = A("projected_psum"), A("x_updated")

        new_stage()
        qv = scratch("qv", [P, 2, 2, NT, D])
        kx = scratch("kx", [P, 2, NT, D])
        qmax = scratch("qmax", [P, NT * HEADS])
        q_sh = scratch("q_sh", [P, NT, D])
        qe = scratch("qe", [P, NT, D])
        qsum = scratch("qsum", [P, NT * HEADS])
        den = scratch("den", [P, NT, D])
        qs = scratch("qs", [P, NT, D])
        kv = scratch("kv", [P, 2, HEADS * L * L])
        prod = scratch("prod", [P, 2, HEADS * L * L])
        state = scratch("state", [P, NT - 1, D])
        tT = scratch("tT", [P, T])
        yT = scratch("yT", [P, T])
        y_in = scratch("y_in", [P, NT, D])
        by_head = lambda ap: ap.rearrange("p k (h l) -> p (k h) l", l=L)
        psT, psN, psS, psY = bank[0], bank[5], bank[6], bank[7]
        psQ = (bank[1], bank[2])


        def dve_lin_qmax(dve, b, par):
            dve.wait_ge(a_qv.sem, a_qv.at(b, NT))
            dve.wait_ge(a_qc.sem, a_qc.at(b, 0))
            nc.vector.tensor_reduce(qmax[:, :], by_head(qv[:, par, 0, :, :]), AX.X, ALU.max).then_inc(a_qmax.sem, 1)

        def dve_lin_qsum(dve, b):
            dve.wait_ge(a_qe.sem, a_qe.at(b, 1))
            dve.wait_ge(a_den.sem, a_den.at(b, 0))
            nc.vector.tensor_reduce(qsum[:, :], by_head(qe[:, :, :]), AX.X, ALU.add).then_inc(a_qsum.sem, 1)

        def dve_lin_den(dve, b):
            dve.wait_ge(a_kn.sem, a_kn.at(b, 1))
            dve.wait_ge(a_qsum.sem, a_qsum.at(b, 1))
            dve.wait_ge(a_qs.sem, a_qs.at(b, 0))
            nc.vector.tensor_tensor(by_head(den[:, :, :]), psN[:, :].rearrange("p (kh l) -> p kh l", l=L),
                                    qsum[:, :].unsqueeze(2).broadcast_to([P, NT * HEADS, L]),
                                    ALU.mult).then_inc(a_den.sem, 1)
            dve.wait_ge(a_den.sem, a_den.at(b, 1))
            nc.vector.reciprocal(den[:, :, :], den[:, :, :]).then_inc(a_rden.sem, 1)

        def dve_lin_xln(dve, b):
            dve.wait_ge(a_xTp.sem, a_xTp.at(b, 0))
            normalise(a_xln, b)

        def dve_lin_prod(dve, b, k):
            dve.wait_ge(a_cum.sem, a_cum.at(b, k + 1))
            dve.wait_ge(a_qs.sem, a_qs.at(b, 1))
            dve.wait_ge(a_red.sem, a_red.at(b, k - 1 if k >= 2 else 0))
            nc.vector.tensor_tensor(
                prod[:, k % 2, :].rearrange("p (hl m) -> p hl m", m=L),
                wide[:, :].rearrange("p (hl m) -> p hl m", m=L),
                qs[:, k, :].unsqueeze(2).broadcast_to([P, D, L]), ALU.mult).then_inc(a_prod.sem, 1)

        def dve_lin_reduce(dve, b, k):
            dve.wait_ge(a_prod.sem, a_prod.at(b, k + 1))
            if k == 0:
                dve.wait_ge(a_yTp.sem, a_yTp.at(b, 0))
            nc.vector.tensor_reduce(
                y_in[:, k, :].rearrange("p (h m) -> p h m", m=L),
                prod[:, k % 2, :].rearrange("p (h l m) -> p h m l", l=L, m=L), AX.X, ALU.add).then_inc(a_red.sem, 1)

        def dve_lin_state(dve, b):
            dve.wait_ge(a_stp.sem, a_stp.at(b, 1))
            dve.wait_ge(a_yTp.sem, a_yTp.at(b, 0))
            nc.vector.tensor_tensor(state[:, :, :], psS[:, 0:(NT - 1) * D].rearrange("p (k d) -> p k d", d=D),
                                    blockdiag.unsqueeze(1).broadcast_to([P, NT - 1, D]), ALU.mult).then_inc(a_st.sem, 1)

        def dve_lin_residual(dve, b):
            dve.wait_ge(a_o.sem, a_o.at(b, 1))
            nc.vector.tensor_tensor(x_sb[:, b, :, :], x_sb[:, b, :, :],
                                    psN[:, :].rearrange("p (k d) -> p k d", d=D), ALU.add).then_inc(a_x.sem, 1)

        def dve_lin_stats(dve, b):
            dve.wait_ge(a_x.sem, a_x.at(b, 1))
            ln2.dve_sequence(dve, b)

        def dve_lin_turn(dve, b, par, tail=True, front=True, ahead=True):
            dve_lin_prod(dve, b, 0)
            dve_lin_reduce(dve, b, 0)
            if tail:
                dve_lin_residual(dve, b - 1)
            dve_lin_prod(dve, b, 1)
            dve_lin_reduce(dve, b, 1)
            if tail:
                dve_lin_stats(dve, b - 1)
            dve_lin_prod(dve, b, 2)
            dve_lin_state(dve, b)
            if front:
                dve_lin_qmax(dve, b + 1, 1 - par)
            dve_lin_reduce(dve, b, 2)
            if ahead:
                dve_lin_xln(dve, b + 2)
            dve_lin_prod(dve, b, 3)
            dve_lin_reduce(dve, b, 3)
            if front:
                dve_lin_qsum(dve, b + 1)
                dve_lin_den(dve, b + 1)

        def lin_dve(dve):
            dve_lin_xln(dve, 0)
            dve_lin_qmax(dve, 0, 0)
            dve_lin_xln(dve, 1)
            dve_lin_qsum(dve, 0)
            dve_lin_den(dve, 0)
            dve_lin_turn(dve, 0, 0, tail=False)
            dve_lin_turn(dve, 1, 1)
            with nc.vector.Fori(1, B // 2 - 1) as i:
                dve_lin_turn(dve, 2 * i, 0)
                dve_lin_turn(dve, 2 * i + 1, 1)
            dve_lin_turn(dve, B - 2, 0, ahead=False)
            dve_lin_turn(dve, B - 1, 1, front=False, ahead=False)
            dve_lin_residual(dve, B - 1)
            dve_lin_stats(dve, B - 1)
            dve.wait_ge(a_x.sem, a_x.total(B))

        def act_lin_xT(act, b):
            act.wait_ge(a_xTp.sem, a_xTp.at(b, 1))
            act.wait_ge(a_qkv.sem, a_qkv.at(b, 0))
            nc.scalar.activation(xT[:, :], psT[:, :], ACT.Copy).then_inc(a_xT.sem, 1)

        def act_lin_kx_qv(act, b, par, k, first=False):
            act.wait_ge(a_qkv.sem, a_qkv.at(b, k + 1))
            if k == 0 and not first:
                act.wait_ge(a_kv.sem, a_kv.at(b - 1, 0))
                act.wait_ge(a_stp.sem, a_stp.at(b - 1, 0))
                act.wait_ge(a_kn.sem, a_kn.at(b - 1, 0))
                act.wait_ge(a_qc.sem, a_qc.at(b - 1, 0))
            psq = psQ[k % 2][:, 0:3 * D].rearrange("p (g d) -> p g d", g=3)
            nc.scalar.activation(kx[:, par, k, :], psq[:, 1, :], ACT.Exp, scale=SCALE).then_inc(a_kx.sem, 1)
            nc.scalar.activation(qv[:, par, :, k, :], psq[:, 0:3:2, :], ACT.Copy).then_inc(a_qv.sem, 1)

        def act_lin_qe(act, b):
            act.wait_ge(a_qc.sem, a_qc.at(b, 1))
            act.wait_ge(a_qs.sem, a_qs.at(b, 0))
            nc.scalar.activation(qe[:, :, :], q_sh[:, :, :], ACT.Exp, scale=SCALE).then_inc(a_qe.sem, 1)

        def act_lin_qsT(act, b):
            act.wait_ge(a_qsTp.sem, a_qsTp.at(b, 1))
            act.wait_ge(a_yTp.sem, a_yTp.at(b, 0))
            nc.scalar.activation(tT[:, 0:(NT - 1) * P], psT[:, 0:(NT - 1) * P], ACT.Copy).then_inc(a_qsT.sem, 1)

        def act_lin_yT(act, b):
            act.wait_ge(a_yTp.sem, a_yTp.at(b, 1))
            act.wait_ge(a_o.sem, a_o.at(b, 0))
            nc.scalar.activation(yT[:, :], psY[:, :], ACT.Copy).then_inc(a_yT.sem, 1)

        def act_lin_turn(act, b, par, tail=True, front=True):
            if front:
                act_lin_xT(act, b + 1)
            if tail:
                act_lin_yT(act, b - 1)
            if front:
                for k in range(NT):
                    act_lin_kx_qv(act, b + 1, 1 - par, k)
            act_lin_qsT(act, b)
            if front:
                act_lin_qe(act, b + 1)

        def lin_act(act):
            act_lin_xT(act, 0)
            for k in range(NT):
                act_lin_kx_qv(act, 0, 0, k, first=True)
            act_lin_qe(act, 0)
            act_lin_turn(act, 0, 0, tail=False)
            act_lin_turn(act, 1, 1)
            with nc.scalar.Fori(1, B // 2 - 1) as i:
                act_lin_turn(act, 2 * i, 0)
                act_lin_turn(act, 2 * i + 1, 1)
            act_lin_turn(act, B - 2, 0)
            act_lin_turn(act, B - 1, 1, front=False)
            act_lin_yT(act, B - 1)

        def pool_lin_keys(pool, b, par):
            pool.wait_ge(a_kx.sem, a_kx.at(b, NT))
            waits_end(pool)
            nc.gpsimd.tensor_scalar(kx[:, par], kx[:, par], 1e-6, None, ALU.add).then_inc(a_kxe.sem, 1)

        def pool_lin_shift(pool, b, par):
            pool.wait_ge(a_qmax.sem, a_qmax.at(b, 1))
            pool.wait_ge(a_qv.sem, a_qv.at(b, NT))
            pool.wait_ge(a_qe.sem, a_qe.at(b, 0))
            nc.gpsimd.tensor_tensor(by_head(q_sh[:, :, :]), by_head(qv[:, par, 0, :, :]),
                                    qmax[:, :].unsqueeze(2).broadcast_to([P, NT * HEADS, L]),
                                    ALU.subtract).then_inc(a_qc.sem, 1)

        def pool_lin_qs(pool, b):
            pool.wait_ge(a_rden.sem, a_rden.at(b, 1))
            pool.wait_ge(a_prod.sem, a_prod.at(b, 0))
            pool.wait_ge(a_qsTp.sem, a_qsTp.at(b, 0))
            nc.gpsimd.tensor_tensor(qs[:, :, :], qe[:, :, :], den[:, :, :], ALU.mult).then_inc(a_qs.sem, 1)

        def pool_lin_outer(pool, b, par, k, first=False):
            pool.wait_ge(a_kxe.sem, a_kxe.at(b, 1))
            pool.wait_ge(a_qv.sem, a_qv.at(b, NT))
            if k >= 2:
                pool.wait_ge(a_cum.sem, a_cum.at(b, k - 1))
            elif not first:
                pool.wait_ge(a_cum.sem, a_cum.at(b - 1, NT + k - 1))
            shape = [P, HEADS, L, L]
            nc.gpsimd.tensor_tensor(
                kv[:, k % 2, :].rearrange("p (h l m) -> p h l m", l=L, m=L),
                kx[:, par, k, :].rearrange("p (h l) -> p h l", l=L).unsqueeze(3).broadcast_to(shape),
                qv[:, par, 1, k, :].rearrange("p (h m) -> p h m", m=L).unsqueeze(2).broadcast_to(shape),
                ALU.mult).then_inc(a_kv.sem, 1)

        def pool_lin_turn(pool, b, par, front=True):
            pool_lin_qs(pool, b)
            pool_lin_outer(pool, b, par, 2)
            pool_lin_outer(pool, b, par, 3)
            if front:
                pool_lin_keys(pool, b + 1, 1 - par)
                pool_lin_shift(pool, b + 1, 1 - par)
                pool_lin_outer(pool, b + 1, 1 - par, 0)
                pool_lin_outer(pool, b + 1, 1 - par, 1)

        def lin_pool(pool):
            pool_lin_keys(pool, 0, 0)
            pool_lin_shift(pool, 0, 0)
            pool_lin_outer(pool, 0, 0, 0, first=True)
            pool_lin_outer(pool, 0, 0, 1, first=True)
            with nc.gpsimd.Fori(0, B // 2 - 1) as i:
                pool_lin_turn(pool, 2 * i, 0)
                pool_lin_turn(pool, 2 * i + 1, 1)
            pool_lin_turn(pool, B - 2, 0)
            pool_lin_turn(pool, B - 1, 1, front=False)

        def pe_lin_xT(pe, b, first=False):
            pe.wait_ge(a_xln.sem, a_xln.at(b, NT))
            if not first:
                pe.wait_ge(a_qsT.sem, a_qsT.at(b - 1, 0))
            for k in range(NT):
                ins = nc.tensor.transpose(psT[:, k * P:(k + 1) * P], xln[:, k, :], ident)
            ins.then_inc(a_xTp.sem, 1)

        def pe_lin_qkv(pe, b, k):
            pe.wait_ge(a_xT.sem, a_xT.at(b, 1))
            if k >= 2:
                pe.wait_ge(a_qv.sem, a_qv.at(b, k - 1))
            else:
                pe.wait_ge(a_qv.sem, a_qv.at(b, 0))
            nc.tensor.matmul(psQ[k % 2][:, 0:3 * D], xT[:, k * P:(k + 1) * P], wqT[:, :],
                             start=True, stop=True).then_inc(a_qkv.sem, 1)

        def pe_lin_key_sums(pe, b, par, first=False):
            pe.wait_ge(a_kxe.sem, a_kxe.at(b, 1))
            if not first:
                pe.wait_ge(a_x.sem, a_x.at(b - 1, 0))
            for k in range(NT):
                for j in range(k):
                    nc.tensor.matmul(psN[:, k * D:(k + 1) * D], ones, kx[:, par, j, :], start=j == 0, stop=False)
                ins = nc.tensor.matmul(psN[:, k * D:(k + 1) * D], tri, kx[:, par, k, :], start=k == 0, stop=True)
            ins.then_inc(a_kn.sem, 1)

        def pe_lin_states(pe, b, par):
            pe.wait_ge(a_st.sem, a_st.at(b, 0))
            pe.wait_ge(a_kxe.sem, a_kxe.at(b, 1))
            pe.wait_ge(a_qv.sem, a_qv.at(b, NT))
            for k in range(1, NT):
                for j in range(k):
                    ins = nc.tensor.matmul(psS[:, (k - 1) * D:k * D], kx[:, par, j, :], qv[:, par, 1, j, :],
                                           start=j == 0, stop=j == k - 1)
            ins.then_inc(a_stp.sem, 1)

        def pe_lin_outer_sums(pe, b, k):
            pe.wait_ge(a_kv.sem, a_kv.at(b, k + 1))
            pe.wait_ge(a_prod.sem, a_prod.at(b, k))
            nc.tensor.matmul(wide[:, 0:512], tri, kv[:, k % 2, 0:512], start=True, stop=True)
            nc.tensor.matmul(wide[:, 512:1024], tri, kv[:, k % 2, 512:1024],
                             start=True, stop=True).then_inc(a_cum.sem, 1)

        def pe_lin_qsT(pe, b, front):
            pe.wait_ge(a_qs.sem, a_qs.at(b, 1))
            if front:
                pe.wait_ge(a_xT.sem, a_xT.at(b + 1, 1))
            else:
                pe.wait_ge(a_qsT.sem, a_qsT.at(b, 0))
            for k in range(1, NT):
                ins = nc.tensor.transpose(psT[:, (k - 1) * P:k * P], qs[:, k, :], ident)
            ins.then_inc(a_qsTp.sem, 1)

        def pe_lin_yT(pe, b):
            pe.wait_ge(a_qsT.sem, a_qsT.at(b, 1))
            pe.wait_ge(a_st.sem, a_st.at(b, 1))
            pe.wait_ge(a_red.sem, a_red.at(b, NT))
            pe.wait_ge(a_yT.sem, a_yT.at(b, 0))
            for k in range(NT):
                at = psY[:, k * P:(k + 1) * P]
                if k:
                    nc.tensor.matmul(at, state[:, k - 1, :], tT[:, (k - 1) * P:k * P], start=True, stop=False)
                ins = nc.tensor.matmul(at, y_in[:, k, :], ident, start=k == 0, stop=True)
            ins.then_inc(a_yTp.sem, 1)

        def pe_lin_project(pe, b, last=False):
            pe.wait_ge(a_yT.sem, a_yT.at(b, 1))
            if not last:
                pe.wait_ge(a_den.sem, a_den.at(b + 1, 1))
            for k in range(NT):
                ins = nc.tensor.matmul(psN[:, k * D:(k + 1) * D], yT[:, k * P:(k + 1) * P], wo_sb[:, :],
                                       start=True, stop=True)
            ins.then_inc(a_o.sem, 1)

        def pe_lin_turn(pe, b, par, tail=True, front=True):
            pe_lin_outer_sums(pe, b, 0)
            if front:
                pe_lin_xT(pe, b + 1)
            if tail:
                pe_lin_yT(pe, b - 1)
                pe_lin_project(pe, b - 1)
            if front:
                pe_lin_qkv(pe, b + 1, 0)
                pe_lin_qkv(pe, b + 1, 1)
            pe_lin_outer_sums(pe, b, 1)
            pe_lin_states(pe, b, par)
            if front:
                pe_lin_qkv(pe, b + 1, 2)
                pe_lin_qkv(pe, b + 1, 3)
            pe_lin_outer_sums(pe, b, 2)
            pe_lin_qsT(pe, b, front)
            if front:
                pe_lin_key_sums(pe, b + 1, 1 - par)
            pe_lin_outer_sums(pe, b, 3)

        def lin_pe(pe):
            pe_lin_xT(pe, 0, first=True)
            for k in range(NT):
                pe_lin_qkv(pe, 0, k)
            pe_lin_key_sums(pe, 0, 0, first=True)
            pe_lin_turn(pe, 0, 0, tail=False)
            pe_lin_turn(pe, 1, 1)
            with nc.tensor.Fori(1, B // 2 - 1) as i:
                pe_lin_turn(pe, 2 * i, 0)
                pe_lin_turn(pe, 2 * i + 1, 1)
            pe_lin_turn(pe, B - 2, 0)
            pe_lin_turn(pe, B - 1, 1, front=False)
            pe_lin_yT(pe, B - 1)
            pe_lin_project(pe, B - 1, last=True)

        R = lambda name, per=1, step=1: signal("route_" + name, per, step)
        r_xln, r_xTp, r_xT, r_lgp, r_lg = R("xln", NT), R("xT_psum"), R("xT"), R("logits_psum"), R("logits")
        r_max, r_sub, r_exp, r_sum, r_inv, r_sc = (R("max"), R("shifted"), R("exp"), R("sum"), R("inverse"),
                                                   R("scores"))
        r_scTp, r_scT, r_top, r_rep, r_eq = R("scores_T_psum"), R("scores_T", 2), R("top8"), R("replaced"), R("tie")
        r_run, r_first, r_mask, r_cnt, r_pos = R("tie_count"), R("tie_first"), R("mask"), R("count"), R("pos")
        r_posb, r_posTp, r_posT, r_last = R("pos_bf"), R("pos_T_psum"), R("pos_T"), R("last_slot", 2)
        r_gt, r_moved = R("gates_T"), R("gates_T_moved", 1, 16)
        r_posd = R("pos_in_dram", 1, 16)
        r_part = R("score_parts", 5)

        NR = NT * BE
        new_stage()
        lg = scratch("lg", [P, NT, B, E])
        rmax = scratch("rmax", [P, NT * B])
        sc = scratch("sc", [P, NT, B, E])
        sc_rest = scratch("sc_rest", [P, NT, B, E])
        scT = scratch("scT", [BE, T])
        work = scratch("work", [BE, T])
        top8 = scratch("top8", [BE, 8])
        tie = scratch("tie", [BE, T])
        cnt = scratch("cnt", [BE, T])
        pos = scratch("pos", [BE, T])
        pos_bf = scratch("pos_bf", [BE, T], BF16)
        gates_T = scratch("gates_T", [BE, T])
        pos_dram = nc.dram_tensor("pos_dram", (BE, T), BF16, kind="Internal").ap()

        rx = scratch("rx", [P, 2, NT, D])
        rxT = scratch("rxT", [P, 2, T])
        psRT, psLG = (bank[0], bank[2]), (bank[1], bank[7])

        def dve_route_xln(b, par):
            for k in range(NT):
                nc.vector.tensor_scalar(rx[:, par, k, :], x_sb[:, b, k, :], mv[:, b, k, 0:1],
                                        rstd[:, b, k:k + 1], ALU.subtract, ALU.mult).then_inc(r_xln.sem, 1)

        def route_dve(dve):
            dve_route_xln(0, 0)
            dve_route_xln(1, 1)
            with nc.vector.Fori(0, B // 2 - 1) as i:
                for par in range(2):
                    dve.wait_ge(r_xTp.sem, r_xTp.at(2 * i + par, 1))
                    dve_route_xln(2 * i + par + 2, par)
            dve.wait_ge(r_lg.sem, r_lg.total(B))
            rows = lambda t: t[:, :, :, :].rearrange("p k b e -> p (k b) e")
            spread = rmax[:, :].unsqueeze(2).broadcast_to([P, NT * B, E])
            nc.vector.tensor_reduce(rmax[:, :], rows(lg), AX.X, ALU.max).then_inc(r_max.sem, 1)
            dve.wait_ge(r_max.sem, r_max.total(1))
            nc.vector.tensor_tensor(rows(lg), rows(lg), spread, ALU.subtract).then_inc(r_sub.sem, 1)
            dve.wait_ge(r_exp.sem, r_exp.total(1))
            nc.vector.tensor_reduce(rmax[:, :], rows(lg), AX.X, ALU.add).then_inc(r_sum.sem, 1)
            dve.wait_ge(r_sum.sem, r_sum.total(1))
            nc.vector.reciprocal(rmax[:, :], rmax[:, :]).then_inc(r_inv.sem, 1)
            dve.wait_ge(r_inv.sem, r_inv.total(1))
            nc.vector.tensor_tensor(rows(sc), rows(lg), spread, ALU.mult).then_inc(r_sc.sem, 1)
            dve.wait_ge(r_scTp.sem, r_scTp.total(1))
            nc.vector.tensor_copy(scT[:, :], bank[0][0:BE, :]).then_inc(r_scT.sem, 1)
            nc.vector.tensor_copy(work[:, :], bank[0][0:BE, :]).then_inc(r_scT.sem, 1)
            with nc.vector.Fori(0, (CAP - 1) // 8) as i:
                dve.wait_ge(r_scT.sem, r_scT.total(2))
                dve.wait_ge(r_rep.sem, r_rep.at(i, 0))
                waits_end(dve)
                nc.vector.max(top8[:, :], work[:, :]).then_inc(r_top.sem, 1)
                dve.wait_ge(r_top.sem, r_top.at(i, 1))
                waits_end(dve)
                nc.vector.match_replace(out=work[:, :], in_to_replace=top8[:, :], in_values=work[:, :],
                                                   imm_value=-1.0).then_inc(r_rep.sem, 1)
            dve.wait_ge(r_rep.sem, r_rep.total((CAP - 1) // 8))
            nc.vector.max(top8[:, :], work[:, :]).then_inc(r_top.sem, 1)
            dve.wait_ge(r_top.sem, r_top.total((CAP - 1) // 8 + 1))
            nc.vector.tensor_scalar(tie[:, :], work[:, :], top8[:, 0:1], None, ALU.is_equal).then_inc(r_eq.sem, 1)
            dve.wait_ge(r_eq.sem, r_eq.total(1))
            nc.vector.tensor_tensor_scan(out=cnt[:, :], data0=tie[:, :], data1=tie[:, :], initial=0.0,
                                                    op0=ALU.add, op1=ALU.bypass).then_inc(r_run.sem, 1)
            dve.wait_ge(r_run.sem, r_run.total(1))
            nc.vector.scalar_tensor_tensor(out=tie[:, :], in0=cnt[:, :], scalar=1.0, in1=tie[:, :],
                                                        op0=ALU.is_equal, op1=ALU.mult).then_inc(r_first.sem, 1)
            dve.wait_ge(r_first.sem, r_first.total(1))
            nc.vector.scalar_tensor_tensor(out=work[:, :], in0=work[:, :], scalar=-1.0, in1=tie[:, :],
                                                       op0=ALU.is_equal, op1=ALU.add).then_inc(r_mask.sem, 1)
            dve.wait_ge(r_mask.sem, r_mask.total(1))
            nc.vector.tensor_tensor_scan(out=cnt[:, :], data0=work[:, :], data1=work[:, :], initial=0.0,
                                                    op0=ALU.add, op1=ALU.bypass).then_inc(r_cnt.sem, 1)
            dve.wait_ge(r_cnt.sem, r_cnt.total(1))
            nc.vector.tensor_tensor(tie[:, :], cnt[:, :], work[:, :], ALU.mult).then_inc(r_run.sem, 1)
            dve.wait_ge(r_run.sem, r_run.total(2))
            nc.vector.tensor_scalar(pos[:, :], tie[:, :], -1.0, None, ALU.add).then_inc(r_pos.sem, 1)
            dve.wait_ge(r_pos.sem, r_pos.total(1))
            nc.vector.tensor_copy(pos_bf[:, :], pos[:, :]).then_inc(r_posb.sem, 1)
            nc.vector.tensor_tensor(gates_T[:, :], work[:, :], scT[:, :], ALU.mult).then_inc(r_gt.sem, 1)
            nc.vector.scalar_tensor_tensor(out=rest_l[0:BE, :], in0=pos[:, :], scalar=float(P),
                                                       in1=scT[:, :], op0=ALU.is_equal, op1=ALU.mult).then_inc(r_last.sem, 1)
            dve.wait_ge(r_posTp.sem, r_posTp.total(1))
            nc.vector.tensor_copy(posT[:, :, :, :].rearrange("p k b e -> p (k b e)"), bank[1][:, 0:NR]).then_inc(r_posT.sem, 1)

        def route_pool(pool):
            whole, rest = sc[:, :, :, :], sc_rest[:, :, :, :]
            parts = [sc_part[:, :, :, :, n] for n in range(PARTS)]
            pool.wait_ge(r_sc.sem, r_sc.total(1))
            nc.gpsimd.tensor_copy(parts[0], whole).then_inc(r_part.sem, 1)
            pool.wait_ge(r_part.sem, r_part.total(1))
            nc.gpsimd.tensor_tensor(rest, whole, parts[0], ALU.subtract).then_inc(r_part.sem, 1)
            pool.wait_ge(r_part.sem, r_part.total(2))
            nc.gpsimd.tensor_copy(parts[1], rest).then_inc(r_part.sem, 1)
            pool.wait_ge(r_part.sem, r_part.total(3))
            nc.gpsimd.tensor_tensor(rest, rest, parts[1], ALU.subtract).then_inc(r_part.sem, 1)
            pool.wait_ge(r_part.sem, r_part.total(4))
            nc.gpsimd.tensor_copy(parts[2], rest).then_inc(r_part.sem, 1)

        def act_route_xT(act, b, par):
            act.wait_ge(r_xTp.sem, r_xTp.at(b, 1))
            nc.scalar.activation(rxT[:, par, :], psRT[par][:, :], ACT.Copy).then_inc(r_xT.sem, 1)

        def act_route_logits(act, b, par):
            act.wait_ge(r_lgp.sem, r_lgp.at(b, 1))
            nc.scalar.activation(lg[:, :, b, :], psLG[par][:, 0:NT * E].rearrange("p (k e) -> p k e", e=E),
                                 ACT.Copy).then_inc(r_lg.sem, 1)

        def route_act(act):
            act_route_xT(act, 0, 0)
            act_route_xT(act, 1, 1)
            with nc.scalar.Fori(0, B // 2 - 1) as i:
                for par in range(2):
                    act_route_logits(act, 2 * i + par, par)
                    act_route_xT(act, 2 * i + par + 2, par)
            for par in range(2):
                act_route_logits(act, B - 2 + par, par)
            act.wait_ge(r_sub.sem, r_sub.total(1))
            nc.scalar.activation(lg[:, :, :, :], lg[:, :, :, :], ACT.Exp).then_inc(r_exp.sem, 1)

        def pe_route_xT(pe, b, par):
            pe.wait_ge(r_xln.sem, r_xln.at(b, NT))
            for k in range(NT):
                ins = nc.tensor.transpose(psRT[par][:, k * P:(k + 1) * P], rx[:, par, k, :], ident)
            ins.then_inc(r_xTp.sem, 1)

        def pe_route_logits(pe, b, par):
            pe.wait_ge(r_xT.sem, r_xT.at(b, 1))
            for k in range(NT):
                ins = nc.tensor.matmul(psLG[par][:, k * E:(k + 1) * E], rxT[:, par, k * P:(k + 1) * P],
                                       rT[:, :], start=True, stop=True)
            ins.then_inc(r_lgp.sem, 1)

        def route_pe(pe):
            pe_route_xT(pe, 0, 0)
            pe_route_xT(pe, 1, 1)
            with nc.tensor.Fori(0, B // 2 - 1) as i:
                pe.wait_ge(r_lg.sem, r_lg.at(2 * i, 0))
                for par in range(2):
                    pe_route_logits(pe, 2 * i + par, par)
                    pe_route_xT(pe, 2 * i + par + 2, par)
            pe.wait_ge(r_lg.sem, r_lg.at(B - 2, 0))
            for par in range(2):
                pe_route_logits(pe, B - 2 + par, par)
            pe.wait_ge(r_sc.sem, r_sc.total(1))
            for k in range(NT):
                ins = nc.tensor.transpose(bank[0][0:BE, k * P:(k + 1) * P],
                                          sc[:, k, :, :].rearrange("p b e -> p (b e)"), ident)
            ins.then_inc(r_scTp.sem, 1)
            pe.wait_ge(r_pos.sem, r_pos.total(1))
            for k in range(NT):
                ins = nc.tensor.transpose(bank[1][:, k * BE:(k + 1) * BE], pos[:, k * P:(k + 1) * P],
                                          ident[0:BE, 0:BE])
            ins.then_inc(r_posTp.sem, 1)

        def route_sync(sp):
            sp.wait_ge(r_posb.sem, r_posb.total(1))
            sp.dma_start(pos_dram, pos_bf[:, :]).then_inc(r_posd.sem, 16)
            sp.wait_ge(r_gt.sem, r_gt.total(1))
            sp.dma_start(rest_l[BE:2 * BE, :], gates_T[:, :]).then_inc(r_moved.sem, 16)

        NP = 2
        M = lambda name, per=1, step=1: signal("moe_" + name, per, step)
        m_bc, m_xln, m_part = M("pos_spread", NP, 16), M("xln", NP * NT), M("x_parts", NP * 5)
        m_scp, m_pick, m_place = M("score_parts", NP), M("pick", NP * NT), M("place", NP)
        m_xgp, m_xg = M("gathered_psum", NP * 3), M("gathered", NP * 3)
        m_gp, m_gate = M("gate_psum", NP), M("gate")
        m_hp, m_h = M("hidden_psum", E * HC), M("hidden", E * HC)
        m_yp, m_y, m_yl = M("y_psum", E), M("y_gated", E), M("y_last", E)
        m_rep, m_repT, m_rest = M("y_last_spread"), M("y_last_T_psum"), M("rest", 2 * NP)
        m_sp, m_x = M("scattered_psum", NP), M("x_updated", NP)

        slots, slot_row = const("slots"), const("slot_row")
        new_stage()
        slots_bf = scratch("slots_bf", [P, CAP], BF16)
        m_slots = M("slots_bf")
        pos_bc = scratch("pos_bc", [P, NP, E, T], BF16)
        sc_now = scratch("sc_now", [P, NP, NT, E, PARTS], BF16)
        pick = scratch("pick", [P, NP, NT, E, CAP], BF16)
        place = scratch("place", [P, NP, E, T])
        xg = scratch("xg", [P, NP, E, CAP])
        gate = scratch("gate", [P, NP, E])
        hT = scratch("hT", [P, 2, HC, NP, CAP])
        yg = scratch("yg", [P, NP, E, D])
        yl = scratch("yl", [P, NP, E])
        yl_rep = scratch("yl_rep", [P, NP, B, E])
        rest_r = scratch("rest_r", [P, NP, D])
        psH = (wide[:, 0:512], wide[:, 512:1024], bank[5], bank[6])
        psYe = (bank[7], bank[2])
        psG = bank[2][:, 448:448 + NP * E * PARTS]
        psRep = (bank[7][0:BE, 384:384 + D], bank[2][0:BE, 264:264 + D])
        GP = 3
        experts_to = [-(-GC * (c + 1) // CAP) for c in range(GP)]
        gathers_for = [NP * -(-CAP * (e + 1) // GC) for e in range(E)]

        PARTS_AT = {0: (1,)}
        PICK_AT = {1: ((1, 0), (1, 1)), 2: ((1, 2), (1, 3))}
        GATE_AT = {2: 0, 4: 1}
        STATS_AT = {4: 0, 5: 1}
        GATHER_AT = {3: (0,), 4: (1,), 5: (2,), 6: (3,), 7: (4, 5)}

        def moe_sync(sp):
            sp.wait_ge(r_posd.sem, r_posd.total(16))
            sp.wait_ge(r_moved.sem, r_moved.total(16))
            sp.wait_ge(r_part.sem, r_part.total(5))
            sp.wait_ge(r_posT.sem, r_posT.total(1))
            with nc.sync.Fori(0, B // NP) as i:
                sp.wait_ge(m_place.sem, m_place.at(i, 0))
                for r in range(NP):
                    src = pos_dram.rearrange("(b e) t -> b (e t)", e=E)[NP * i + r]
                    src = src.rearrange("(a n) -> a n", a=1) if len(src.shape) == 1 else src
                    sp.dma_start(pos_bc[:, r, :, :].rearrange("p e t -> p (e t)"),
                                 src.broadcast_to([P, E * T])).then_inc(m_bc.sem, 16)

        def moe_pool(pool):
            pool.wait_ge(ln2.rstd.sem, ln2.rstd.total(1))
            for r in range(NP):
                moe_parts(pool, nc.gpsimd, 0, r)
            with nc.gpsimd.Fori(0, B // NP) as i:
                for r in range(NP):
                    pool.wait_ge(m_bc.sem, m_bc.at(i, NP))
                    pool.wait_ge(m_sp.sem, m_sp.at(i, 0))
                    waits_end(pool)
                    nc.gpsimd.tensor_scalar(place[:, r, :, :].rearrange("p e t -> p (e t)"),
                                                         pos_bc[:, r, :, :].rearrange("p e t -> p (e t)"),
                                                         slot_row, None, ALU.is_equal).then_inc(m_place.sem, 1)

        def moe_parts(engine, ops, i, r):
            s = lambda n: 5 * r + n
            engine.wait_ge(m_part.sem, m_part.at(i, 5 * r))
            for k in range(NT):
                ins = ops.tensor_scalar(xln[:, k, :], x_sb[:, NP * i + r, k, :], mv[:, NP * i + r, k, 0:1],
                                        rstd[:, NP * i + r, k:k + 1], ALU.subtract, ALU.mult)
                ins.then_inc(m_xln.sem, 1)
            engine.wait_ge(m_xln.sem, m_xln.at(i, (r + 1) * NT))
            engine.wait_ge(m_xgp.sem, m_xgp.at(i, 0))
            ops.tensor_copy(x_part[:, r, 0], xln[:, :, :]).then_inc(m_part.sem, 1)
            engine.wait_ge(m_part.sem, m_part.at(i, s(1)))
            ops.tensor_tensor(x_rest[:, :, :], xln[:, :, :], x_part[:, r, 0], ALU.subtract).then_inc(m_part.sem, 1)
            engine.wait_ge(m_part.sem, m_part.at(i, s(2)))
            ops.tensor_copy(x_part[:, r, 1], x_rest[:, :, :]).then_inc(m_part.sem, 1)
            engine.wait_ge(m_part.sem, m_part.at(i, s(3)))
            ops.tensor_tensor(x_rest[:, :, :], x_rest[:, :, :], x_part[:, r, 1], ALU.subtract).then_inc(m_part.sem, 1)
            engine.wait_ge(m_part.sem, m_part.at(i, s(4)))
            ops.tensor_copy(x_part[:, r, 2], x_rest[:, :, :]).then_inc(m_part.sem, 1)

        def dve_moe_scores(dve, i, r):
            dve.wait_ge(m_xgp.sem, m_xgp.at(i, 0))
            dve.wait_ge(m_gp.sem, m_gp.at(i, 0))
            nc.vector.tensor_copy(sc_now[:, r], sc_part[:, :, NP * i + r, :, :]).then_inc(m_scp.sem, 1)

        def dve_moe_pick(dve, i, r, k):
            nc.vector.tensor_tensor(
                pick[:, r, k, :, :], slots_bf[:, :].unsqueeze(1).broadcast_to([P, E, CAP]),
                posT[:, k, NP * i + r, :].unsqueeze(2).broadcast_to([P, E, CAP]), ALU.is_equal).then_inc(m_pick.sem, 1)

        def dve_moe_gate(dve, i):
            dve.wait_ge(m_gp.sem, m_gp.at(i, NP))
            dve.wait_ge(m_y.sem, m_y.at(i, 0))
            nc.vector.tensor_reduce(gate[:, :, :], psG.rearrange("p (r e n) -> p r e n", e=E, n=PARTS),
                                    AX.X, ALU.add).then_inc(m_gate.sem, 1)

        def dve_moe_gated(dve, i, e):
            if e == 0:
                dve.wait_ge(m_gate.sem, m_gate.at(i, 1))
                dve.wait_ge(m_sp.sem, m_sp.at(i, 0))
                dve.wait_ge(m_rep.sem, m_rep.at(i, 0))
            dve.wait_ge(m_yp.sem, m_yp.at(i, e + 1))
            nc.vector.tensor_tensor(yg[:, :, e, :], psYe[e % 2][:, 0:NP * D].rearrange("p (r d) -> p r d", d=D),
                                    gate[:, :, e].unsqueeze(2).broadcast_to([P, NP, D]), ALU.mult).then_inc(m_y.sem, 1)
            nc.vector.tensor_copy(yl[:, :, e], psYe[e % 2][:, NP * D:NP * D + NP]).then_inc(m_yl.sem, 1)

        def dve_moe_last_spread(dve, i):
            dve.wait_ge(m_yl.sem, m_yl.at(i, E))
            dve.wait_ge(m_repT.sem, m_repT.at(i, 0))
            nc.vector.tensor_copy(yl_rep[:, :, :, :], yl[:, :, :].unsqueeze(2).broadcast_to([P, NP, B, E])).then_inc(m_rep.sem, 1)

        def dve_moe_rest(dve, i):
            dve.wait_ge(m_repT.sem, m_repT.at(i, 1))
            dve.wait_ge(m_sp.sem, m_sp.at(i, 0))
            for r in range(NP):
                nc.vector.tensor_scalar(rest_r[0:BE, r, :], psRep[r], seqmask[0:BE, NP * i + r].unsqueeze(1),
                                        None, ALU.mult).then_inc(m_rest.sem, 1)
                nc.vector.tensor_scalar(rest_r[BE:2 * BE, r, :], b2rep[BE:2 * BE, :],
                                        seqmask[BE:2 * BE, NP * i + r].unsqueeze(1), None, ALU.mult).then_inc(m_rest.sem, 1)

        def dve_moe_residual(dve, i, r):
            dve.wait_ge(m_sp.sem, m_sp.at(i, r + 1))
            nc.vector.tensor_tensor(x_sb[:, NP * i + r], x_sb[:, NP * i + r],
                                    bank[r][:, :].rearrange("p (k d) -> p k d", d=D), ALU.add).then_inc(m_x.sem, 1)

        def dve_moe_stats(dve, i, r):
            dve.wait_ge(m_x.sem, m_x.at(i, r + 1))
            ln3.dve_sequence(dve, NP * i + r)

        def dve_moe_turn(dve, i, scatter=True, gather=True):
            if scatter:
                dve_moe_rest(dve, i - 1)
            if gather:
                moe_parts(dve, nc.vector, i + 1, 0)
                dve_moe_scores(dve, i + 1, 0)
                for k in range(NT):
                    dve_moe_pick(dve, i + 1, 0, k)
            if scatter:
                for r in range(NP):
                    dve_moe_residual(dve, i - 1, r)
            for e in range(E):
                dve_moe_gated(dve, i, e)
                if gather:
                    for r in PARTS_AT.get(e, ()):
                        moe_parts(dve, nc.vector, i + 1, r)
                        dve_moe_scores(dve, i + 1, r)
                    for r, k in PICK_AT.get(e, ()):
                        dve_moe_pick(dve, i + 1, r, k)
                if scatter and e in STATS_AT:
                    dve_moe_stats(dve, i - 1, STATS_AT[e])
            dve_moe_last_spread(dve, i)
            if gather:
                dve_moe_gate(dve, i + 1)

        def moe_dve(dve):
            dve.wait_ge(r_part.sem, r_part.total(5))
            dve.wait_ge(s_we.sem, s_we.total(16 * NWE))
            nc.vector.tensor_copy(slots_bf[:, :], slots).then_inc(m_slots.sem, 1)
            dve.wait_ge(m_slots.sem, m_slots.total(1))
            for r in range(NP):
                dve_moe_scores(dve, 0, r)
                for k in range(NT):
                    dve_moe_pick(dve, 0, r, k)
            dve_moe_gate(dve, 0)
            dve_moe_turn(dve, 0, scatter=False)
            with nc.vector.Fori(1, B // NP - 1) as i:
                dve_moe_turn(dve, i)
            dve_moe_turn(dve, B // NP - 1, gather=False)
            dve_moe_rest(dve, B // NP - 1)
            for r in range(NP):
                dve_moe_residual(dve, B // NP - 1, r)
                dve_moe_stats(dve, B // NP - 1, r)
            dve.wait_ge(m_x.sem, m_x.at(B // NP, 0))

        def act_moe_gathered(act, i, n, first=False):
            c, r = divmod(n, NP)
            act.wait_ge(m_xgp.sem, m_xgp.at(i, n + 1))
            if not first:
                act.wait_ge(m_hp.sem, m_hp.at(i - 1, experts_to[c] * HC))
            nc.scalar.activation(xg[:, r, :, :].rearrange("p e c -> p (e c)")[:, c * GC:(c + 1) * GC],
                                 bank[n % 2][:, 0:GC], ACT.Copy).then_inc(m_xg.sem, 1)

        def act_moe_gelu(act, i, e):
            for c in range(HC):
                act.wait_ge(m_hp.sem, m_hp.at(i, e * HC + c + 1))
                act.wait_ge(m_yp.sem, m_yp.at(i, e - 1 if e >= 2 else 0))
                nc.scalar.activation(hT[:, e % 2, c, :, :],
                                     psH[c][:, 0:NP * CAP].rearrange("p (r c) -> p r c", c=CAP),
                                     ACT.Gelu, bias=b1T[:, e * HC + c:e * HC + c + 1]).then_inc(m_h.sem, 1)

        def act_moe_turn(act, i, gather=True):
            act_moe_gelu(act, i, 0)
            for e in range(E):
                if e + 1 < E:
                    act_moe_gelu(act, i, e + 1)
                if gather:
                    for n in GATHER_AT.get(e, ()):
                        act_moe_gathered(act, i + 1, n)

        def moe_act(act):
            for n in range(NP * GP):
                act_moe_gathered(act, 0, n, first=True)
            with nc.scalar.Fori(0, B // NP - 1) as i:
                act_moe_turn(act, i)
            act_moe_turn(act, B // NP - 1, gather=False)

        def pe_moe_gather(pe, i, n):
            c, r = divmod(n, NP)
            pe.wait_ge(m_part.sem, m_part.at(i, 5 * (r + 1)))
            pe.wait_ge(m_pick.sem, m_pick.at(i, (r + 1) * NT))
            if n >= 2:
                pe.wait_ge(m_xg.sem, m_xg.at(i, n - 1))
            else:
                pe.wait_ge(m_xg.sem, m_xg.at(i, 0))
            for k in range(NT):
                for part in range(PARTS):
                    ins = nc.tensor.matmul(
                        bank[n % 2][:, 0:GC], x_part[:, r, part, k, :],
                        pick[:, r, k, :, :].rearrange("p e c -> p (e c)")[:, c * GC:(c + 1) * GC],
                        start=k == 0 and part == 0, stop=k == NT - 1 and part == PARTS - 1)
            ins.then_inc(m_xgp.sem, 1)

        def pe_moe_gates(pe, i, r, experts_before=0):
            pe.wait_ge(m_pick.sem, m_pick.at(i, (r + 1) * NT))
            pe.wait_ge(m_scp.sem, m_scp.at(i, r + 1))
            pe.wait_ge(m_gate.sem, m_gate.at(i, 0))
            if experts_before:
                pe.wait_ge(m_yl.sem, m_yl.at(i - 1, experts_before))
            for e in range(E):
                for k in range(NT):
                    at = (r * E + e) * PARTS
                    ins = nc.tensor.matmul(psG[:, at:at + PARTS], pick[:, r, k, e, 0:P], sc_now[:, r, k, e, :],
                                           start=k == 0, stop=k == NT - 1)
            ins.then_inc(m_gp.sem, 1)

        def pe_moe_hidden(pe, i, e):
            pe.wait_ge(m_xg.sem, m_xg.at(i, gathers_for[e]))
            for c in range(HC):
                if e:
                    pe.wait_ge(m_h.sem, m_h.at(i, (e - 1) * HC + c + 1))
                else:
                    pe.wait_ge(m_h.sem, m_h.at(i, 0))
                nc.tensor.matmul(psH[c][:, 0:NP * CAP].rearrange("p (r c) -> p r c", c=CAP),
                                 w1_sb[:, e, c * P:(c + 1) * P], xg[:, :, e, :], start=True, stop=True).then_inc(m_hp.sem, 1)

        def pe_moe_output(pe, i, e):
            pe.wait_ge(m_h.sem, m_h.at(i, (e + 1) * HC))
            if e >= 2:
                pe.wait_ge(m_yl.sem, m_yl.at(i, e - 1))
            else:
                pe.wait_ge(m_yl.sem, m_yl.at(i, 0))
            if e == 1:
                pe.wait_ge(m_gate.sem, m_gate.at(i, 1))
            for r in range(NP):
                for c in range(HC):
                    nc.tensor.matmul(psYe[e % 2][:, r * D:(r + 1) * D], hT[:, e % 2, c, r, 0:P], w2_sb[:, e, c, :],
                                     start=c == 0, stop=c == HC - 1)
            for c in range(HC):
                ins = nc.tensor.matmul(psYe[e % 2][:, NP * D:NP * D + NP], w2_sb[:, e, c, :],
                                       hT[:, e % 2, c, :, P], start=c == 0, stop=c == HC - 1)
            ins.then_inc(m_yp.sem, 1)

        def pe_moe_last_T(pe, i, last=False):
            pe.wait_ge(m_rep.sem, m_rep.at(i, 1))
            pe.wait_ge(m_rest.sem, m_rest.at(i, 0))
            if not last:
                pe.wait_ge(m_gate.sem, m_gate.at(i + 1, 1))
            waits_end(pe)
            for r in range(NP):
                ins = nc.tensor.transpose(psRep[r], yl_rep[:, r, :, :].rearrange("p b e -> p (b e)"), ident)
            ins.then_inc(m_repT.sem, 1)

        def pe_moe_scatter(pe, i, r, last=False):
            pe.wait_ge(m_y.sem, m_y.at(i, E))
            pe.wait_ge(m_place.sem, m_place.at(i, r + 1))
            pe.wait_ge(m_x.sem, m_x.at(i, 0))
            if not last:
                pe.wait_ge(m_xg.sem, m_xg.at(i + 1, NP * GP))
            for k in range(NT):
                at = bank[r][:, k * D:(k + 1) * D]
                for e in range(E):
                    nc.tensor.matmul(at, place[:, r, e, k * P:(k + 1) * P], yg[:, r, e, :],
                                     start=e == 0, stop=False)
                if k == 0:
                    pe.wait_ge(m_rest.sem, m_rest.at(i, 2 * NP))
                ins = nc.tensor.matmul(at, rest_l[:, k * P:(k + 1) * P], rest_r[:, r, :], start=False, stop=True)
            ins.then_inc(m_sp.sem, 1)

        def pe_moe_turn(pe, i, scatter=True, gather=True):
            pe_moe_hidden(pe, i, 0)
            if scatter:
                pe_moe_last_T(pe, i - 1)
                pe_moe_scatter(pe, i - 1, 0)
            pe_moe_hidden(pe, i, 1)
            if scatter:
                pe_moe_scatter(pe, i - 1, 1)
            for e in range(E):
                if 1 <= e < E - 1:
                    pe_moe_hidden(pe, i, e + 1)
                pe_moe_output(pe, i, e)
                if gather:
                    if e in GATE_AT:
                        pe_moe_gates(pe, i + 1, GATE_AT[e], experts_before=e)
                    for n in GATHER_AT.get(e, ()):
                        if n < NP and scatter:
                            pe.wait_ge(m_x.sem, m_x.at(i, 0))
                        pe_moe_gather(pe, i + 1, n)

        def moe_pe(pe):
            pe.wait_ge(r_moved.sem, r_moved.total(16))
            pe.wait_ge(s_we.sem, s_we.total(16 * NWE))
            for n in range(NP * GP):
                pe_moe_gather(pe, 0, n)
            for r in range(NP):
                pe_moe_gates(pe, 0, r)
            pe_moe_turn(pe, 0, scatter=False)
            with nc.tensor.Fori(1, B // NP - 1) as i:
                pe_moe_turn(pe, i)
            pe_moe_turn(pe, B // NP - 1, gather=False)
            pe_moe_last_T(pe, B // NP - 1, last=True)
            for r in range(NP):
                pe_moe_scatter(pe, B // NP - 1, r, last=True)

        Q = lambda name, per=1, step=1: signal("mqa_" + name, per, step)
        q_init, q_zero = Q("buffers_set"), Q("rows_zeroed")
        q_xln, q_xTp, q_xT, q_qkvp, q_qkv = Q("xln", NT), Q("xT_psum"), Q("xT"), Q("qkv_psum", 2), Q("qkv", 2)
        q_kpart, q_qpart, q_v, q_kx, q_qx = Q("k_parts", 5), Q("q_parts", 5), Q("v"), Q("k_slots", PARTS), Q("q_slots", NT * (PARTS - 1))
        q_kTp, q_kTm, q_kTe = Q("kT_psum"), Q("kT_for_max"), Q("kT_for_exp")
        q_qx0 = Q("q_slots_first_part", NT)
        NU = HEADS // 2
        q_qTp, q_qT = Q("qT_psum", 2 * NT), Q("qT", 2 * NT)
        max_units = [(k, h, n) for k in range(NT) for n in (max(1, 4 // (k + 1) if k != 2 else 1),)
                     for h in range(0, HEADS, n)]
        NM = len(max_units)
        q_smp, q_mx, q_neg, q_mpart = Q("max_scores_psum", NM), Q("max", NM), Q("neg_max"), Q("neg_max_parts", 5)
        q_mTp, q_mT, q_mrow = Q("neg_max_T_psum"), Q("neg_max_T"), Q("shift_rows", PARTS, 16)
        NX = NQ * NT * 2
        q_sp, q_p, q_pc = Q("scores_psum", NX), Q("exp", NX), Q("exp_causal", NX)
        q_av, q_o = Q("values_summed", NQ * NT), Q("o", NQ)
        q_oTp, q_rd, q_y = Q("o_back_psum", NT), Q("sum_inverse", NT), Q("y", NT)
        q_yTp, q_yT, q_prp, q_x = Q("yT_psum"), Q("yT"), Q("projected_psum"), Q("x_updated")

        new_stage()
        qkv = scratch("qkv", [P, NT, D + 2 * L])
        kp = scratch("kp", [P, PARTS, NT, L], BF16)
        k_rest = scratch("k_rest", [P, NT, L])
        qp = scratch("qp", [P, PARTS, NT, D], BF16)
        q_rest = scratch("q_rest", [P, NT, D])
        vx = scratch("vx", [P, 2, NT, 32])
        kx3 = scratch("kx3", [P, NT, PARTS, PARTS, L], BF16)
        qx3 = scratch("qx3", [P, NT, HEADS, PARTS, PARTS, L], BF16)
        kTm = scratch("kTm", [P, T], BF16)
        kTe = scratch("kTe", [P, 2, T], BF16)
        qT = scratch("qT", [P, 2, HEADS, T], BF16)
        mx = scratch("mx", [P, NT, HEADS])
        mp = scratch("mp", [P, NT, PARTS, HEADS], BF16)
        mT = scratch("mT", [PARTS * HEADS, T], BF16)
        pexp = scratch("pexp", [P, 4, 2, T])
        oT = scratch("oT", [P, NQ, T])
        rd = scratch("rd", [P, 2, HEADS])
        y2 = scratch("y2", [P, NT, D])
        y2T = scratch("y2T", [P, T])
        mask_qk = scratch("mask_qk", [P, P], BF16)
        causal_qk, shift_rows = const("causal_qk"), const("shift_rows")
        psM4 = (bank[1], bank[2], bank[7], wide[:, 0:512])
        psM2, psE, psO = (bank[1], bank[2]), (wide, wide2), bank[7]

        STEPS = NQ * NT
        XLN_STEP, XT_STEP, QKV_STEPS, SPLIT_STEP, SLOT_STEP = 1, 5, (6, 7), 8, 11
        SPLIT_IN_STEP = 4
        MAX_STEPS = range(2, 14)
        max_in, at_unit = {}, 0
        for s in MAX_STEPS:
            count = -(-(NM - at_unit) // (MAX_STEPS[-1] + 1 - s))
            max_in[s] = range(at_unit, at_unit + count)
            at_unit += count
        assert at_unit == NM and count <= 4
        NM_EARLY = sum(k < 2 for k, _, _ in max_units)
        YT_STEP, PROJECT_STEP = 0, 1
        SHIFT_T_STEP = STEPS - 1

        def max_unit(s, n):
            return max_in.get(s, ())[n:n + 1]

        def qT_unit(s, half):
            return (s + 2,) if half == 0 and s + 2 < 2 * NT else ()

        def fill_k_slots(ops, n):
            return ops(kx3[:, :, :, n, :], kp[:, n].unsqueeze(2).broadcast_to([P, NT, PARTS, L]))

        def fill_q_slots(ops, k, n):
            return ops(qx3[:, k, :, n, :, :], qp[:, n, k].rearrange("p (h l) -> p h l", l=L).unsqueeze(2)
                       .broadcast_to([P, HEADS, PARTS, L]))

        def act_copy(out, in_):
            return nc.scalar.activation(out, in_, ACT.Copy)

        def split(dve, sig, b, whole, rest, parts, ops=range(2 * PARTS - 1)):
            for n in ops:
                part = parts[n // 2]
                if n:
                    dve.wait_ge(sig.sem, sig.at(b, n))
                if n % 2 == 0:
                    nc.vector.tensor_copy(part, whole if n == 0 else rest).then_inc(sig.sem, 1)
                else:
                    nc.vector.tensor_tensor(rest, whole if n == 1 else rest, part, ALU.subtract).then_inc(sig.sem, 1)

        def dve_xln(dve, b):
            dve.wait_ge(q_xTp.sem, q_xTp.at(b, 0))
            normalise(q_xln, b)

        def dve_k_parts(dve, b, ops=range(5)):
            dve.wait_ge(q_qkv.sem, q_qkv.at(b, 2))
            dve.wait_ge(q_kx.sem, q_kx.at(b, 0))
            split(dve, q_kpart, b, qkv[:, :, D:D + L], k_rest[:, :, :], [kp[:, n] for n in range(PARTS)], ops)

        def dve_k_slots(dve, b):
            dve.wait_ge(q_kpart.sem, q_kpart.at(b, 5))
            dve.wait_ge(q_kTp.sem, q_kTp.at(b, 0))
            for n in range(PARTS):
                fill_k_slots(nc.vector.tensor_copy, n).then_inc(q_kx.sem, 1)

        def dve_q_parts(dve, b, ops=range(5)):
            dve.wait_ge(q_qkv.sem, q_qkv.at(b, 2))
            dve.wait_ge(q_qx.sem, q_qx.at(b, 0))
            split(dve, q_qpart, b, qkv[:, :, 0:D], q_rest[:, :, :], [qp[:, n] for n in range(PARTS)], ops)

        def dve_v(dve, b, par, first):
            dve.wait_ge(q_qkv.sem, q_qkv.at(b, 2))
            if not first:
                dve.wait_ge(q_av.sem, q_av.at(b - 1, 0))
            nc.vector.tensor_copy(vx[:, par, :, 0:L], qkv[:, :, D + L:D + 2 * L]).then_inc(q_v.sem, 1)

        def dve_keys(dve, b, par):
            dve.wait_ge(q_kTp.sem, q_kTp.at(b, 1))
            src = bank[0][:, :].bitcast(BF16)[0:QR, 0:T]
            nc.vector.tensor_copy(kTm[0:QR, :], src).then_inc(q_kTm.sem, 1)
            nc.vector.tensor_copy(kTe[0:QR, par, :], src).then_inc(q_kTe.sem, 1)

        def dve_max(dve, b, units, banks):
            for n in units:
                k, h, nh = max_units[n]
                w = P * (k + 1)
                if n == 0:
                    dve.wait_ge(q_mpart.sem, q_mpart.at(b, 0))
                dve.wait_ge(q_smp.sem, q_smp.at(b, n + 1))
                nc.vector.tensor_reduce(mx[:, k, h:h + nh],
                                        banks[n % len(banks)][:, 0:nh * w].rearrange("p (h s) -> p h s", s=w),
                                        AX.X, ALU.max).then_inc(q_mx.sem, 1)

        def dve_shift(dve, b):
            dve.wait_ge(q_mx.sem, q_mx.at(b, NM))
            nc.vector.tensor_scalar(mx[:, :, :], mx[:, :, :], -1.0, None, ALU.mult).then_inc(q_neg.sem, 1)
            dve.wait_ge(q_neg.sem, q_neg.at(b, 1))
            dve.wait_ge(q_mTp.sem, q_mTp.at(b, 0))
            split(dve, q_mpart, b, mx[:, :, :], mx[:, :, :], [mp[:, :, n, :] for n in range(PARTS)])

        def dve_shift_T(dve, b):
            dve.wait_ge(q_mTp.sem, q_mTp.at(b, 1))
            dve.wait_ge(q_mrow.sem, q_mrow.at(b, 0))
            nc.vector.tensor_copy(mT[:, :], bank[0][:, :].bitcast(BF16)[0:PARTS * HEADS, 0:T]).then_inc(q_mT.sem, 1)

        def dve_divide(dve, b, tiles):
            for k in tiles:
                dve.wait_ge(q_oTp.sem, q_oTp.at(b, k + 1))
                ps = psM2[k % 2][:, :].rearrange("p (h c) -> p h c", c=32)
                nc.vector.reciprocal(rd[:, k % 2, :], ps[:, :, L]).then_inc(q_rd.sem, 1)
                dve.wait_ge(q_rd.sem, q_rd.at(b, k + 1))
                dve.wait_ge(q_yTp.sem, q_yTp.at(b, 0))
                nc.vector.tensor_tensor(y2[:, k, :].rearrange("p (h l) -> p h l", l=L), ps[:, :, 0:L],
                                        rd[:, k % 2, :].unsqueeze(2).broadcast_to([P, HEADS, L]),
                                        ALU.mult).then_inc(q_y.sem, 1)

        def dve_residual(dve, b):
            dve.wait_ge(q_prp.sem, q_prp.at(b, 1))
            nc.vector.tensor_tensor(x_sb[:, b], x_sb[:, b], psM2[1][:, :].rearrange("p (k d) -> p k d", d=D),
                                    ALU.add).then_inc(q_x.sem, 1)

        def dve_stats(dve, b):
            dve.wait_ge(q_x.sem, q_x.at(b, 1))
            ln4.dve_sequence(dve, b)

        def dve_turn(dve, b, par, tail=True, middle=True, front=True, stats=True):
            if middle:
                dve_v(dve, b + 1, 1 - par, False)
                dve_keys(dve, b + 1, 1 - par)
            if tail:
                dve_divide(dve, b - 1, (0, 1))
                dve_divide(dve, b - 1, (2, 3))
            if stats:
                dve_stats(dve, b - 2)
            for s in range(STEPS):
                if tail and s == PROJECT_STEP:
                    dve_residual(dve, b - 1)
                if front and s == XLN_STEP:
                    dve_xln(dve, b + 2)
                for n in range(4):
                    if middle:
                        dve_max(dve, b + 1, max_unit(s, n), psM2)
                    at = SPLIT_IN_STEP * (s - SPLIT_STEP) + n
                    if front and 0 <= at < 5:
                        dve_k_parts(dve, b + 2, (at,))
                    if front and 5 <= at < 10:
                        dve_q_parts(dve, b + 2, (at - 5,))
                if front and s == SLOT_STEP:
                    dve_k_slots(dve, b + 2)
                if middle and s == MAX_STEPS[-1]:
                    dve_shift(dve, b + 1)
                if middle and s == SHIFT_T_STEP:
                    dve_shift_T(dve, b + 1)

        def mqa_dve(dve):
            dve_xln(dve, 0)
            nc.vector.tensor_copy(mask_qk[:, :], causal_qk)
            nc.vector.memset(vx[:, :, :, :], 0.0)
            nc.vector.tensor_copy(kTe[64:P, :, :], shift_rows[64:P, :].unsqueeze(2).broadcast_to([64, 2, T])).then_inc(q_init.sem, 1)
            dve.wait_ge(q_init.sem, q_init.total(1))
            nc.vector.memset(vx[:, :, :, L:L + 1], 1.0).then_inc(q_init.sem, 1)
            dve.wait_ge(q_init.sem, q_init.total(2))
            dve_k_parts(dve, 0)
            dve_k_slots(dve, 0)
            dve_q_parts(dve, 0)
            dve_v(dve, 0, 0, True)
            dve_xln(dve, 1)
            dve.wait_ge(q_zero.sem, q_zero.total(2))
            dve_keys(dve, 0, 0)
            dve_max(dve, 0, range(NM_EARLY), psM4)
            dve_k_parts(dve, 1)
            dve_k_slots(dve, 1)
            dve_q_parts(dve, 1)
            dve_max(dve, 0, range(NM_EARLY, NM), psM4)
            dve_shift(dve, 0)
            dve_shift_T(dve, 0)
            dve_turn(dve, 0, 0, tail=False, stats=False)
            dve_turn(dve, 1, 1, stats=False)
            with nc.vector.Fori(1, B // 2 - 1) as i:
                dve_turn(dve, 2 * i, 0)
                dve_turn(dve, 2 * i + 1, 1)
            dve_turn(dve, B - 2, 0, front=False)
            dve_turn(dve, B - 1, 1, middle=False, front=False)
            dve_stats(dve, B - 2)
            dve_divide(dve, B - 1, range(NT))
            dve_residual(dve, B - 1)
            dve_stats(dve, B - 1)
            dve.wait_ge(q_x.sem, q_x.total(B))

        NSLOT = NT * (PARTS - 1)
        slots_ahead = STEPS - SLOT_STEP

        def pool_slots(pool, b, m):
            k, n = divmod(m, PARTS - 1)
            pool.wait_ge(q_qpart.sem, q_qpart.at(b, 5))
            pool.wait_ge(q_qTp.sem, q_qTp.at(b, 0))
            waits_end(pool)
            fill_q_slots(nc.gpsimd.tensor_copy, k, n + 1).then_inc(q_qx.sem, 1)

        def pool_causal(pool, b, n):
            pool.wait_ge(q_p.sem, q_p.at(b, n + 1))
            waits_end(pool)
            nc.gpsimd.affine_select(out=pexp[:, n % 4, :, 0:P], in_=pexp[:, n % 4, :, 0:P],
                                    pattern=[[0, 2], [1, P]], compare_op=ALU.is_ge, fill=0.0, base=0,
                                    channel_multiplier=-1).then_inc(q_pc.sem, 1)

        def pool_turn(pool, b, middle=True, front=True):
            for s in range(STEPS):
                pool_causal(pool, b, 2 * s)
                pool_causal(pool, b, 2 * s + 1)
                if middle and slots_ahead + s < NSLOT:
                    pool_slots(pool, b + 1, slots_ahead + s)
                if front and s >= SLOT_STEP:
                    pool_slots(pool, b + 2, s - SLOT_STEP)

        def mqa_pool(pool):
            pool.wait_ge(m_x.sem, m_x.total(B))
            nc.gpsimd.memset(kTm[64:P, :], 0.0).then_inc(q_zero.sem, 1)
            nc.gpsimd.memset(qT[64:P, :, :, :], 0.0).then_inc(q_zero.sem, 1)
            for m in range(slots_ahead):
                pool_slots(pool, 1, m)
            pool_turn(pool, 0)
            pool_turn(pool, 1)
            with nc.gpsimd.Fori(1, B // 2 - 1) as i:
                pool_turn(pool, 2 * i)
                pool_turn(pool, 2 * i + 1)
            pool_turn(pool, B - 2, front=False)
            pool_turn(pool, B - 1, middle=False, front=False)

        def act_xT(act, b):
            act.wait_ge(q_xTp.sem, q_xTp.at(b, 1))
            act.wait_ge(q_qkvp.sem, q_qkvp.at(b, 0))
            nc.scalar.activation(xT[:, :], bank[0][:, :], ACT.Copy).then_inc(q_xT.sem, 1)

        def act_qkv(act, b, r):
            act.wait_ge(q_qkvp.sem, q_qkvp.at(b, r + 1))
            act.wait_ge(q_qpart.sem, q_qpart.at(b, 0))
            act.wait_ge(q_kpart.sem, q_kpart.at(b, 0))
            act.wait_ge(q_v.sem, q_v.at(b, 0))
            nc.scalar.activation(qkv[:, 2 * r:2 * r + 2, :],
                                 bank[0][:, 0:2 * (D + 2 * L)].rearrange("p (k n) -> p k n", k=2),
                                 ACT.Copy).then_inc(q_qkv.sem, 1)

        def act_qT(act, b, par, u):
            k, half = divmod(u, 2)
            act.wait_ge(q_qTp.sem, q_qTp.at(b, u + 1))
            nc.scalar.activation(qT[0:QR, par, half * NU:(half + 1) * NU, k * P:(k + 1) * P],
                                 bank[0][:, :].bitcast(BF16)[0:QR, :].rearrange("p (h t) -> p h t", h=NU),
                                 ACT.Copy).then_inc(q_qT.sem, 1)

        def act_exp(act, b, step, halves=(0, 1)):
            w = T - P * (step % NT)
            for n in (2 * step + half for half in halves):
                act.wait_ge(q_sp.sem, q_sp.at(b, n + 1))
                act.wait_ge(q_av.sem, q_av.at(b, step - 1 if step >= 2 else 0))
                nc.scalar.activation(pexp[:, n % 4, :, 0:w],
                                     psE[n % 2][:, :].rearrange("p (h t) -> p h t", h=2)[:, :, 0:w],
                                     ACT.Exp, scale=SCALE).then_inc(q_p.sem, 1)

        def act_quad(act, b, qd):
            act.wait_ge(q_av.sem, q_av.at(b, (qd + 1) * NT))
            act.wait_ge(q_oTp.sem, q_oTp.at(b, 0))
            nc.scalar.activation(oT[:, qd, :], psO[:, :], ACT.Copy).then_inc(q_o.sem, 1)

        def act_yT(act, b):
            act.wait_ge(q_yTp.sem, q_yTp.at(b, 1))
            act.wait_ge(q_prp.sem, q_prp.at(b, 0))
            nc.scalar.activation(y2T[:, :], psM2[0][:, :], ACT.Copy).then_inc(q_yT.sem, 1)

        def act_turn(act, b, par, tail=True, middle=True, front=True):
            if middle:
                act.wait_ge(q_sp.sem, q_sp.at(b, 0))
                act_qT(act, b + 1, 1 - par, 0)
                act_qT(act, b + 1, 1 - par, 1)
            act_exp(act, b, 0)
            for s in range(STEPS):
                if s and s % NT == 0:
                    act_quad(act, b, s // NT - 1)
                for half in range(2):
                    if s + 1 < STEPS:
                        act_exp(act, b, s + 1, (half,))
                    if middle:
                        for u in qT_unit(s, half):
                            act_qT(act, b + 1, 1 - par, u)
                if tail and s == YT_STEP:
                    act_yT(act, b - 1)
                if front and s == XT_STEP:
                    act_xT(act, b + 2)
                if front and s in QKV_STEPS:
                    act_qkv(act, b + 2, QKV_STEPS.index(s))
                if front and SLOT_STEP <= s < SLOT_STEP + NT:
                    act_first_part(act, b + 2, s - SLOT_STEP)
            act_quad(act, b, NQ - 1)

        def act_first_part(act, b, k):
            act.wait_ge(q_qpart.sem, q_qpart.at(b, 5))
            act.wait_ge(q_qTp.sem, q_qTp.at(b, 0))
            fill_q_slots(act_copy, k, 0).then_inc(q_qx0.sem, 1)

        def mqa_act(act):
            act_xT(act, 0)
            for r in range(2):
                act_qkv(act, 0, r)
            for k in range(NT):
                act_first_part(act, 0, k)
                for n in range(1, PARTS):
                    fill_q_slots(act_copy, k, n).then_inc(q_qx.sem, 1)
            act_xT(act, 1)
            for r in range(2):
                act_qkv(act, 1, r)
            act.wait_ge(q_zero.sem, q_zero.total(2))
            for u in range(2 * NT):
                act_qT(act, 0, 0, u)
            for k in range(NT):
                act_first_part(act, 1, k)
            act_turn(act, 0, 0, tail=False)
            act_turn(act, 1, 1)
            with nc.scalar.Fori(1, B // 2 - 1) as i:
                act_turn(act, 2 * i, 0)
                act_turn(act, 2 * i + 1, 1)
            act_turn(act, B - 2, 0, front=False)
            act_turn(act, B - 1, 1, middle=False, front=False)
            act_yT(act, B - 1)

        def sp_rows(sp, b, par):
            sp.wait_ge(q_mT.sem, q_mT.at(b, 1))
            for n in range(PARTS):
                sp.dma_start(qT[QR + n:QR + n + 1, par, :, :],
                             mT[n * HEADS:(n + 1) * HEADS, :]).then_inc(q_mrow.sem, 16)

        def mqa_sync(sp):
            with nc.sync.Fori(0, B // 2) as i:
                sp_rows(sp, 2 * i, 0)
                sp_rows(sp, 2 * i + 1, 1)

        def pe_xT(pe, b, first=False):
            pe.wait_ge(q_xln.sem, q_xln.at(b, NT))
            if first:
                pe.wait_ge(q_qkv.sem, q_qkv.at(b, 0))
            else:
                pe.wait_ge(q_qT.sem, q_qT.at(b, 0))
            for k in range(NT):
                ins = nc.tensor.transpose(bank[0][:, k * P:(k + 1) * P], xln[:, k, :], ident)
            ins.then_inc(q_xTp.sem, 1)

        def pe_qkv(pe, b, r):
            pe.wait_ge(q_xT.sem, q_xT.at(b, 1))
            if r:
                pe.wait_ge(q_qkv.sem, q_qkv.at(b, r))
            n = D + 2 * L
            for j in range(2):
                k = 2 * r + j
                ins = nc.tensor.matmul(bank[0][:, j * n:(j + 1) * n], xT[:, k * P:(k + 1) * P], wa_sb[:, :],
                                       start=True, stop=True)
            ins.then_inc(q_qkvp.sem, 1)

        def pe_kT(pe, b, first=False):
            pe.wait_ge(q_kx.sem, q_kx.at(b, 3))
            pe.wait_ge(q_qkv.sem, q_qkv.at(b + 1 if first else b, 2))
            pe.wait_ge(q_mT.sem, q_mT.at(b, 0))
            for k in range(NT):
                ins = nc.tensor.transpose(bank[0][:, :].bitcast(BF16)[0:QR, k * P:(k + 1) * P],
                                          kx3[:, k].rearrange("p n j l -> p (n j l)"), ident_bf[:, :])
            ins.then_inc(q_kTp.sem, 1)

        def pe_qT(pe, b, u):
            k, half = divmod(u, 2)
            pe.wait_ge(q_qx.sem, q_qx.at(b, (PARTS - 1) * (k + 1)))
            pe.wait_ge(q_qx0.sem, q_qx0.at(b, k + 1))
            if u == 0:
                pe.wait_ge(q_kTe.sem, q_kTe.at(b, 1))
            else:
                pe.wait_ge(q_qT.sem, q_qT.at(b, u))
            for h in range(NU):
                ins = nc.tensor.transpose(bank[0][:, :].bitcast(BF16)[0:QR, h * P:(h + 1) * P],
                                          qx3[:, k, half * NU + h].rearrange("p n j l -> p (n j l)"), ident_bf[:, :])
            ins.then_inc(q_qTp.sem, 1)

        def pe_max(pe, b, par, units, banks, first=False):
            for n in units:
                k, h, nh = max_units[n]
                pe.wait_ge(q_qT.sem, q_qT.at(b, 2 * k + 2))
                if n >= len(banks):
                    pe.wait_ge(q_mx.sem, q_mx.at(b, n + 1 - len(banks)))
                elif not first:
                    pe.wait_ge(q_x.sem, q_x.at(b - 1, 0))
                w = P * (k + 1)
                for hh in range(nh):
                    at = banks[n % len(banks)][:, hh * w:(hh + 1) * w]
                    nc.tensor.matmul(at, qT[:, par, h + hh, k * P:(k + 1) * P], kTm[:, 0:w], start=True, stop=False)
                    ins = nc.tensor.matmul(at[:, w - P:w], ident_bf[:, :], mask_qk[:, :], start=False, stop=True)
                ins.then_inc(q_smp.sem, 1)

        def pe_shift(pe, b, front):
            pe.wait_ge(q_mpart.sem, q_mpart.at(b, 5))
            if front:
                pe.wait_ge(q_qkv.sem, q_qkv.at(b + 1, 2))
            waits_end(pe)
            for k in range(NT):
                ins = nc.tensor.transpose(bank[0][:, :].bitcast(BF16)[0:PARTS * HEADS, k * P:(k + 1) * P],
                                          mp[:, k].rearrange("p n h -> p (n h)"), ident_bf[:, :])
            ins.then_inc(q_mTp.sem, 1)

        def pe_scores(pe, b, par, step, halves=(0, 1)):
            qd, j = divmod(step, NT)
            w = T - P * j
            if step == 0:
                pe.wait_ge(q_mrow.sem, q_mrow.at(b, PARTS))
            for half in halves:
                n = 2 * step + half
                pe.wait_ge(q_p.sem, q_p.at(b, n - 1 if n >= 2 else 0))
                for hh in range(2):
                    h = 4 * qd + 2 * half + hh
                    at = psE[half][:, hh * 512:hh * 512 + w]
                    ins = nc.tensor.matmul(at, kTe[:, par, j * P:(j + 1) * P], qT[:, par, h, j * P:T],
                                           start=True, stop=True)
                ins.then_inc(q_sp.sem, 1)

        def pe_values(pe, b, par, step):
            qd, j = divmod(step, NT)
            w = T - P * j
            pe.wait_ge(q_pc.sem, q_pc.at(b, 2 * step + 2))
            if j == 0:
                pe.wait_ge(q_v.sem, q_v.at(b, 1))
                pe.wait_ge(q_o.sem, q_o.at(b, qd))
            for g in range(4):
                ins = nc.tensor.matmul(psO[32 * g:32 * g + 32, j * P:T], vx[:, par, j, :],
                                       pexp[:, (2 * step + g // 2) % 4, g % 2, 0:w], start=j == 0, stop=j == NT - 1)
            ins.then_inc(q_av.sem, 1)

        def pe_back(pe, b, tiles, last):
            for k in tiles:
                pe.wait_ge(q_o.sem, q_o.at(b, NQ))
                if k >= 2:
                    pe.wait_ge(q_y.sem, q_y.at(b, k - 1))
                else:
                    pe.wait_ge(q_mx.sem, q_mx.at(b + (1 if last else 2), 0))
                    pe.wait_ge(q_x.sem, q_x.at(b, 0))
                for qd in range(NQ):
                    ins = nc.tensor.transpose(psM2[k % 2][:, qd * P:(qd + 1) * P], oT[:, qd, k * P:(k + 1) * P], ident)
                ins.then_inc(q_oTp.sem, 1)

        def pe_yT(pe, b):
            pe.wait_ge(q_y.sem, q_y.at(b, NT))
            for k in range(NT):
                ins = nc.tensor.transpose(psM2[0][:, k * P:(k + 1) * P], y2[:, k, :], ident)
            ins.then_inc(q_yTp.sem, 1)

        def pe_project(pe, b):
            pe.wait_ge(q_yT.sem, q_yT.at(b, 1))
            for k in range(NT):
                ins = nc.tensor.matmul(psM2[1][:, k * D:(k + 1) * D], y2T[:, k * P:(k + 1) * P], wp_sb[:, :],
                                       start=True, stop=True)
            ins.then_inc(q_prp.sem, 1)

        def pe_turn(pe, b, par, tail=True, middle=True, front=True):
            if middle:
                pe_kT(pe, b + 1)
                pe_qT(pe, b + 1, 0)
            if tail:
                pe_back(pe, b - 1, (0, 1), False)
            if middle:
                pe_qT(pe, b + 1, 1)
            if tail:
                pe_back(pe, b - 1, (2, 3), False)
            pe_scores(pe, b, par, 0)
            for s in range(STEPS):
                for half in range(2):
                    if s + 1 < STEPS:
                        pe_scores(pe, b, par, s + 1, (half,))
                    if middle:
                        for u in qT_unit(s, half):
                            pe_qT(pe, b + 1, u)
                    if middle:
                        pe_max(pe, b + 1, 1 - par, max_unit(s, half), psM2)
                if tail and s == YT_STEP:
                    pe_yT(pe, b - 1)
                if tail and s == PROJECT_STEP:
                    pe_project(pe, b - 1)
                if front and s == XT_STEP:
                    pe_xT(pe, b + 2)
                if front and s in QKV_STEPS:
                    pe_qkv(pe, b + 2, QKV_STEPS.index(s))
                if middle:
                    pe_max(pe, b + 1, 1 - par, max_unit(s, 2), psM2)
                if middle and s == SHIFT_T_STEP:
                    pe_shift(pe, b + 1, front)
                pe_values(pe, b, par, s)
                if middle:
                    pe_max(pe, b + 1, 1 - par, max_unit(s, 3), psM2)

        def mqa_pe(pe):
            pe_xT(pe, 0, first=True)
            for r in range(2):
                pe_qkv(pe, 0, r)
            pe_xT(pe, 1, first=True)
            for r in range(2):
                pe_qkv(pe, 1, r)
            pe.wait_ge(q_init.sem, q_init.total(2))
            pe_kT(pe, 0, first=True)
            for u in range(2 * NT):
                pe_qT(pe, 0, u)
                if u == 2 * NT - 1:
                    pe_max(pe, 0, 0, range(NM_EARLY, NM), psM4, first=True)
                elif u % 2 and u > 1:
                    pe_max(pe, 0, 0, [n for n in range(NM) if max_units[n][0] == u // 2 - 1], psM4, first=True)
            pe_shift(pe, 0, True)
            pe_turn(pe, 0, 0, tail=False)
            pe_turn(pe, 1, 1)
            with nc.tensor.Fori(1, B // 2 - 1) as i:
                pe_turn(pe, 2 * i, 0)
                pe_turn(pe, 2 * i + 1, 1)
            pe_turn(pe, B - 2, 0, front=False)
            pe_turn(pe, B - 1, 1, middle=False, front=False)
            pe_back(pe, B - 1, range(NT), True)
            pe_yT(pe, B - 1)
            pe_project(pe, B - 1)

        F = lambda name, per=1, step=1: signal("filter_" + name, per, step)
        f_xln, f_xTp, f_xT, f_yp, f_b, f_x, f_out = (F("xln", NT), F("xT_psum"), F("xT"), F("y_psum"), F("biased"),
                                                     F("x_updated"), F("stored", 1, 16))
        new_stage()
        fx = scratch("fx", [P, 2, NT, D])
        fxT = scratch("fxT", [P, 2, T])
        psFT, psFY = (bank[0], bank[2]), (bank[1], bank[7])

        def dve_filter_xln(dve, b, par):
            for k in range(NT):
                nc.vector.tensor_scalar(fx[:, par, k, :], x_sb[:, b, k, :], mv[:, b, k, 0:1],
                                        rstd[:, b, k:k + 1], ALU.subtract, ALU.mult).then_inc(f_xln.sem, 1)

        def dve_filter_residual(dve, b, par):
            dve.wait_ge(f_yp.sem, f_yp.at(b, 1))
            dve.wait_ge(f_b.sem, f_b.at(b, 1))
            nc.vector.tensor_tensor(x_sb[:, b], x_sb[:, b], psFY[par][:, :].rearrange("p (k d) -> p k d", d=D),
                                    ALU.add).then_inc(f_x.sem, 1)

        def filter_dve(dve):
            dve_filter_xln(dve, 0, 0)
            dve_filter_xln(dve, 1, 1)
            with nc.vector.Fori(0, B // 2 - 1) as i:
                for par in range(2):
                    dve.wait_ge(f_xTp.sem, f_xTp.at(2 * i + par, 1))
                    dve_filter_xln(dve, 2 * i + par + 2, par)
                    dve_filter_residual(dve, 2 * i + par, par)
            for par in range(2):
                dve_filter_residual(dve, B - 2 + par, par)

        def filter_pool(pool):
            with nc.gpsimd.Fori(0, B) as i:
                pool.wait_ge(f_xln.sem, f_xln.at(i, NT))
                nc.gpsimd.tensor_tensor(x_sb[:, i], x_sb[:, i], fb_sb[:, :].unsqueeze(1).broadcast_to([P, NT, D]),
                                        ALU.add).then_inc(f_b.sem, 1)

        def act_filter_xT(act, b, par):
            act.wait_ge(f_xTp.sem, f_xTp.at(b, 1))
            nc.scalar.activation(fxT[:, par, :], psFT[par][:, :], ACT.Copy).then_inc(f_xT.sem, 1)

        def filter_act(act):
            act_filter_xT(act, 0, 0)
            act_filter_xT(act, 1, 1)
            with nc.scalar.Fori(0, B // 2 - 1) as i:
                for par in range(2):
                    act.wait_ge(f_yp.sem, f_yp.at(2 * i + par, 1))
                    act_filter_xT(act, 2 * i + par + 2, par)

        def pe_filter_xT(pe, b, par):
            pe.wait_ge(f_xln.sem, f_xln.at(b, NT))
            for k in range(NT):
                ins = nc.tensor.transpose(psFT[par][:, k * P:(k + 1) * P], fx[:, par, k, :], ident)
            ins.then_inc(f_xTp.sem, 1)

        def pe_filter_product(pe, b, par):
            pe.wait_ge(f_xT.sem, f_xT.at(b, 1))
            for k in range(NT):
                ins = nc.tensor.matmul(psFY[par][:, k * D:(k + 1) * D], fxT[:, par, k * P:(k + 1) * P], m_sb[:, :],
                                       start=True, stop=True)
            ins.then_inc(f_yp.sem, 1)

        def filter_pe(pe):
            pe_filter_xT(pe, 0, 0)
            pe_filter_xT(pe, 1, 1)
            with nc.tensor.Fori(0, B // 2 - 1) as i:
                for par in range(2):
                    if par == 0:
                        pe.wait_ge(f_x.sem, f_x.at(2 * i, 0))
                    pe_filter_product(pe, 2 * i + par, par)
                    pe_filter_xT(pe, 2 * i + par + 2, par)
            pe.wait_ge(f_x.sem, f_x.at(B - 2, 0))
            for par in range(2):
                pe_filter_product(pe, B - 2 + par, par)

        def filter_sync(sp):
            with nc.sync.Fori(0, B) as i:
                sp.wait_ge(f_x.sem, f_x.at(i, 1))
                sp.dma_start(out[i].rearrange("(k p) d -> p k d", p=P), x_sb[:, i]).then_inc(f_out.sem, 16)
            sp.wait_ge(f_out.sem, f_out.total(16 * B))

        block = ctx.enter_context(nc.Block())

        @block.sync
        def _(sp):
            prep_sync(sp)
            sp.wait_ge(s_started, 1)
            route_sync(sp)
            moe_sync(sp)
            mqa_sync(sp)
            filter_sync(sp)

        @block.scalar
        def _(act):
            prep_act(act)
            act.wait_ge(s_started, 1)
            ln1.act_std(act)
            lin_act(act)
            ln2.act_std(act)
            route_act(act)
            moe_act(act)
            ln3.act_std(act)
            mqa_act(act)
            ln4.act_std(act)
            filter_act(act)

        @block.tensor
        def _(pe):
            prep_pe(pe)
            lin_pe(pe)
            route_pe(pe)
            moe_pe(pe)
            mqa_pe(pe)
            filter_pe(pe)

        @block.vector
        def _(dve):
            dve.wait_ge(s_started, 1)
            dve.wait_ge(s_x.sem, s_x.total(16 * B))
            with nc.vector.Fori(0, B) as i:
                ln1.dve_sequence(dve, i)
            ln1.dve_rstd(dve)
            prep_dve(dve)
            lin_dve(dve)
            ln2.dve_rstd(dve)
            route_dve(dve)
            moe_dve(dve)
            ln3.dve_rstd(dve)
            mqa_dve(dve)
            ln4.dve_rstd(dve)
            filter_dve(dve)

        @block.gpsimd
        def _(pool):
            start_signals(pool)
            lin_pool(pool)
            route_pool(pool)
            moe_pool(pool)
            mqa_pool(pool)
            filter_pool(pool)


def constants():
    import numpy as np
    n = np.arange(P)
    angle = 2.0 * np.pi * ((n[:, None] * n[None, :]) % P) / P
    head = n // 8
    parts = {
        "ident": np.eye(P),
        "tri": n[:, None] <= n[None, :],
        "ones": np.ones((P, P)),
        "dft_c": np.cos(angle),
        "dft_s": np.sin(angle),
        "dft_ns": -np.sin(angle),
        "blockdiag": head[:, None] == head[None, :],
        "causal_qk": np.where(n[:, None] < n[None, :], NEG, 0.0),
        "slots": np.broadcast_to(np.arange(P + 1)[None, :], (P, P + 1)),
        "slot_row": n[:, None],
        "seqmask": ((n[:, None] % 64) // 8) == np.arange(8)[None, :],
        "shift_rows": ((n >= 72) & (n < 75))[:, None],
    }
    layout, at = {}, 0
    for name, a in parts.items():
        layout[name] = (at, a.shape[1])
        at += a.shape[1]
    layout["width"] = at
    return layout, np.concatenate([np.asarray(a, np.float32) for a in parts.values()], axis=1)


_INS = ["L0_attn_x", "L0_attn_w", "L0_attn_w_out", "L0_ffn_router_w", "L0_ffn_w1", "L0_ffn_b1", "L0_ffn_w2",
        "L0_ffn_b2", "L1_attn_w_attn", "L1_attn_w_proj", "L1_ffn_w_freq_real", "L1_ffn_w_freq_imag",
        "L1_ffn_bias"]


def kernel(**inputs):
    import numpy as np
    import concourse.bacc as bacc
    from concourse.bass_utils import run_bass_kernel_spmd

    nc = bacc.Bacc("TRN2", target_bir_lowering=False, num_devices=1)
    layout, table = constants()
    arrays, args = {}, []
    for name in _INS:
        arrays[f"in_{name}"] = np.ascontiguousarray(inputs[name])
    arrays["constants"] = table
    for name, a in arrays.items():
        args.append(nc.dram_tensor(name, a.shape, mybir.dt.from_np(a.dtype), kind="ExternalInput").ap())
    x = arrays["in_L0_attn_x"]
    out = nc.dram_tensor("out_x", x.shape, F32, kind="ExternalOutput").ap()
    build(nc, *args, out, layout)
    return run_bass_kernel_spmd(nc, [arrays], core_ids=[0]).results[0]["out_x"]
```
